# Optimizing a Trainium2 kernel written in Bass

```python
import numpy as np
import jax
import jax.numpy as jnp

def _softmax(x, axis=-1):
    return jax.nn.softmax(x, axis=axis)

def _gelu(x):
    return jax.nn.gelu(x, approximate=True)

def _silu(x):
    return jax.nn.silu(x)

def _sigmoid(x):
    return jax.nn.sigmoid(x)

def _layernorm(x, axis=-1, eps=1e-05):
    m = jnp.mean(x, axis=axis, keepdims=True)
    v = jnp.var(x, axis=axis, keepdims=True)
    return (x - m) / jnp.sqrt(v + eps)

def _scatter_add(tgt, idx, src, axis=0):
    return tgt.at[idx].add(src)

def _segment_sum(src, seg, n):
    return jax.ops.segment_sum(src, seg, n)
kernel_name = 'mk_decoder_preln_d2_seqx_r8_a3b781'

def setup_inputs(seed: int=0):
    np.random.seed(seed)
    _w = jnp.asarray

    def _rec_inputs():
        import jax
        import jax.numpy as jnp
        _rk = jax.random.key(seed)
        x = 7.22e-05 + 1 * jax.random.normal(jax.random.fold_in(_rk, 1), (8, 128, 256), jnp.float32)
        _lenS = 128 - jax.random.randint(jax.random.fold_in(_rk, 7), (8,), 0, max(1, 128 // 4) + 1, jnp.int32)
        _lenS2 = 128 - jax.random.randint(jax.random.fold_in(_rk, 8), (8,), 0, max(1, 128 // 4) + 1, jnp.int32)
        _ctx_512P = jax.random.normal(jax.random.fold_in(_rk, 11), (8, 16, 64), jnp.float32)
        _ctx_512c = jax.random.dirichlet(jax.random.fold_in(_rk, 511), 0.3 * jnp.ones((16,), jnp.float32), (8, 128))
        _ctx_512t = jnp.einsum('bsk,bkd->bsd', _ctx_512c, _ctx_512P)
        _ctx_512t = _ctx_512t * jax.lax.rsqrt(jnp.mean(jnp.square(_ctx_512t)) + 1e-12) * 0.953939
        ctx_512 = -0.000514642 + 1.00011 * (_ctx_512t + 0.3 * jax.random.normal(jax.random.fold_in(_rk, 611), (8, 128, 64), jnp.float32))
        return (x, ctx_512)
    x, ctx_512 = _rec_inputs()

    def _L0_attn_setup():
        import jax, jax.numpy as jnp
        import numpy as np
        N_HEAD = 32
        HEAD_ID = 0
        MASKED_BIAS = -10000.0
        key = jax.random.key(seed)
        k1, k2, k3 = jax.random.split(key, 3)
        B, S, E = (1, 256, 256)
        hidden_states = jax.random.normal(k1, (B, S, E), dtype=jnp.float32)
        W_attn = jax.random.normal(k2, (E, 3 * E), dtype=jnp.float32) * (1.0 / np.sqrt(E))
        b_attn = jnp.zeros((3 * E,), dtype=jnp.float32)
        W_proj = jax.random.normal(k3, (E, E), dtype=jnp.float32) * (1.0 / np.sqrt(E))
        b_proj = jnp.zeros((E,), dtype=jnp.float32)
        return {'hidden_states': hidden_states, 'W_attn': W_attn, 'b_attn': b_attn, 'W_proj': W_proj, 'b_proj': b_proj}
    _L0_attn_all = _L0_attn_setup()
    _L0_attn_in = {k: v for k, v in _L0_attn_all.items() if k in ('W_attn', 'b_attn', 'W_proj', 'b_proj')}
    del _L0_attn_all

    def _L0_xattn_setup():
        import jax, jax.numpy as jnp
        import numpy as np
        B, S, E = (2, 256, 256)
        QH, KVH = (32, 8)
        D = E // QH
        G = QH // KVH
        DROPOUT = 1.0
        key = jax.random.key(seed)
        k1, k2, k3 = jax.random.split(key, 3)
        q = jax.random.normal(k1, (B, S, E), dtype=jnp.float32)
        k = jax.random.normal(k2, (B, S, E // G), dtype=jnp.float32)
        v = jax.random.normal(k3, (B, S, E // G), dtype=jnp.float32)
        return {'q': q, 'k': k, 'v': v}
    _L0_xattn_all = _L0_xattn_setup()
    _L0_xattn_in = {k: v for k, v in _L0_xattn_all.items() if k in ()}
    del _L0_xattn_all

    def _L0_ffn_setup():
        import jax, jax.numpy as jnp
        import numpy as np
        B, S, D = (2, 256, 256)
        E, I, TOPK = (64, 96, 8)
        M = B * S
        CAP = 2 * (M * TOPK) // E

        def _moe(x, router_weight, gate_proj, up_proj, down_proj):
            b, s, d = x.shape
            xf = x.reshape(-1, d)
            m = xf.shape[0]
            logits = xf @ router_weight
            probs = jax.nn.softmax(logits.astype(jnp.float32), axis=-1)
            topw, topi = jax.lax.top_k(probs, TOPK)
            topw = topw / topw.sum(axis=-1, keepdims=True)
            flat_e = topi.reshape(-1)
            flat_w = topw.reshape(-1).astype(x.dtype)
            order = jnp.argsort(flat_e)
            se = flat_e[order]
            tok = order // TOPK
            counts = jax.ops.segment_sum(jnp.ones_like(flat_e), flat_e, num_segments=E)
            starts = jnp.cumsum(counts) - counts
            pos = jnp.arange(m * TOPK) - starts[se]
            valid = pos < CAP
            posc = jnp.minimum(pos, CAP - 1)
            xe = jnp.zeros((E, CAP, d), x.dtype).at[se, pos].set(xf[tok], mode='drop')
            h = jax.nn.silu(jnp.einsum('ecd,edi->eci', xe, gate_proj)) * jnp.einsum('ecd,edi->eci', xe, up_proj)
            ye = jnp.einsum('eci,eid->ecd', h, down_proj)
            contrib = jnp.where(valid[:, None], ye[se, posc], 0.0) * flat_w[order][:, None]
            out = jnp.zeros((m, d), x.dtype).at[tok].add(contrib)
            return out.reshape(b, s, d)
        key = jax.random.key(seed)
        k0, k1, k2, k3, k4 = jax.random.split(key, 5)
        return {'x': jax.random.normal(k0, (B, S, D), jnp.float32), 'router_weight': jax.random.normal(k1, (D, E), jnp.float32) * 0.02, 'gate_proj': jax.random.normal(k2, (E, D, I), jnp.float32) * 0.02, 'up_proj': jax.random.normal(k3, (E, D, I), jnp.float32) * 0.02, 'down_proj': jax.random.normal(k4, (E, I, D), jnp.float32) * 0.02}
    _L0_ffn_all = _L0_ffn_setup()
    _L0_ffn_in = {k: v for k, v in _L0_ffn_all.items() if k in ('router_weight', 'gate_proj', 'up_proj', 'down_proj')}
    del _L0_ffn_all

    def _L1_attn_setup():
        import jax, jax.numpy as jnp
        import numpy as np
        NUM_HEADS = 16
        NUM_KV_HEADS = 4
        ROPE_BASE = 10000.0

        def _rotate_half(x):
            x1 = x[..., ::2]
            x2 = x[..., 1::2]
            return jnp.stack((-x2, x1), axis=-1).reshape(x.shape)

        def apply_rope(x, positions, base):
            head_dim = x.shape[-1]
            inv_freq = 1.0 / base ** (jnp.arange(0, head_dim, 2, dtype=jnp.float32) / head_dim)
            freqs = positions.astype(jnp.float32)[:, None] * inv_freq[None, :]
            cos = jnp.repeat(jnp.cos(freqs), 2, axis=-1)[None, :, None, :]
            sin = jnp.repeat(jnp.sin(freqs), 2, axis=-1)[None, :, None, :]
            return x * cos + _rotate_half(x) * sin
        key = jax.random.key(seed)
        ks = jax.random.split(key, 9)
        B, S, H = (2, 256, 256)
        kvdim = NUM_KV_HEADS * (H // NUM_HEADS)
        s = 0.02
        return {'x': jax.random.normal(ks[0], (B, S, H), jnp.float32), 'Wq': jax.random.normal(ks[1], (H, H), jnp.float32) * s, 'bq': jnp.zeros((H,), jnp.float32), 'Wk': jax.random.normal(ks[2], (kvdim, H), jnp.float32) * s, 'bk': jnp.zeros((kvdim,), jnp.float32), 'Wv': jax.random.normal(ks[3], (kvdim, H), jnp.float32) * s, 'bv': jnp.zeros((kvdim,), jnp.float32), 'Wo': jax.random.normal(ks[4], (H, H), jnp.float32) * s, 'bo': jnp.zeros((H,), jnp.float32)}
    _L1_attn_all = _L1_attn_setup()
    _L1_attn_in = {k: v for k, v in _L1_attn_all.items() if k in ('Wq', 'bq', 'Wk', 'bk', 'Wv', 'bv', 'Wo', 'bo')}
    del _L1_attn_all

    def _L1_xattn_setup():
        import jax, jax.numpy as jnp
        import numpy as np
        B, S, L = (2, 128, 128)
        DIM_Q, H, K, D_C, D_CQ, R = (256, 16, 128, 64, 192, 64)

        def _rope_tables(length, dim):
            inv = 1.0 / 10000.0 ** (jnp.arange(0, dim, 2, dtype=jnp.float32) / dim)
            f = jnp.arange(length, dtype=jnp.float32)[:, None] * inv[None, :]
            sin = jnp.repeat(jnp.sin(f), 2, axis=-1)
            cos = jnp.repeat(jnp.cos(f), 2, axis=-1)
            return (sin, cos)

        def _rotate_half(x):
            half = x.shape[-1] // 2
            return jnp.concatenate([-x[..., half:], x[..., :half]], axis=-1)

        def _apply_rope(x, sin, cos):
            return x * cos + _rotate_half(x) * sin
        key = jax.random.key(seed)
        ks = jax.random.split(key, 8)
        return {'hidden_q': jax.random.normal(ks[0], (B, S, DIM_Q), jnp.float32), 'kv_c': jax.random.normal(ks[1], (B, L, D_C), jnp.float32), 'Wq': jax.random.normal(ks[2], (H * K, DIM_Q), jnp.float32) / np.sqrt(DIM_Q).astype(np.float32), 'w_kc_q': jax.random.normal(ks[3], (H, K, D_CQ), jnp.float32) / np.sqrt(K).astype(np.float32), 'w_kc_kv': jax.random.normal(ks[4], (H, K, D_C), jnp.float32) / np.sqrt(K).astype(np.float32), 'W_qr': jax.random.normal(ks[5], (H, D_CQ, R), jnp.float32) / np.float32(np.sqrt(D_CQ) * np.sqrt(R)), 'W_kr': jax.random.normal(ks[6], (H, D_C, R), jnp.float32) / np.sqrt(D_C).astype(np.float32), 'Wo': jax.random.normal(ks[7], (DIM_Q, H * K), jnp.float32) / np.sqrt(H * K).astype(np.float32)}
    _L1_xattn_all = _L1_xattn_setup()
    _L1_xattn_in = {k: v for k, v in _L1_xattn_all.items() if k in ('Wq', 'w_kc_q', 'w_kc_kv', 'W_qr', 'W_kr', 'Wo')}
    del _L1_xattn_all

    def _L1_ffn_setup():
        import jax, jax.numpy as jnp
        import numpy as np
        TOP_K = 4
        key = jax.random.key(seed)
        ks = jax.random.split(key, 8)
        B, S, H, E, F = (1, 256, 256, 16, 176)
        Fs = 2 * F
        s = 0.02
        return {'hidden_states': jax.random.normal(ks[0], (B, S, H), jnp.float32), 'gate_weight': jax.random.normal(ks[1], (E, H), jnp.float32) * s, 'w_gate': jax.random.normal(ks[2], (E, H, F), jnp.float32) * s, 'w_up': jax.random.normal(ks[3], (E, H, F), jnp.float32) * s, 'w_down': jax.random.normal(ks[4], (E, F, H), jnp.float32) * s, 'ws_gate': jax.random.normal(ks[5], (H, Fs), jnp.float32) * s, 'ws_up': jax.random.normal(ks[6], (H, Fs), jnp.float32) * s, 'ws_down': jax.random.normal(ks[7], (Fs, H), jnp.float32) * s}
    _L1_ffn_all = _L1_ffn_setup()
    _L1_ffn_in = {k: v for k, v in _L1_ffn_all.items() if k in ('gate_weight', 'w_gate', 'w_up', 'w_down', 'ws_gate', 'ws_up', 'ws_down')}
    del _L1_ffn_all
    return {'x': x, 'ctx_512': ctx_512, 'L0_attn_W_attn': _L0_attn_in['W_attn'], 'L0_attn_b_attn': _L0_attn_in['b_attn'], 'L0_attn_W_proj': _L0_attn_in['W_proj'], 'L0_attn_b_proj': _L0_attn_in['b_proj'], 'L0_ffn_router_weight': _L0_ffn_in['router_weight'], 'L0_ffn_gate_proj': _L0_ffn_in['gate_proj'], 'L0_ffn_up_proj': _L0_ffn_in['up_proj'], 'L0_ffn_down_proj': _L0_ffn_in['down_proj'], 'L1_attn_Wq': _L1_attn_in['Wq'], 'L1_attn_bq': _L1_attn_in['bq'], 'L1_attn_Wk': _L1_attn_in['Wk'], 'L1_attn_bk': _L1_attn_in['bk'], 'L1_attn_Wv': _L1_attn_in['Wv'], 'L1_attn_bv': _L1_attn_in['bv'], 'L1_attn_Wo': _L1_attn_in['Wo'], 'L1_attn_bo': _L1_attn_in['bo'], 'L1_xattn_Wq': _L1_xattn_in['Wq'], 'L1_xattn_w_kc_q': _L1_xattn_in['w_kc_q'], 'L1_xattn_w_kc_kv': _L1_xattn_in['w_kc_kv'], 'L1_xattn_W_qr': _L1_xattn_in['W_qr'], 'L1_xattn_W_kr': _L1_xattn_in['W_kr'], 'L1_xattn_Wo': _L1_xattn_in['Wo'], 'L1_ffn_gate_weight': _L1_ffn_in['gate_weight'], 'L1_ffn_w_gate': _L1_ffn_in['w_gate'], 'L1_ffn_w_up': _L1_ffn_in['w_up'], 'L1_ffn_w_down': _L1_ffn_in['w_down'], 'L1_ffn_ws_gate': _L1_ffn_in['ws_gate'], 'L1_ffn_ws_up': _L1_ffn_in['ws_up'], 'L1_ffn_ws_down': _L1_ffn_in['ws_down']}

def reference(x, ctx_512, L0_attn_W_attn, L0_attn_b_attn, L0_attn_W_proj, L0_attn_b_proj, L0_ffn_router_weight, L0_ffn_gate_proj, L0_ffn_up_proj, L0_ffn_down_proj, L1_attn_Wq, L1_attn_bq, L1_attn_Wk, L1_attn_bk, L1_attn_Wv, L1_attn_bv, L1_attn_Wo, L1_attn_bo, L1_xattn_Wq, L1_xattn_w_kc_q, L1_xattn_w_kc_kv, L1_xattn_W_qr, L1_xattn_W_kr, L1_xattn_Wo, L1_ffn_gate_weight, L1_ffn_w_gate, L1_ffn_w_up, L1_ffn_w_down, L1_ffn_ws_gate, L1_ffn_ws_up, L1_ffn_ws_down):
    import jax
    import jax.numpy as jnp

    def _L0_attn_ref(hidden_states, W_attn, b_attn, W_proj, b_proj):
        import jax, jax.numpy as jnp
        import numpy as np
        N_HEAD = 32
        HEAD_ID = 0
        MASKED_BIAS = -10000.0
        B, S, E = hidden_states.shape
        H = N_HEAD
        D = E // H
        m = 2.0 ** (-(8.0 / H) * (HEAD_ID + 1))
        qkv = hidden_states @ W_attn + b_attn
        q, k, v = jnp.split(qkv, 3, axis=-1)
        q = q.reshape(B, S, H, D).transpose(0, 2, 1, 3)
        k = k.reshape(B, S, H, D).transpose(0, 2, 1, 3)
        v = v.reshape(B, S, H, D).transpose(0, 2, 1, 3)
        scores = jnp.einsum('bhqd,bhkd->bhqk', q, k) / jnp.sqrt(jnp.float32(D))
        rows = jnp.arange(S)[:, None]
        cols = jnp.arange(S)[None, :]
        causal = cols <= rows
        scores = jnp.where(causal, scores, jnp.float32(MASKED_BIAS))
        alibi = jnp.where(causal, (cols - rows).astype(scores.dtype), 0.0)
        scores = scores + alibi * m
        probs = jax.nn.softmax(scores, axis=-1)
        attn = jnp.einsum('bhqk,bhkd->bhqd', probs, v)
        attn = attn.transpose(0, 2, 1, 3).reshape(B, S, E)
        out = attn @ W_proj + b_proj
        return out

    def _L0_xattn_ref(q, k, v):
        import jax, jax.numpy as jnp
        import numpy as np
        B, S, E = (2, 256, 256)
        QH, KVH = (32, 8)
        D = E // QH
        G = QH // KVH
        DROPOUT = 1.0
        b, s, _ = q.shape
        qh = q.reshape(b, s, KVH, G, D).transpose(0, 2, 3, 1, 4)
        kh = k.reshape(b, s, KVH, D).transpose(0, 2, 1, 3)
        vh = v.reshape(b, s, KVH, D).transpose(0, 2, 1, 3)
        scale = 1.0 / jnp.sqrt(jnp.float32(D))
        scores = jnp.einsum('bkgsd,bktd->bkgst', qh, kh) * scale
        attn = jax.nn.softmax(scores, axis=-1) / DROPOUT
        out = jnp.einsum('bkgst,bktd->bkgsd', attn, vh)
        return out.transpose(0, 3, 1, 2, 4).reshape(b, s, E)

    def _L0_ffn_ref(x, router_weight, gate_proj, up_proj, down_proj):
        import jax, jax.numpy as jnp
        import numpy as np
        B, S, D = (2, 256, 256)
        E, I, TOPK = (64, 96, 8)
        M = B * S
        CAP = 2 * (M * TOPK) // E

        def _moe(x, router_weight, gate_proj, up_proj, down_proj):
            b, s, d = x.shape
            xf = x.reshape(-1, d)
            m = xf.shape[0]
            logits = xf @ router_weight
            probs = jax.nn.softmax(logits.astype(jnp.float32), axis=-1)
            topw, topi = jax.lax.top_k(probs, TOPK)
            topw = topw / topw.sum(axis=-1, keepdims=True)
            flat_e = topi.reshape(-1)
            flat_w = topw.reshape(-1).astype(x.dtype)
            order = jnp.argsort(flat_e)
            se = flat_e[order]
            tok = order // TOPK
            counts = jax.ops.segment_sum(jnp.ones_like(flat_e), flat_e, num_segments=E)
            starts = jnp.cumsum(counts) - counts
            pos = jnp.arange(m * TOPK) - starts[se]
            valid = pos < CAP
            posc = jnp.minimum(pos, CAP - 1)
            xe = jnp.zeros((E, CAP, d), x.dtype).at[se, pos].set(xf[tok], mode='drop')
            h = jax.nn.silu(jnp.einsum('ecd,edi->eci', xe, gate_proj)) * jnp.einsum('ecd,edi->eci', xe, up_proj)
            ye = jnp.einsum('eci,eid->ecd', h, down_proj)
            contrib = jnp.where(valid[:, None], ye[se, posc], 0.0) * flat_w[order][:, None]
            out = jnp.zeros((m, d), x.dtype).at[tok].add(contrib)
            return out.reshape(b, s, d)
        return _moe(x, router_weight, gate_proj, up_proj, down_proj)

    def _L1_attn_ref(x, Wq, bq, Wk, bk, Wv, bv, Wo, bo):
        import jax, jax.numpy as jnp
        import numpy as np
        NUM_HEADS = 16
        NUM_KV_HEADS = 4
        ROPE_BASE = 10000.0

        def _rotate_half(x):
            x1 = x[..., ::2]
            x2 = x[..., 1::2]
            return jnp.stack((-x2, x1), axis=-1).reshape(x.shape)

        def apply_rope(x, positions, base):
            head_dim = x.shape[-1]
            inv_freq = 1.0 / base ** (jnp.arange(0, head_dim, 2, dtype=jnp.float32) / head_dim)
            freqs = positions.astype(jnp.float32)[:, None] * inv_freq[None, :]
            cos = jnp.repeat(jnp.cos(freqs), 2, axis=-1)[None, :, None, :]
            sin = jnp.repeat(jnp.sin(freqs), 2, axis=-1)[None, :, None, :]
            return x * cos + _rotate_half(x) * sin
        B, S, hidden = x.shape
        head_dim = hidden // NUM_HEADS
        scale = head_dim ** (-0.5)
        rep = NUM_HEADS // NUM_KV_HEADS
        positions = jnp.arange(S)
        q = (x @ Wq.T + bq).reshape(B, S, NUM_HEADS, head_dim)
        k = (x @ Wk.T + bk).reshape(B, S, NUM_KV_HEADS, head_dim)
        v = (x @ Wv.T + bv).reshape(B, S, NUM_KV_HEADS, head_dim)
        q = apply_rope(q, positions, ROPE_BASE)
        k = apply_rope(k, positions, ROPE_BASE)
        k = jnp.repeat(k, rep, axis=2)
        v = jnp.repeat(v, rep, axis=2)
        scores = jnp.einsum('bthd,bshd->bhts', q, k) * scale
        causal = jnp.tril(jnp.ones((S, S), dtype=bool))
        scores = jnp.where(causal[None, None, :, :], scores, -jnp.inf)
        probs = jax.nn.softmax(scores, axis=-1)
        attended = jnp.einsum('bhts,bshd->bthd', probs, v).reshape(B, S, hidden)
        return attended @ Wo.T + bo

    def _L1_xattn_ref(hidden_q, kv_c, Wq, w_kc_q, w_kc_kv, W_qr, W_kr, Wo):
        import jax, jax.numpy as jnp
        import numpy as np
        B, S, L = (2, 128, 128)
        DIM_Q, H, K, D_C, D_CQ, R = (256, 16, 128, 64, 192, 64)

        def _rope_tables(length, dim):
            inv = 1.0 / 10000.0 ** (jnp.arange(0, dim, 2, dtype=jnp.float32) / dim)
            f = jnp.arange(length, dtype=jnp.float32)[:, None] * inv[None, :]
            sin = jnp.repeat(jnp.sin(f), 2, axis=-1)
            cos = jnp.repeat(jnp.cos(f), 2, axis=-1)
            return (sin, cos)

        def _rotate_half(x):
            half = x.shape[-1] // 2
            return jnp.concatenate([-x[..., half:], x[..., :half]], axis=-1)

        def _apply_rope(x, sin, cos):
            return x * cos + _rotate_half(x) * sin
        Bv, Sv, _ = hidden_q.shape
        _, Lv, _ = kv_c.shape
        q_hk = (hidden_q @ Wq.T).reshape(Bv, Sv, H, K)
        q_big = jnp.einsum('bshk,hkq->bshq', q_hk, w_kc_q)
        sin_q, cos_q = _rope_tables(Sv, D_CQ)
        q_big = _apply_rope(q_big, sin_q[None, :, None, :], cos_q[None, :, None, :])
        sin_k, cos_k = _rope_tables(Lv, D_C)
        kv_r = _apply_rope(kv_c, sin_k[None], cos_k[None])
        q_r = jnp.einsum('bshq,hqr->bhsr', q_big, W_qr)
        k_r = jnp.einsum('bld,hdr->bhlr', kv_r, W_kr)
        scores = jnp.einsum('bhsr,bhlr->bhsl', q_r, k_r)
        attn = jax.nn.softmax(scores, axis=-1)
        ctx_c = jnp.einsum('bhsl,bld->bhsd', attn, kv_r)
        ctx_lat = jnp.einsum('bhsd,hkd->bhsk', ctx_c, w_kc_kv)
        ctx = ctx_lat.transpose(0, 2, 1, 3).reshape(Bv, Sv, H * K)
        return ctx @ Wo.T

    def _L1_ffn_ref(hidden_states, gate_weight, w_gate, w_up, w_down, ws_gate, ws_up, ws_down):
        import jax, jax.numpy as jnp
        import numpy as np
        TOP_K = 4
        B, S, H = hidden_states.shape
        E = gate_weight.shape[0]
        x = hidden_states.reshape(-1, H)
        T = x.shape[0]
        logits = jnp.einsum('th,eh->te', x.astype(jnp.float32), gate_weight.astype(jnp.float32))
        probs = jax.nn.softmax(logits, axis=1)
        top_vals, top_idx = jax.lax.top_k(probs, TOP_K)
        dense_w = jnp.zeros((T, E), probs.dtype).at[jnp.arange(T)[:, None], top_idx].add(top_vals)
        g = jnp.einsum('th,ehf->tef', x, w_gate)
        u = jnp.einsum('th,ehf->tef', x, w_up)
        a = jax.nn.silu(g) * u
        routed = jnp.einsum('te,tef,efh->th', dense_w.astype(x.dtype), a, w_down)
        shared = jnp.einsum('tf,fh->th', jax.nn.silu(x @ ws_gate) * (x @ ws_up), ws_down)
        out = (routed + shared).reshape(B, S, H)
        return out
    x = x + _L0_attn_ref(_layernorm(x, axis=-1), L0_attn_W_attn, L0_attn_b_attn, L0_attn_W_proj, L0_attn_b_proj)
    x = x + _L0_xattn_ref(_layernorm(x, axis=-1), ctx_512, ctx_512)
    x = x + _L0_ffn_ref(_layernorm(x, axis=-1), L0_ffn_router_weight, L0_ffn_gate_proj, L0_ffn_up_proj, L0_ffn_down_proj)
    x = x + _L1_attn_ref(_layernorm(x, axis=-1), L1_attn_Wq, L1_attn_bq, L1_attn_Wk, L1_attn_bk, L1_attn_Wv, L1_attn_bv, L1_attn_Wo, L1_attn_bo)
    x = x + _L1_xattn_ref(_layernorm(x, axis=-1), ctx_512, L1_xattn_Wq, L1_xattn_w_kc_q, L1_xattn_w_kc_kv, L1_xattn_W_qr, L1_xattn_W_kr, L1_xattn_Wo)
    x = x + _L1_ffn_ref(_layernorm(x, axis=-1), L1_ffn_gate_weight, L1_ffn_w_gate, L1_ffn_w_up, L1_ffn_w_down, L1_ffn_ws_gate, L1_ffn_ws_up, L1_ffn_ws_down)
    return x

_drawn_inputs = setup_inputs


def setup_inputs(seed=0):
    import zlib

    import numpy as np

    out = dict(_drawn_inputs(seed))
    spreads = {'L0_attn_b_attn': (0.0, 0.1),
     'L0_attn_b_proj': (0.0, 0.1),
     'L1_attn_bq': (0.0, 0.8),
     'L1_attn_bk': (0.0, 2.0),
     'L1_attn_bv': (0.0, 0.399),
     'L1_attn_bo': (0.0, 0.1)}
    factors = {'L0_ffn_router_weight': 8.0,
     'L0_ffn_gate_proj': 8.0,
     'L0_ffn_up_proj': 8.0,
     'L0_ffn_down_proj': 8.0,
     'L1_attn_Wq': 8.0,
     'L1_attn_Wk': 8.0,
     'L1_ffn_gate_weight': 8.0,
     'L1_ffn_w_gate': 8.0,
     'L1_ffn_w_up': 8.0,
     'L1_ffn_w_down': 8.0,
     'L1_ffn_ws_gate': 4.651,
     'L1_ffn_ws_up': 4.62,
     'L1_ffn_ws_down': 4.61}
    for name, (base, spread) in spreads.items():
        noise = np.random.default_rng([zlib.crc32(name.encode()), seed]).standard_normal(out[name].shape)
        drawn = base * np.exp(spread * noise) if base else spread * noise
        out[name] = jnp.asarray(drawn.astype(out[name].dtype))
    for name, factor in factors.items():
        out[name] = (out[name] * factor).astype(out[name].dtype)
    return out
```

```python
from contextlib import ExitStack

import concourse.bass as bass
from concourse import mybir

F32 = mybir.dt.float32
BF16 = mybir.dt.bfloat16
I32 = mybir.dt.int32
U32 = mybir.dt.uint32
ALU = mybir.AluOpType
ACT = mybir.ActivationFunctionType
AX = mybir.AxisListType

B, S, D = 8, 128, 256
C = 64
KC = D // 128
EPS = 1e-5
E0, I0, TOP0, CAP = 64, 96, 8, 128
NSLOT = E0 * CAP
NTOK = B * S
HX, KX, QX, RX = 16, 128, 192, 64
HQ = QX // 2
E1, I1, TOP1 = 16, 176, 4
NF, FH = E1 + 2, I1 // 2
RING = 4


class Chain:

    def __init__(self, eng, sem):
        self.eng, self.sem, self.n = eng, sem, 0

    def turn(self):
        self.eng.sem_clear(self.sem)
        self.n = 0

    def __call__(self, ins):
        self.n += 1
        ins.then_inc(self.sem, 1)
        self.eng.wait_ge(self.sem, self.n)


class Attention:

    def __init__(self, name, halves, dim, shared, causal, scale):
        self.name, self.halves, self.dim, self.shared = name, halves, dim, shared
        self.causal, self.scale = causal, scale
        self.heads = 16 * halves
        self.groups = 4 * halves
        self.kgroups = halves if shared else 4 * halves
        self.kbanks = -(-self.kgroups // 4)
        self.jobs = [(half, row) for half in range(halves) for row in range(4)]
        self.rows = dim + 2

    def head(self, half, row, g):
        return (4 * half + row) * 4 + g if self.shared else 4 * (4 * half + g) + row


L0 = Attention("a0", 2, 8, False, True, 8.0 ** -0.5)
X0 = Attention("x0", 2, 8, True, False, 8.0 ** -0.5)
L1 = Attention("a1", 1, 16, True, True, 16.0 ** -0.5)
XJ = HX // 4


class Sems(dict):

    def __init__(self, nc, ctx, stage, names):
        self.make = lambda n: ctx.enter_context(nc.semaphore(f"{stage}_{n}"))
        self.names = names.split()

    def __missing__(self, n):
        assert n in self.names, n
        self[n] = self.make(n)
        return self[n]


sems = Sems


LN_SEMS = "stats rstd xn"
ATT_SEMS = (LN_SEMS + " xnt_ps xnt_sb qkv_ps qkv_sb kq_ps kq_sb s_ps s_max q2_ps q2_sb st_ps st_exp "
            "pv_ps on_sb ot_ps ot_sb pr_ps x_new")
ROUTE_SEMS = LN_SEMS + " xnt_ps xnt_sb lg_ps top ex msk pos_ps idx xn_st scat"
MOE_SEMS = ("credit xg0 xg1 xg2 xg3 wl0 wl1 wl2 wl3 xt_ps xt_sb h_ps sg a_sb y_ps y_sb yst0 yst1 yst2 yst3 slots")
XATT_SEMS = (LN_SEMS + " xnt_ps xnt_sb kv_sb kt_ps kt_sb qb_ps rope qk_ps qk_sb s_ps s_max nm_ps nm_sb st_ps st_exp "
             "pv_ps cn_sb ct_ps ct_sb pr_ps x_new fold_ld fold_ps fold_sb fold_free")
FFN_SEMS = "credit wl0 wl1 g_ps sg a_sb y_ps y_sb x_new"


def program(nc, t, out, stages):
    with ExitStack() as ctx:
        def sb(name, shape, dt=F32):
            return ctx.enter_context(nc.sbuf_tensor(name, shape, dt))

        bank = [ctx.enter_context(nc.psum_tensor(f"bank{n}", [128, 512], F32)) for n in range(8)]
        SC, ST, PV, M0, M1 = bank[0:2], bank[2:5], bank[5], bank[6], bank[7]

        x = sb("x", [128, B, D])
        ctxt = sb("ctxt", [128, B, C])
        ident = sb("ident", [128, 128])
        identb = sb("identb", [128, 128], BF16)
        maskq = sb("maskq", [128, 128], BF16)
        maskk = sb("maskk", [128, 128], BF16)
        alibi = sb("alibi", [128, 1])
        never = sb("never", [128, 128])
        neverT = sb("neverT", [128, 128])
        neghalf = sb("neghalf", [128, 1])
        eps = sb("eps", [128, 1])
        w_qkv0 = sb("w_qkv0", [128, KC, 3 * D])
        b_qkv0 = sb("b_qkv0", [128, 3 * D])
        w_pr0 = sb("w_pr0", [128, KC, D])
        b_pr0 = sb("b_pr0", [128, D])

        stats = sb("stats", [128, 6])
        mv = sb("mv", [128, 2])
        var = sb("var", [128, 1])
        rstd = sb("rstd", [128, 1])
        xn = sb("xn", [128, D])
        xnT = sb("xnT", [128, KC, 128])
        qpad = sb("qpad", [128, 8, 4, 32])
        kpad = sb("kpad", [128, 8, 4, 32])
        kpadx = sb("kpadx", [128, 2, 4, 32])
        vx = sb("vx", [128, 32, 9])
        vc = sb("vc", [128, 8, 9])
        qT = sb("qT", [128, 8, 128])
        kT = sb("kT", [128, 8, 128])
        q2T = sb("q2T", [128, 8, 128])
        PT = sb("PT", [128, 2, 4, 128])
        rden = sb("rden", [128, 32])
        on = sb("on", [128, D])
        onT = sb("onT", [128, KC, 128])
        tmp = sb("tmp", [128, D])

        w_rt0 = sb("w_rt0", [128, KC, E0])
        tri = sb("tri", [128, 128])
        ones = sb("ones", [128, 128])
        eplus1 = sb("eplus1", [128, E0])
        tokall = sb("tokall", [128, B], I32)
        xr = sb("xr", [128, D])
        zrow = sb("zrow", [1, D])
        fillt = sb("fillt", [128, E0], I32)
        lg = sb("lg", [128, E0])
        lg2 = sb("lg2", [128, E0])
        top8 = sb("top8", [128, 8])
        nmax = sb("nmax", [128, 1])
        ex = sb("ex", [128, E0])
        msk = sb("msk", [128, E0])
        macc = sb("macc", [128, E0])
        keep = sb("keep", [128, E0])
        slm = sb("slm", [128, E0])
        s8 = sb("s8", [128, 8])
        zz = sb("zz", [128, 8])
        wk = sb("wk", [128, E0])
        den = sb("den", [128, 1])
        eq = sb("eq", [128, 8, E0])
        w8 = sb("w8", [128, B, 8])
        idx8 = sb("idx8", [128, B, 8], U32)
        idxw = sb("idxw", [128, 8], U32)
        tokw = sb("tokw", [128, 1], I32)
        slots = sb("slots", [128, E0], I32)
        ixe = sb("ixe", [128, RING, 1], U32)
        xe = sb("xe", [128, RING, D])
        wgu = sb("wgu", [128, RING, KC, 2 * I0])
        wdn = sb("wdn", [I0, RING, D])
        xeT = sb("xeT", [128, 2, KC, 128])
        sg = sb("sg", [I0, 2, 128])
        aT = sb("aT", [I0, 2, 128])
        ye = sb("ye", [128, RING, D])
        yg = sb("yg", [128, 8, D])
        w8c = sb("w8c", [128, 8])
        w_qkv1 = sb("w_qkv1", [128, KC, 384])
        b_qkv1 = sb("b_qkv1", [128, 384])
        w_pr1 = sb("w_pr1", [128, KC, D])
        b_pr1 = sb("b_pr1", [128, D])
        cos1 = sb("cos1", [128, 16])
        sin1 = sb("sin1", [128, 16])
        qk1 = sb("qk1", [128, 320])
        ra1 = sb("ra1", [128, 320])
        rb1 = sb("rb1", [128, 320])
        qpad1 = sb("qpad1", [128, 4, 4, 32])
        kpad1 = sb("kpad1", [128, 1, 4, 32])
        vx1 = sb("vx1", [128, 4, 17])
        wqc = sb("wqc", [128, KC, HX * QX])
        wqk = sb("wqk", [HQ, 2, HX, C])
        weff = sb("weff", [128, HX // 2, D])
        cosq = sb("cosq", [HQ, 2, 128])
        sinq = sb("sinq", [HQ, 2, 128])
        cosk = sb("cosk", [128, C])
        sink = sb("sink", [128, C])
        onehot = sb("onehot", [HX, HX, 128])
        fq, fo = yg[:, 0:2, :], ye[:, 0:2, :]
        fc, fr = yg[:, 2:4, 0:QX], yg[0:RX, 4:6, 0:QX]
        fk, fv = yg[0:RX, 6:8, 0:C], yg[:, 6:8, C:2 * C]
        kvr = sb("kvr", [128, 128])
        ka = sb("ka", [128, C])
        kvT = sb("kvT", [C, 128])
        rp = sb("rp", [HQ, 4, 4, 128])
        qkT = sb("qkT", [C, HX, 128])
        nmx = sb("nmx", [128, HX])
        nmT = sb("nmT", [HX, 128])
        cn = sb("cn", [128, HX, C])
        cT = sb("cT", [128, HX // 2, 128])
        w_rt1 = sb("w_rt1", [128, KC, E1])
        lgp = sb("lgp", [128, E1 + 8])
        lgp2 = sb("lgp2", [128, E1 + 8])
        dw = sb("dw", [128, B, NF])
        dwc = sb("dwc", [128, 2, B])
        xT6 = sb("xT6", [128, KC, B, 128])
        wf = sb("wf", [128, 2, KC, 2 * I1])
        wfd = sb("wfd", [FH, 2, 2, D])
        sgf = cT[0:FH, :, :].rearrange("p (f a) t -> p f (a t)", f=2)
        af = cn[0:FH, :, :].rearrange("p (f a) t -> p f (a t)", f=2)

        xn3 = nc.dram_tensor("xn3", [NTOK + 1, D], F32).ap()
        table = nc.dram_tensor("table", [NSLOT, 1], I32).ap()
        yrows = nc.dram_tensor("yrows", [NSLOT + 1, D], F32).ap()

        loaded = sems(nc, ctx, "load", "x ctx const w0 w1 fill")
        chains = sems(nc, ctx, "chain", "dve pool act")
        ready = sems(nc, ctx, "ready", "pads masks")
        a0 = sems(nc, ctx, "a0", ATT_SEMS)
        x0 = sems(nc, ctx, "x0", ATT_SEMS)
        r0 = sems(nc, ctx, "r0", ROUTE_SEMS)
        m0 = sems(nc, ctx, "m0", MOE_SEMS)
        c0 = sems(nc, ctx, "c0", "credit yg sum")
        a1 = sems(nc, ctx, "a1", ATT_SEMS)
        x1 = sems(nc, ctx, "x1", XATT_SEMS)
        r1 = sems(nc, ctx, "r1", LN_SEMS + " xnt_ps xnt_sb lg_ps top ex done")
        f1 = sems(nc, ctx, "f1", FFN_SEMS)
        stored = ctx.enter_context(nc.semaphore("stored"))

        consts1 = ((tri, "tri"), (ones, "ones"), (eplus1, "eplus1"), (tokall, "tokall"), (cos1, "cos1"),
                   (sin1, "sin1"), (cosq, "cosq"), (sinq, "sinq"), (cosk, "cosk"), (sink, "sink"),
                   (onehot, "onehot"))
        N_W0, N_W1 = 5, len(consts1) + 5

        def xb(b):
            return x[:, bass.ds(b, 1), :].rearrange("p a d -> p (a d)")

        block = ctx.enter_context(nc.Block())

        @block.sync
        def _(sp):
            for dst, src in ((ident[:], "ident"), (never[:], "never"), (neverT[:], "neverT"), (alibi[:], "alibi")):
                sp.dma_start(dst, t[src]).then_inc(loaded["const"], 16)
            sp.dma_start(x[:], t["x"].rearrange("b s d -> s b d")).then_inc(loaded["x"], 16)
            sp.dma_start(w_qkv0[:], t["L0_attn_W_attn"].rearrange("(c p) n -> p c n", p=128)).then_inc(loaded["w0"], 16)
            sp.dma_start(b_qkv0[:], t["L0_attn_b_attn"].partition_broadcast(128)).then_inc(loaded["w0"], 16)
            sp.dma_start(w_pr0[:], t["L0_attn_W_proj"].rearrange("(c p) n -> p c n", p=128)).then_inc(loaded["w0"], 16)
            sp.dma_start(b_pr0[:], t["L0_attn_b_proj"].partition_broadcast(128)).then_inc(loaded["w0"], 16)
            sp.dma_start(ctxt[:], t["ctx_512"].rearrange("b s d -> s b d")).then_inc(loaded["ctx"], 16)
            sp.dma_start(w_rt0[:], t["L0_ffn_router_weight"].rearrange("(c p) n -> p c n", p=128)).then_inc(loaded["w0"], 16)
            for dst, src in consts1:
                sp.dma_start(dst[:], t[src]).then_inc(loaded["w1"], 16)
            sp.dma_start(w_qkv1[:], t["w_qkv1"].rearrange("(c p) n -> p c n", p=128)).then_inc(loaded["w1"], 16)
            sp.dma_start(b_qkv1[:], t["b_qkv1"].partition_broadcast(128)).then_inc(loaded["w1"], 16)
            sp.dma_start(w_pr1[:], t["w_o1"].rearrange("(c p) n -> p c n", p=128)).then_inc(loaded["w1"], 16)
            sp.dma_start(b_pr1[:], t["L1_attn_bo"].partition_broadcast(128)).then_inc(loaded["w1"], 16)
            sp.dma_start(w_rt1[:], t["w_rt1"].rearrange("(c p) n -> p c n", p=128)).then_inc(loaded["w1"], 16)
            sp.wait_ge(ready["pads"], 1)
            sp.dma_start(table.rearrange("(p e) a -> p (e a)", e=E0), fillt[:]).then_inc(loaded["fill"], 16)
            sp.dma_start(xn3[NTOK:NTOK + 1, :], zrow[:]).then_inc(loaded["fill"], 16)
            sp.dma_start(yrows[NSLOT:NSLOT + 1, :], zrow[:]).then_inc(loaded["fill"], 16)

            with sp.Fori(0, HX // 2) as hp:
                sp.wait_ge(x1["fold_free"], hp + 1)
                for dst, src in ((fq, "wq_x"), (fc, "w_kc_q"), (fr, "w_qr"), (fk, "w_kr"), (fv, "w_kc_kv"), (fo, "wo_x")):
                    sp.dma_start(dst, t[src][bass.ds(hp, 1)].rearrange("a p u n -> p (a u) n")) \
                        .then_inc(x1["fold_ld"], 16)

            with sp.Fori(0, B) as b:
                sp.wait_ge(r0["xn"], b + 1)
                sp.dma_start(xn3[0:NTOK, :].rearrange("(b p) d -> b p d", p=128)[bass.ds(b, 1)]
                             .rearrange("a p d -> (a p) d"), xr[:]).then_inc(r0["xn_st"], 16)

            sp.wait_ge(r0["scat"], 16 * 8 * B)
            sp.wait_ge(loaded["fill"], 16 * 3)
            sp.dma_start(slots[:], table.rearrange("(p e) a -> p (e a)", e=E0)).then_inc(m0["slots"], 16)
            yv = yrows[0:NSLOT, :].rearrange("(p e) d -> e p d", e=E0)

            def load_expert(u, e):
                sp.dma_start(wgu[:, u, :, :], t["w_gu0"][bass.ds(e, 1)].rearrange("a (c p) n -> p (a c) n", p=128)) \
                    .then_inc(m0[f"wl{u}"], 16)
                sp.dma_start(wdn[:, u, :], t["L0_ffn_down_proj"][bass.ds(e, 1)].rearrange("a p d -> p (a d)")) \
                    .then_inc(m0[f"wl{u}"], 16)

            def store_expert(u, e):
                sp.wait_ge(m0["y_sb"], e + 1)
                sp.dma_start(yv[bass.ds(e, 1)].rearrange("a p d -> (a p) d"), ye[:, u, :]).then_inc(m0[f"yst{u}"], 16)

            for u in range(RING):
                load_expert(u, u)
            with sp.Fori(0, E0 // RING - 1) as i:
                for u in range(RING):
                    store_expert(u, i * RING + u)
                    load_expert(u, i * RING + u + RING)
            for u in range(RING):
                store_expert(u, E0 - RING + u)

            def load_ffn(u, e):
                sp.dma_start(wf[:, u], t["w_gu1"][bass.ds(e, 1)].rearrange("a (c p) n -> p (a c) n", p=128)) \
                    .then_inc(f1[f"wl{u}"], 16)
                sp.dma_start(wfd[:, u], t["w_d1"][bass.ds(e, 1)].rearrange("a (c p) n -> p (a c) n", p=FH)) \
                    .then_inc(f1[f"wl{u}"], 16)

            for u in range(2):
                load_ffn(u, u)
            with sp.Fori(0, NF // 2 - 1) as i:
                for u in range(2):
                    sp.wait_ge(f1["y_ps"], (i * 2 + u + 1) * 8)
                    load_ffn(u, i * 2 + u + 2)
            with sp.Fori(0, B) as b:
                sp.wait_ge(f1["x_new"], 1)
                sp.dma_start(out[bass.ds(b, 1)].rearrange("a p d -> (a p) d"), xb(b)).then_inc(stored, 16)
            sp.wait_ge(stored, 16 * B)

        @block.gpsimd
        def _(pool):
            chain = Chain(pool, chains["pool"])

            def norm_rstd(s, b):
                pool.wait_ge(s["stats"], b + 1)
                chain(pool.tensor_tensor(var[:], mv[:, 1:2], eps[:], ALU.add))
                pool.tensor_tensor(rstd[:], var[:], neghalf[:], ALU.pow).then_inc(s["rstd"], 1)

            chain(pool.memset(neghalf[:], -0.5))
            chain(pool.memset(eps[:], EPS))
            pool.wait_ge(loaded["fill"], 16 * 3)
            pool.wait_ge(loaded["w1"], 16 * N_W1)
            with pool.Fori(0, B) as b:
                chain.turn()
                norm_rstd(a0, b)
                norm_rstd(x0, b)
                norm_rstd(r0, b)
                pool.wait_ge(r0["idx"], b + 1)
                chain(pool.tensor_copy(idxw[:], idx8[:, bass.ds(b, 1), :].rearrange("p a j -> p (a j)")))
                chain(pool.tensor_copy(tokw[:], tokall[:, bass.ds(b, 1)]))
                for j in range(TOP0):
                    pool.indirect_dma_start(table[:, :], bass.IndirectOffsetOnAxis(idxw[:, j:j + 1], 0), tokw[:, :],
                                            None, bounds_check=NSLOT - 1, oob_is_err=False) \
                        .then_inc(r0["scat"], 16)
                pool.wait_ge(r0["scat"], (b + 1) * (16 * TOP0))

            pool.sem_inc(m0["credit"], RING)
            pool.wait_ge(m0["slots"], 16)
            pool.wait_ge(r0["xn_st"], 16 * B)
            with pool.Fori(0, E0 // RING) as i:
                chain.turn()
                for u in range(RING):
                    pool.wait_ge(m0["credit"], i * RING + u + 1)
                    chain(pool.tensor_copy(ixe[:, u, :], slots[:, bass.ds(i * RING + u, 1)]))
                    pool.indirect_dma_start(xe[:, u, :], None, xn3[:, :],
                                            bass.IndirectOffsetOnAxis(ixe[:, u, :], 0)).then_inc(m0[f"xg{u}"], 16)

            for u in range(RING):
                pool.wait_ge(m0[f"yst{u}"], 16 * (E0 // RING + 1))
            pool.sem_inc(c0["credit"], 1)
            with pool.Fori(0, B) as b:
                chain.turn()
                pool.wait_ge(c0["credit"], b + 1)
                chain(pool.tensor_copy(idxw[:], idx8[:, bass.ds(b, 1), :].rearrange("p a j -> p (a j)")))
                for j in range(TOP0):
                    pool.indirect_dma_start(yg[:, j, :], None, yrows[:, :],
                                            bass.IndirectOffsetOnAxis(idxw[:, j:j + 1], 0)).then_inc(c0["yg"], 16)
                norm_rstd(a1, b)
                norm_rstd(x1, b)
                norm_rstd(r1, b)

        @block.scalar
        def _(act):
            def copy(dst, src):
                return act.activation(dst, src, ACT.Copy)

            def norm_turned(s, b):
                act.wait_ge(s["xnt_ps"], b + 1)
                copy(xnT[:], M0[:, 0:D].rearrange("p (c t) -> p c t", c=KC)).then_inc(s["xnt_sb"], 1)

            def attention(a, s, b):
                kbanks, qbanks = a.kbanks, a.halves
                for n in range(kbanks + qbanks):
                    m = bank[6 + n % 2]
                    act.wait_ge(s["kq_ps"], b * (kbanks + qbanks) + n + 1)
                    if n < kbanks:
                        g = min(4, a.kgroups)
                        dst = kT[:, 4 * n:4 * n + g, :]
                    else:
                        g = 4
                        dst = qT[:, 4 * (n - kbanks):4 * (n - kbanks) + 4, :]
                    copy(dst, m[:, 0:128 * g].rearrange("p (g t) -> p g t", g=g)).then_inc(s["kq_sb"], 1)
                for n in range(qbanks):
                    act.wait_ge(s["q2_ps"], b * qbanks + n + 1)
                    copy(q2T[:, 4 * n:4 * n + 4, :], bank[6 + n % 2][:].rearrange("p (g t) -> p g t", g=4)) \
                        .then_inc(s["q2_sb"], 1)
                jobs = len(a.jobs)
                for n in range(jobs):
                    act.wait_ge(s["st_ps"], b * jobs + n + 1)
                    if n >= 2:
                        act.wait_ge(s["pv_ps"], b * jobs + n - 1)
                    act.activation(PT[:, n % 2], ST[n % 3][:].rearrange("p (g t) -> p g t", g=4), ACT.Exp,
                                   scale=a.scale).then_inc(s["st_exp"], 1)

            def out_turned(s, b):
                act.wait_ge(s["ot_ps"], b + 1)
                copy(onT[:], M0[:, 0:D].rearrange("p (c t) -> p c t", c=KC)).then_inc(s["ot_sb"], 1)

            chain = Chain(act, chains["act"])
            with act.Fori(0, HX // 2) as hp:
                for u in range(2):
                    act.wait_ge(x1["fold_ps"], hp * 2 + u + 1)
                    copy(wqc[:, 0, bass.ds(hp * (2 * QX) + u * QX, QX)], M0[:, 0:QX])
                    copy(wqc[:, 1, bass.ds(hp * (2 * QX) + u * QX, QX)], M0[:, QX:2 * QX])
                    for half in range(2):
                        copy(wqk[:, half, bass.ds(hp * 2 + u, 1), :].rearrange("p a c -> p (a c)"),
                             M1[0:HQ, C * half:C * half + C])
                    copy(weff[64 * u:64 * u + 64, bass.ds(hp, 1), :].rearrange("p a d -> p (a d)"),
                         bank[5][64 * u:64 * u + 64, 0:D]).then_inc(x1["fold_sb"], 1)

            with act.Fori(0, B) as b:
                norm_turned(a0, b)
                attention(L0, a0, b)
                out_turned(a0, b)
                attention(X0, x0, b)
                norm_turned(r0, b)
                act.wait_ge(r0["top"], b + 1)
                act.activation(ex[:], lg[:], ACT.Exp, bias=nmax[:]).then_inc(r0["ex"], 1)

            with act.Fori(0, E0 // RING) as i:
                for u in range(RING):
                    e = i * RING + u
                    act.wait_ge(m0["xt_ps"], e + 1)
                    copy(xeT[:, u % 2], bank[6 + u % 2][:, 0:D].rearrange("p (c t) -> p c t", c=KC)).then_inc(m0["xt_sb"], 1)
                    act.wait_ge(m0["h_ps"], e + 1)
                    act.activation(sg[:, u % 2, :], SC[u % 2][0:I0, 0:128], ACT.Silu).then_inc(m0["sg"], 1)

            with act.Fori(0, B) as b:
                norm_turned(a1, b)
                attention(L1, a1, b)
                out_turned(a1, b)
                norm_turned(x1, b)
                act.wait_ge(x1["kt_ps"], b + 1)
                copy(kvT[:], M1[0:C, 0:128]).then_inc(x1["kt_sb"], 1)
                for n in range(XJ):
                    act.wait_ge(x1["qk_ps"], b * XJ + n + 1)
                    copy(qkT[:, 4 * n:4 * n + 4, :], bank[6 + n % 2][0:C, :].rearrange("p (h t) -> p h t", h=4)) \
                        .then_inc(x1["qk_sb"], 1)
                act.wait_ge(x1["nm_ps"], b + 1)
                copy(nmT[:], M0[0:HX, 0:128]).then_inc(x1["nm_sb"], 1)
                for n in range(XJ):
                    act.wait_ge(x1["st_ps"], b * XJ + n + 1)
                    if n >= 2:
                        act.wait_ge(x1["pv_ps"], b * XJ + n - 1)
                    act.activation(PT[:, n % 2], ST[n % 3][:].rearrange("p (g t) -> p g t", g=4), ACT.Exp) \
                        .then_inc(x1["st_exp"], 1)
                for n in range(2):
                    act.wait_ge(x1["ct_ps"], b * 2 + n + 1)
                    copy(cT[:, 4 * n:4 * n + 4, :], bank[6 + n][:].rearrange("p (h t) -> p h t", h=4)) \
                        .then_inc(x1["ct_sb"], 1)
                act.wait_ge(r1["xnt_ps"], b + 1)
                copy(xT6[:, :, bass.ds(b, 1), :].rearrange("p c a t -> p c (a t)"),
                     M0[:, 0:D].rearrange("p (c t) -> p c t", c=KC))
                copy(xnT[:], M0[:, 0:D].rearrange("p (c t) -> p c t", c=KC)).then_inc(r1["xnt_sb"], 1)
                act.wait_ge(r1["top"], b + 1)
                act.activation(ex[:, 0:E1], lgp[:, 0:E1], ACT.Exp, bias=nmax[:]).then_inc(r1["ex"], 1)

            with act.Fori(0, NF // 2) as i:
                for u in range(2):
                    for th in range(2):
                        for f in range(2):
                            act.wait_ge(f1["g_ps"], i * 8 + u * 4 + th * 2 + f + 1)
                            act.activation(sgf[:, f, :], bank[2 * f][0:FH, :], ACT.Silu).then_inc(f1["sg"], 1)

        @block.tensor
        def _(pe):
            def norm_turn(s, b, rows=xn):
                pe.wait_ge(s["xn"], b + 1)
                for c in range(KC):
                    last = pe.transpose(M0[:, 128 * c:128 * c + 128], rows[:, 128 * c:128 * c + 128], ident[:])
                last.then_inc(s["xnt_ps"], 1)
                pe.wait_ge(s["xnt_sb"], b + 1)

            def rows_times(dst, lhs, w, lo, n):
                for c in range(KC):
                    last = pe.matmul(dst, lhs[:, c, :], w[:, c, lo:lo + n], start=(c == 0), stop=(c == KC - 1))
                return last

            def attention(a, s, b, queries, keys, values):
                kbanks, qbanks, jobs = a.kbanks, a.halves, len(a.jobs)
                kflat = keys.rearrange("p g r c -> p g (r c)")
                qflat = queries.rearrange("p g r c -> p g (r c)")
                pe.wait_ge(s["qkv_sb"], b + 1)
                for n in range(kbanks + qbanks):
                    if n >= 2:
                        pe.wait_ge(s["kq_sb"], b * (kbanks + qbanks) + n - 1)
                    src, g0, g = (kflat, 4 * n, min(4, a.kgroups)) if n < kbanks else (qflat, 4 * (n - kbanks), 4)
                    for g1 in range(g):
                        last = pe.transpose(bank[6 + n % 2][:, 128 * g1:128 * g1 + 128], src[:, g0 + g1, :], ident[:])
                    last.then_inc(s["kq_ps"], 1)
                pe.wait_ge(s["kq_sb"], (b + 1) * (kbanks + qbanks))
                for n, (half, row) in enumerate(a.jobs):
                    lo, hi = 32 * row, 32 * row + a.dim + 1
                    if n >= 2:
                        pe.wait_ge(s["s_max"], b * jobs + n - 1)
                    dst = SC[n % 2]
                    if a.causal:
                        pe.matmul(dst[:].rearrange("p (g t) -> p g t", g=4), identb[:],
                                  maskq[:].unsqueeze(1).broadcast_to([128, 4, 128]), start=True, stop=True,
                                  skip_group_check=True)
                    for g in range(4):
                        kg = half if a.shared else 4 * half + g
                        last = pe.matmul(dst[:, 128 * g:128 * g + 128], qT[lo:hi, 4 * half + g, :], kT[lo:hi, kg, :],
                                         start=not a.causal, stop=True, skip_group_check=True)
                    last.then_inc(s["s_ps"], 1)
                for n in range(qbanks):
                    pe.wait_ge(s["s_max"], b * jobs + 4 * (n + 1))
                    for g in range(4):
                        last = pe.transpose(bank[6 + n % 2][:, 128 * g:128 * g + 128], qflat[:, 4 * n + g, :], ident[:])
                    last.then_inc(s["q2_ps"], 1)

                def scores(n):
                    half, row = a.jobs[n]
                    lo, hi = 32 * row, 32 * row + a.rows
                    if row == 0:
                        pe.wait_ge(s["q2_sb"], b * qbanks + half + 1)
                    if n >= 3:
                        pe.wait_ge(s["st_exp"], b * jobs + n - 2)
                    dst = ST[n % 3]
                    if a.causal:
                        pe.matmul(dst[:].rearrange("p (g t) -> p g t", g=4), identb[:],
                                  maskk[:].unsqueeze(1).broadcast_to([128, 4, 128]), start=True, stop=True,
                                  skip_group_check=True)
                    if a.shared:
                        last = pe.matmul(dst[:].rearrange("p (g t) -> p g t", g=4), kT[lo:hi, half, :],
                                         q2T[lo:hi, 4 * half:4 * half + 4, :], start=not a.causal, stop=True,
                                         skip_group_check=True)
                    else:
                        for g in range(4):
                            last = pe.matmul(dst[:, 128 * g:128 * g + 128], kT[lo:hi, 4 * half + g, :],
                                             q2T[lo:hi, 4 * half + g, :], start=not a.causal, stop=True,
                                             skip_group_check=True)
                    last.then_inc(s["st_ps"], 1)

                def mix(n):
                    half, row = a.jobs[n]
                    w = a.dim + 1
                    pe.wait_ge(s["st_exp"], b * jobs + n + 1)
                    for g in range(4):
                        h = a.head(half, row, g)
                        kv = h // 4 if a.shared else h
                        last = pe.matmul(PV[:, w * h:w * h + w], PT[:, n % 2, g, :], values[:, kv, :],
                                         start=True, stop=True, skip_group_check=True)
                    last.then_inc(s["pv_ps"], 1)

                for n in range(jobs + 1):
                    if n < jobs:
                        scores(n)
                    if n >= 1:
                        mix(n - 1)

            def project(s, b, w):
                pe.wait_ge(s["on_sb"], b + 1)
                for c in range(KC):
                    last = pe.transpose(M0[:, 128 * c:128 * c + 128], on[:, 128 * c:128 * c + 128], ident[:])
                last.then_inc(s["ot_ps"], 1)
                pe.wait_ge(s["ot_sb"], b + 1)
                rows_times(M1[:, 0:D], onT, w, 0, D).then_inc(s["pr_ps"], 1)

            pe.wait_ge(loaded["const"], 16 * 4)
            pe.wait_ge(ready["masks"], 3)
            pe.wait_ge(loaded["w0"], 16 * N_W0)
            pe.wait_ge(loaded["w1"], 16 * N_W1)
            pe.sem_inc(x1["fold_free"], 1)
            with pe.Fori(0, HX // 2) as hp:
                pe.wait_ge(x1["fold_ld"], (hp + 1) * 96)
                for u in range(2):
                    if u == 1:
                        pe.wait_ge(x1["fold_sb"], hp * 2 + 1)
                    for c in range(KC):
                        pe.matmul(M0[:, QX * c:QX * c + QX], fq[:, u, 128 * c:128 * c + 128], fc[:, u, :], start=True, stop=True)
                    for half in range(2):
                        pe.matmul(M1[0:HQ, C * half:C * half + C], fr[:, u, HQ * half:HQ * half + HQ], fk[:, u, :],
                                  start=True, stop=True)
                    pe.matmul(bank[5][64 * u:64 * u + 64, 0:D], fv[:, u, :], fo[:, u, :], start=True, stop=True) \
                        .then_inc(x1["fold_ps"], 1)
                pe.wait_ge(x1["fold_sb"], hp * 2 + 2)
                pe.sem_inc(x1["fold_free"], 1)

            with pe.Fori(0, B) as b:
                norm_turn(a0, b)
                rows_times(M1[:], xnT, w_qkv0, 0, 2 * D)
                rows_times(M0[:, 0:D], xnT, w_qkv0, 2 * D, D).then_inc(a0["qkv_ps"], 1)
                attention(L0, a0, b, qpad[:], kpad[:], vx)
                project(a0, b, w_pr0)
                attention(X0, x0, b, qpad[:], kpadx[:], vc)
                norm_turn(r0, b, xr)
                rows_times(M1[:, 0:E0], xnT, w_rt0, 0, E0).then_inc(r0["lg_ps"], 1)
                pe.wait_ge(r0["msk"], b + 1)
                pe.matmul(M0[:, 0:E0], tri[:], msk[:], start=True, stop=False)
                pe.matmul(M0[:, 0:E0], ones[:], macc[:], start=False, stop=True).then_inc(r0["pos_ps"], 1)

            with pe.Fori(0, E0 // RING) as i:
                for u in range(RING):
                    e, v = i * RING + u, u % 2
                    pe.wait_ge(m0[f"xg{u}"], (i + 1) * 16)
                    for c in range(KC):
                        last = pe.transpose(bank[6 + v][:, 128 * c:128 * c + 128], xe[:, u, 128 * c:128 * c + 128], ident[:])
                    last.then_inc(m0["xt_ps"], 1)
                    pe.wait_ge(m0["xt_sb"], e + 1)
                    pe.sem_inc(m0["credit"], 1)
                    pe.wait_ge(m0[f"wl{u}"], (i + 1) * 32)
                    for k in range(2):
                        for c in range(KC):
                            last = pe.matmul(SC[v][0:I0, 128 * k:128 * k + 128], wgu[:, u, c, I0 * k:I0 * k + I0],
                                             xeT[:, v, c, :], start=(c == 0), stop=(c == KC - 1))
                    last.then_inc(m0["h_ps"], 1)
                    pe.wait_ge(m0["a_sb"], e + 1)
                    pe.matmul(ST[v][:, 0:D], aT[:, v, :], wdn[:, u, :], start=True, stop=True).then_inc(m0["y_ps"], 1)

            with pe.Fori(0, B) as b:
                norm_turn(a1, b)
                rows_times(M1[:, 0:384], xnT, w_qkv1, 0, 384).then_inc(a1["qkv_ps"], 1)
                attention(L1, a1, b, qpad1[:], kpad1[:], vx1)
                project(a1, b, w_pr1)
                norm_turn(x1, b)
                pe.wait_ge(x1["kv_sb"], b + 1)
                pe.transpose(M1[:, 0:128], kvr[:], ident[:]).then_inc(x1["kt_ps"], 1)
                pe.wait_ge(x1["kt_sb"], b + 1)

                def queries(n):
                    for half in range(2):
                        for h in range(4):
                            lo = (4 * n + h) * QX + half * HQ
                            for c in range(KC):
                                last = pe.matmul(bank[2 + 2 * (n % 2) + half][0:HQ, 128 * h:128 * h + 128],
                                                 wqc[:, c, lo:lo + HQ], xnT[:, c, :], start=(c == 0), stop=(c == KC - 1))
                    last.then_inc(x1["qb_ps"], 1)

                def to_keys(n):
                    pe.wait_ge(x1["rope"], b * XJ + n + 1)
                    for h in range(4):
                        for k in range(4):
                            last = pe.matmul(bank[6 + n % 2][0:C, 128 * h:128 * h + 128], wqk[:, k // 2, 4 * n + h, :],
                                             rp[:, k, h, :], start=(k == 0), stop=(k == 3))
                    last.then_inc(x1["qk_ps"], 1)

                for n in range(XJ + 1):
                    if n < XJ:
                        if n >= 2:
                            pe.wait_ge(x1["rope"], b * XJ + n - 1)
                        queries(n)
                    if n >= 1:
                        if n >= 3:
                            pe.wait_ge(x1["qk_sb"], b * XJ + n - 2)
                        to_keys(n - 1)
                for n in range(XJ):
                    pe.wait_ge(x1["qk_sb"], b * XJ + n + 1)
                    if n >= 2:
                        pe.wait_ge(x1["s_max"], b * XJ + n - 1)
                    for h in range(4):
                        last = pe.matmul(SC[n % 2][:, 128 * h:128 * h + 128], qkT[:, 4 * n + h, :], kvT[:],
                                         start=True, stop=True)
                    last.then_inc(x1["s_ps"], 1)
                pe.wait_ge(x1["s_max"], (b + 1) * XJ)
                pe.transpose(M0[0:HX, 0:128], nmx[:], ident[:]).then_inc(x1["nm_ps"], 1)
                pe.wait_ge(x1["nm_sb"], b + 1)

                def xscores(n):
                    if n >= 3:
                        pe.wait_ge(x1["st_exp"], b * XJ + n - 2)
                    dst = ST[n % 3]
                    pe.matmul(dst[:].rearrange("p (g t) -> p g t", g=4), kvT[:], qkT[:, 4 * n:4 * n + 4, :],
                              start=True, stop=True, skip_group_check=True)
                    for h in range(4):
                        last = pe.matmul(dst[:, 128 * h:128 * h + 128], onehot[:, 4 * n + h, :], nmT[:],
                                         start=False, stop=True, skip_group_check=True)
                    last.then_inc(x1["st_ps"], 1)

                def xmix(n):
                    pe.wait_ge(x1["st_exp"], b * XJ + n + 1)
                    if n >= 2:
                        pe.wait_ge(x1["cn_sb"], b * XJ + n - 1)
                    for h in range(4):
                        last = pe.matmul((PV, SC[1])[n % 2][:, (C + 1) * h:(C + 1) * (h + 1)], PT[:, n % 2, h, :], kvr[:, 0:C + 1],
                                         start=True, stop=True)
                    last.then_inc(x1["pv_ps"], 1)

                for n in range(XJ + 1):
                    if n < XJ:
                        xscores(n)
                    if n >= 1:
                        xmix(n - 1)
                for n in range(2):
                    pe.wait_ge(x1["cn_sb"], b * XJ + 2 * n + 2)
                    for h in range(4):
                        last = pe.transpose(bank[6 + n][:, 128 * h:128 * h + 128],
                                            cn[:, 8 * n + 2 * h:8 * n + 2 * h + 2, :].rearrange("p h c -> p (h c)"), ident[:])
                    last.then_inc(x1["ct_ps"], 1)
                pe.wait_ge(x1["ct_sb"], b * 2 + 2)
                for n in range(HX // 2):
                    last = pe.matmul(SC[0][:, 0:D], cT[:, n, :], weff[:, n, :], start=(n == 0), stop=(n == HX // 2 - 1))
                last.then_inc(x1["pr_ps"], 1)
                norm_turn(r1, b)
                rows_times(M1[:, 0:E1], xnT, w_rt1, 0, E1).then_inc(r1["lg_ps"], 1)

            pe.wait_ge(r1["done"], B)
            pe.sem_inc(f1["credit"], 1)
            with pe.Fori(0, NF // 2) as i:
                for u in range(2):
                    pe.wait_ge(f1[f"wl{u}"], (i + 1) * 32)
                    for th in range(2):
                        step = i * 4 + u * 2 + th
                        pe.wait_ge(f1["credit"], step + 1)
                        for f in range(2):
                            for k in range(2):
                                for c in range(KC):
                                    last = pe.matmul(bank[2 * f + k][0:FH, :], wf[:, u, c, I1 * k + FH * f:I1 * k + FH * f + FH],
                                                     xT6[:, c, 4 * th:4 * th + 4, :].rearrange("p b t -> p (b t)"),
                                                     start=(c == 0), stop=(c == KC - 1))
                            last.then_inc(f1["g_ps"], 1)
                        pe.wait_ge(f1["a_sb"], (step + 1) * 2)
                        for q in range(4):
                            if q >= 2:
                                pe.wait_ge(f1["y_sb"], step * 4 + q - 1)
                            for f in range(2):
                                last = pe.matmul(bank[4 + q % 2][:, 0:D], af[:, f, 128 * q:128 * q + 128], wfd[:, u, f, :],
                                                 start=(f == 0), stop=(f == 1))
                            last.then_inc(f1["y_ps"], 1)

        @block.vector
        def _(dve):
            chain = Chain(dve, chains["dve"])

            def norm(s, b):
                chain(dve.bn_stats(stats[:], xb(b)))
                dve.bn_aggr(mv[:], stats[:]).then_inc(s["stats"], 1)
                dve.wait_ge(s["rstd"], b + 1)
                return (xb(b), mv[:, 0:1], rstd[:], ALU.subtract, ALU.mult)

            def maxima(a, s, b, qpad=qpad):
                for n, (half, row) in enumerate(a.jobs):
                    dve.wait_ge(s["s_ps"], b * len(a.jobs) + n + 1)
                    dve.tensor_reduce(qpad[:, 4 * half:4 * half + 4, row, a.dim + 1],
                                      SC[n % 2][:].rearrange("p (g t) -> p g t", g=4), AX.X, ALU.max,
                                      negate=True).then_inc(s["s_max"], 1)

            def weighted(a, s, b, dst):
                w = a.dim + 1
                pv = PV[:, 0:w * a.heads].rearrange("p (h w) -> p h w", w=w)
                dve.wait_ge(s["pv_ps"], (b + 1) * len(a.jobs))
                chain(dve.reciprocal(rden[:, 0:a.heads], pv[:, :, a.dim]))
                return dve.tensor_tensor(dst.rearrange("p (h d) -> p h d", d=a.dim), pv[:, :, 0:a.dim],
                                         rden[:, 0:a.heads].unsqueeze(2).broadcast_to([128, a.heads, a.dim]),
                                         ALU.mult)

            dve.wait_ge(loaded["const"], 16 * 4)
            for dst, src in ((identb, ident), (maskq, never), (maskk, neverT)):
                dve.tensor_copy(dst[:], src[:]).then_inc(ready["masks"], 1)
            for tile in (qpad, kpad, kpadx, vx, vc, qpad1, kpad1, zrow, macc, kvr):
                chain(dve.memset(tile[:], 0.0))
            dve.wait_ge(loaded["const"], 16 * 4)
            chain(dve.memset(qpad[:, :, :, L0.dim:L0.dim + 1], 1.0))
            chain(dve.memset(kpad[:, :, :, L0.dim:L0.dim + 2], 1.0))
            chain(dve.memset(kpadx[:, :, :, X0.dim + 1:X0.dim + 2], 1.0))
            chain(dve.tensor_scalar(kpad[:, :, :, L0.dim:L0.dim + 1], kpad[:, :, :, L0.dim:L0.dim + 1], alibi[:],
                                    None, ALU.mult))
            chain(dve.memset(vx[:, :, 8:9], 1.0))
            chain(dve.memset(vc[:, :, 8:9], 1.0))
            chain(dve.memset(kpad1[:, :, :, L1.dim + 1:L1.dim + 2], 1.0))
            chain(dve.memset(vx1[:, :, 16:17], 1.0))
            chain(dve.memset(kvr[:, C:C + 1], 1.0))
            chain(dve.memset(dw[:, :, E1:NF], 1.0))
            chain(dve.memset(lgp[:, E1:E1 + 8], -3e38))
            dve.memset(fillt[:], NTOK).then_inc(ready["pads"], 1)
            dve.wait_ge(ready["pads"], 1)
            dve.wait_ge(loaded["w1"], 16 * N_W1)
            dve.wait_ge(loaded["x"], 16)
            dve.wait_ge(loaded["ctx"], 16)
            dve.wait_ge(loaded["w0"], 16 * N_W0)

            with dve.Fori(0, B) as b:
                chain.turn()
                ln = norm(a0, b)
                dve.tensor_scalar(xn[:], *ln).then_inc(a0["xn"], 1)
                dve.wait_ge(a0["qkv_ps"], b + 1)
                d8 = dict(r=4, c=8)
                dve.tensor_tensor(kpad[:, :, :, 0:8], M1[:, D:2 * D].rearrange("p (g r c) -> p g r c", **d8),
                                  b_qkv0[:, D:2 * D].rearrange("p (g r c) -> p g r c", **d8), ALU.add)
                dve.tensor_tensor(vx[:, :, 0:8], M0[:, 0:D].rearrange("p (h c) -> p h c", c=8),
                                  b_qkv0[:, 2 * D:3 * D].rearrange("p (h c) -> p h c", c=8), ALU.add)
                dve.tensor_tensor(qpad[:, :, :, 0:8], M1[:, 0:D].rearrange("p (g r c) -> p g r c", **d8),
                                  b_qkv0[:, 0:D].rearrange("p (g r c) -> p g r c", **d8), ALU.add) \
                    .then_inc(a0["qkv_sb"], 1)
                maxima(L0, a0, b)
                weighted(L0, a0, b, on[:]).then_inc(a0["on_sb"], 1)
                dve.wait_ge(a0["pr_ps"], b + 1)
                chain(dve.tensor_tensor(tmp[:], M1[:, 0:D], b_pr0[:], ALU.add))
                chain(dve.tensor_tensor(xb(b), xb(b), tmp[:], ALU.add))
                _, mean, rs, op0, op1 = norm(x0, b)
                cb = ctxt[:, bass.ds(b, 1), :].rearrange("p a d -> p (a d)")
                dve.tensor_copy(kpadx[:, :, :, 0:8], cb.rearrange("p (h r c) -> p h r c", r=4, c=8))
                dve.tensor_copy(vc[:, :, 0:8], cb.rearrange("p (h c) -> p h c", c=8))
                chain(dve.tensor_scalar(xn[:], xb(b), mean, rs, op0, op1))
                xv = xn[:].rearrange("p (h r g c) -> p h r g c", h=2, r=4, g=4)
                for half in range(2):
                    last = dve.tensor_copy(qpad[:, 4 * half:4 * half + 4, :, 0:8],
                                           xv[:, half].rearrange("p r g c -> p g r c"))
                last.then_inc(x0["qkv_sb"], 1)
                maxima(X0, x0, b)
                chain(weighted(X0, x0, b, tmp[:]))
                chain(dve.tensor_tensor(xb(b), xb(b), tmp[:], ALU.add))
                ln = norm(r0, b)
                dve.tensor_scalar(xr[:], *ln).then_inc(r0["xn"], 1)
                dve.wait_ge(r0["lg_ps"], b + 1)
                chain(dve.tensor_copy(lg[:], M1[:, 0:E0]))
                chain(dve.max(top8[:], lg[:]))
                dve.tensor_scalar(nmax[:], top8[:, 0:1], -1.0, None, ALU.mult).then_inc(r0["top"], 1)
                chain(dve.match_replace(lg2[:], top8[:], lg[:], -3e38))
                dve.tensor_tensor(msk[:], lg[:], lg2[:], ALU.not_equal).then_inc(r0["msk"], 1)
                dve.wait_ge(r0["msk"], b + 1)
                dve.wait_ge(r0["ex"], b + 1)
                chain(dve.tensor_tensor(wk[:], ex[:], msk[:], ALU.mult))
                chain(dve.tensor_reduce(den[:], wk[:], AX.X, ALU.add))
                chain(dve.reciprocal(den[:], den[:]))
                dve.wait_ge(r0["pos_ps"], b + 1)
                chain(dve.scalar_tensor_tensor(keep[:], M0[:, 0:E0], float(CAP), msk[:], ALU.is_lt, ALU.mult))
                chain(dve.scalar_tensor_tensor(slm[:], M0[:, 0:E0], float(E0), eplus1[:], ALU.mult, ALU.add))
                chain(dve.tensor_tensor(slm[:], slm[:], keep[:], ALU.mult))
                chain(dve.max(s8[:], slm[:]))
                chain(dve.tensor_scalar(zz[:], s8[:], 0.0, float(NSLOT + 1), ALU.is_equal, ALU.mult))
                dve.scalar_tensor_tensor(idx8[:, bass.ds(b, 1), :].rearrange("p a j -> p (a j)"), s8[:], -1.0, zz[:],
                                         ALU.add, ALU.add).then_inc(r0["idx"], 1)
                chain(dve.scalar_tensor_tensor(wk[:], wk[:], den[:], keep[:], ALU.mult, ALU.mult))
                chain(dve.tensor_tensor(eq[:], slm[:].unsqueeze(1).broadcast_to([128, 8, E0]),
                                        s8[:].unsqueeze(2).broadcast_to([128, 8, E0]), ALU.is_equal))
                chain(dve.tensor_tensor(eq[:], eq[:], wk[:].unsqueeze(1).broadcast_to([128, 8, E0]), ALU.mult))
                chain(dve.tensor_reduce(w8[:, bass.ds(b, 1), :].rearrange("p a j -> p (a j)"), eq[:], AX.X, ALU.add))
                chain(dve.tensor_tensor(macc[:], macc[:], msk[:], ALU.add))
                dve.wait_ge(r0["xn_st"], (b + 1) * 16)

            chain.turn()
            for u in range(RING):
                dve.sem_inc(m0[f"yst{u}"], 16)
            with dve.Fori(0, E0 // RING) as i:
                chain.turn()
                for u in range(RING):
                    e = i * RING + u
                    dve.wait_ge(m0["sg"], e + 1)
                    dve.tensor_tensor(aT[:, u % 2, :], sg[:, u % 2, :], SC[u % 2][0:I0, 128:256], ALU.mult) \
                        .then_inc(m0["a_sb"], 1)
                    dve.wait_ge(m0["y_ps"], e + 1)
                    dve.wait_ge(m0[f"yst{u}"], (i + 1) * 16)
                    dve.tensor_copy(ye[:, u, :], ST[u % 2][:, 0:D]).then_inc(m0["y_sb"], 1)

            with dve.Fori(0, B) as b:
                chain.turn()
                chain(dve.tensor_copy(w8c[:], w8[:, bass.ds(b, 1), :].rearrange("p a j -> p (a j)")))
                dve.wait_ge(c0["yg"], (b + 1) * (16 * TOP0))
                for j in range(TOP0):
                    last = dve.scalar_tensor_tensor(xb(b), yg[:, j, :], w8c[:, j:j + 1], xb(b), ALU.mult, ALU.add)
                    chain(last)
                dve.sem_inc(c0["credit"], 1)
                ln = norm(a1, b)
                dve.tensor_scalar(xn[:], *ln).then_inc(a1["xn"], 1)
                dve.wait_ge(a1["qkv_ps"], b + 1)
                chain(dve.tensor_tensor(qk1[:], M1[:, 0:320], b_qkv1[:, 0:320], ALU.add))
                dve.tensor_tensor(vx1[:, :, 0:16], M1[:, 320:384].rearrange("p (h c) -> p h c", c=16),
                                  b_qkv1[:, 320:384].rearrange("p (h c) -> p h c", c=16), ALU.add)
                h16 = qk1[:].rearrange("p (h c) -> p h c", c=16)
                dve.tensor_tensor(ra1[:].rearrange("p (h c) -> p h c", c=16), h16,
                                  cos1[:].unsqueeze(1).broadcast_to([128, 20, 16]), ALU.mult)
                pairs = qk1[:].rearrange("p (h c t) -> p h c t", c=8, t=2)
                rpairs = rb1[:].rearrange("p (h c t) -> p h c t", c=8, t=2)
                spairs = sin1[:].rearrange("p (c t) -> p c t", t=2)
                dve.tensor_tensor(rpairs[:, :, :, 0], pairs[:, :, :, 1],
                                  spairs[:, :, 0].unsqueeze(1).broadcast_to([128, 20, 8]), ALU.mult)
                chain(dve.tensor_tensor(rpairs[:, :, :, 1], pairs[:, :, :, 0],
                                        spairs[:, :, 1].unsqueeze(1).broadcast_to([128, 20, 8]), ALU.mult))
                dve.tensor_tensor(kpad1[:, 0, :, 0:16], ra1[:, 256:320].rearrange("p (r c) -> p r c", c=16),
                                  rb1[:, 256:320].rearrange("p (r c) -> p r c", c=16), ALU.add)
                dve.tensor_tensor(qpad1[:, :, :, 0:16], ra1[:, 0:256].rearrange("p (g r c) -> p g r c", r=4, c=16),
                                  rb1[:, 0:256].rearrange("p (g r c) -> p g r c", r=4, c=16), ALU.add) \
                    .then_inc(a1["qkv_sb"], 1)
                maxima(L1, a1, b, qpad1)
                weighted(L1, a1, b, on[:]).then_inc(a1["on_sb"], 1)
                dve.wait_ge(a1["pr_ps"], b + 1)
                chain(dve.tensor_tensor(tmp[:], M1[:, 0:D], b_pr1[:], ALU.add))
                chain(dve.tensor_tensor(xb(b), xb(b), tmp[:], ALU.add))
                ln = norm(x1, b)
                dve.tensor_scalar(xn[:], *ln).then_inc(x1["xn"], 1)
                cb = ctxt[:, bass.ds(b, 1), :].rearrange("p a d -> p (a d)")
                dve.tensor_tensor(kvr[:, 0:C], cb, cosk[:], ALU.mult)
                dve.tensor_tensor(ka[:, 0:C // 2], cb[:, C // 2:C], sink[:, 0:C // 2], ALU.mult)
                chain(dve.tensor_tensor(ka[:, C // 2:C], cb[:, 0:C // 2], sink[:, C // 2:C], ALU.mult))
                dve.tensor_tensor(kvr[:, 0:C], kvr[:, 0:C], ka[:], ALU.add).then_inc(x1["kv_sb"], 1)
                for n in range(XJ):
                    dve.wait_ge(x1["qb_ps"], b * XJ + n + 1)
                    if n >= 1:
                        dve.wait_ge(x1["qk_ps"], b * XJ + n)
                    lo, hi = (bank[2 + 2 * (n % 2) + k][0:HQ, :].rearrange("p (h t) -> p h t", h=4) for k in range(2))
                    for k, (src, tab) in enumerate(((lo, cosq[:, 0]), (hi, sinq[:, 0]), (hi, cosq[:, 1]), (lo, sinq[:, 1]))):
                        last = dve.tensor_tensor(rp[:, k], src, tab.unsqueeze(1).broadcast_to([HQ, 4, 128]), ALU.mult)
                    last.then_inc(x1["rope"], 1)
                for n in range(XJ):
                    dve.wait_ge(x1["s_ps"], b * XJ + n + 1)
                    dve.tensor_reduce(nmx[:, 4 * n:4 * n + 4], SC[n % 2][:].rearrange("p (g t) -> p g t", g=4), AX.X,
                                      ALU.max, negate=True).then_inc(x1["s_max"], 1)
                for n in range(XJ):
                    dve.wait_ge(x1["pv_ps"], b * XJ + n + 1)
                    pv = (PV, SC[1])[n % 2][:, 0:4 * (C + 1)].rearrange("p (h w) -> p h w", w=C + 1)
                    chain(dve.reciprocal(rden[:, 4 * n:4 * n + 4], pv[:, :, C]))
                    dve.tensor_tensor(cn[:, 4 * n:4 * n + 4, :], pv[:, :, 0:C],
                                      rden[:, 4 * n:4 * n + 4].unsqueeze(2).broadcast_to([128, 4, C]), ALU.mult) \
                        .then_inc(x1["cn_sb"], 1)
                dve.wait_ge(x1["pr_ps"], b + 1)
                chain(dve.tensor_tensor(xb(b), SC[0][:, 0:D], xb(b), ALU.add))
                ln = norm(r1, b)
                dve.tensor_scalar(xn[:], *ln).then_inc(r1["xn"], 1)
                dve.wait_ge(r1["lg_ps"], b + 1)
                chain(dve.tensor_copy(lgp[:, 0:E1], M1[:, 0:E1]))
                chain(dve.max(top8[:], lgp[:, 0:E1]))
                chain(dve.memset(top8[:, TOP1:8], -3e38))
                dve.tensor_scalar(nmax[:], top8[:, 0:1], -1.0, None, ALU.mult).then_inc(r1["top"], 1)
                chain(dve.match_replace(lgp2[:], top8[:], lgp[:], -2e38))
                chain(dve.tensor_tensor(msk[:, 0:E1], lgp[:, 0:E1], lgp2[:, 0:E1], ALU.not_equal))
                dve.wait_ge(r1["ex"], b + 1)
                chain(dve.tensor_reduce(den[:], ex[:, 0:E1], AX.X, ALU.add))
                chain(dve.reciprocal(den[:], den[:]))
                dve.scalar_tensor_tensor(dw[:, bass.ds(b, 1), 0:E1].rearrange("p a e -> p (a e)"), ex[:, 0:E1], den[:],
                                         msk[:, 0:E1], ALU.mult, ALU.mult).then_inc(r1["done"], 1)

            dve.wait_ge(r1["done"], B)
            chain.turn()
            with dve.Fori(0, NF // 2) as i:
                for u in range(2):
                    chain.turn()
                    chain(dve.tensor_copy(dwc[:, u, :], dw[:, :, bass.ds(i * 2 + u, 1)].rearrange("p b a -> p (b a)")))
                    for th in range(2):
                        step = i * 4 + u * 2 + th
                        for f in range(2):
                            dve.wait_ge(f1["sg"], step * 2 + f + 1)
                            dve.tensor_tensor(af[:, f, :], sgf[:, f, :], bank[2 * f + 1][0:FH, :], ALU.mult) \
                                .then_inc(f1["a_sb"], 1)
                        dve.sem_inc(f1["credit"], 1)
                        for q in range(4):
                            dve.wait_ge(f1["y_ps"], step * 4 + q + 1)
                            dve.scalar_tensor_tensor(x[:, 4 * th + q, :], bank[4 + q % 2][:, 0:D], dwc[:, u, 4 * th + q:4 * th + q + 1],
                                                     x[:, 4 * th + q, :], ALU.mult, ALU.add).then_inc(f1["y_sb"], 1)
            dve.wait_ge(f1["y_sb"], NF * 8)
            dve.sem_inc(f1["x_new"], 1)


def constants():
    import numpy as np
    q, k = np.arange(128)[:, None], np.arange(128)[None, :]
    never = np.where(k > q, -1e30, 0.0)
    slope = 2.0 ** (-8.0 / 32.0)
    e = np.arange(E0)[None, :]

    def angles(n, dim):
        inv = (1.0 / 10000.0 ** (np.arange(0, dim, 2, dtype=np.float32) / np.float32(dim))).astype(np.float32)
        return np.repeat((np.arange(n, dtype=np.float32)[:, None] * inv[None, :]).astype(np.float32), 2, axis=1)

    f1, fq, fk = angles(S, 16), angles(S, QX), angles(S, C)
    sign = np.where(np.arange(16) % 2 == 0, -1.0, 1.0)
    halves = lambda a: np.ascontiguousarray(a.T.reshape(2, HQ, S).transpose(1, 0, 2)).astype(np.float32)
    first = lambda w: np.where(np.arange(w) < w // 2, -1.0, 1.0)
    f = lambda a: np.ascontiguousarray(a).astype(np.float32)
    return {
        "tri": f(q < k), "ones": np.ones((128, 128), np.float32), "eplus1": f(np.broadcast_to(e + 1, (128, E0))),
        "tokall": (np.arange(B)[None, :] * S + np.arange(128)[:, None]).astype(np.int32),
        "cos1": f(np.cos(f1)), "sin1": f(np.sin(f1) * sign),
        "cosq": halves(np.cos(fq)), "sinq": halves(np.sin(fq) * first(QX)),
        "cosk": f(np.cos(fk)), "sink": f(np.sin(fk) * first(C)),
        "onehot": f(np.broadcast_to(np.eye(HX)[:, :, None], (HX, HX, 128))),
        "ident": np.eye(128, dtype=np.float32),
        "never": never.astype(np.float32),
        "neverT": np.ascontiguousarray(never.T).astype(np.float32),
        "alibi": (slope * np.arange(128) * np.sqrt(8.0)).astype(np.float32)[:, None],
    }


def laid_out(w):
    import numpy as np

    def by_group(a):
        return a.reshape(*a.shape[:-1], 4, 4, 16).swapaxes(-3, -2).reshape(*a.shape)

    def pairs(a):
        return a.reshape(HX // 2, 2, *a.shape[1:]).transpose(0, 2, 1, 3)

    shared = lambda a: a.reshape(D, 2, I1).transpose(1, 0, 2)
    return {
        "w_gu0": np.concatenate([w["L0_ffn_gate_proj"], w["L0_ffn_up_proj"]], axis=2),
        "w_qkv1": np.concatenate([by_group(w["L1_attn_Wq"].T), w["L1_attn_Wk"].T, w["L1_attn_Wv"].T], axis=1),
        "b_qkv1": np.concatenate([by_group(w["L1_attn_bq"]), w["L1_attn_bk"], w["L1_attn_bv"]]),
        "w_o1": w["L1_attn_Wo"].T,
        "w_rt1": w["L1_ffn_gate_weight"].T,
        "wq_x": pairs(w["L1_xattn_Wq"].reshape(HX, KX, D)),
        "w_kc_q": pairs(w["L1_xattn_w_kc_q"]),
        "w_qr": pairs(w["L1_xattn_W_qr"].transpose(0, 2, 1)),
        "w_kr": pairs(w["L1_xattn_W_kr"].transpose(0, 2, 1)),
        "w_kc_kv": pairs(w["L1_xattn_w_kc_kv"]),
        "wo_x": pairs(w["L1_xattn_Wo"].T.reshape(HX, KX, D)),
        "w_gu1": np.concatenate([
            np.concatenate([w["L1_ffn_w_gate"], shared(w["L1_ffn_ws_gate"])], axis=0),
            np.concatenate([w["L1_ffn_w_up"], shared(w["L1_ffn_ws_up"])], axis=0)], axis=2),
        "w_d1": np.concatenate([w["L1_ffn_w_down"], w["L1_ffn_ws_down"].reshape(2, I1, D)], axis=0),
    }


def kernel(**inputs):
    import numpy as _np
    import concourse.bacc as _bacc
    from concourse import mybir as _mybir
    from concourse.bass_utils import run_bass_kernel_spmd as _run

    nc = _bacc.Bacc("TRN2", target_bir_lowering=False, num_devices=1)
    host = {n: inputs[n] for n in ("x", "ctx_512", "L0_attn_W_attn", "L0_attn_b_attn", "L0_attn_W_proj",
                                   "L0_attn_b_proj", "L0_ffn_router_weight", "L0_ffn_down_proj", "L1_attn_bo")}
    host.update(laid_out({k: _np.asarray(v) for k, v in inputs.items()}))
    host = {k: _np.ascontiguousarray(v) for k, v in host.items()}
    host.update(constants())
    arrays, t = {}, {}
    for name, a in host.items():
        arrays[f"in_{name}"] = a
        t[name] = nc.dram_tensor(f"in_{name}", a.shape, _mybir.dt.from_np(a.dtype), kind="ExternalInput").ap()
    out = nc.dram_tensor("out_x", (B, S, D), F32, kind="ExternalOutput").ap()
    program(nc, t, out, None)
    r = _run(nc, [arrays], core_ids=[0])
    return r.results[0]["out_x"]
```

```python
from contextlib import ExitStack

import concourse.bass as bass
from concourse import mybir

F32 = mybir.dt.float32
F32R = mybir.dt.float32r
BF16 = mybir.dt.bfloat16
I32 = mybir.dt.int32
U32 = mybir.dt.uint32
ALU = mybir.AluOpType
ACT = mybir.ActivationFunctionType
AX = mybir.AxisListType

B, S, D = 8, 128, 256
C = 64
KC = D // 128
PAIRS = B // 2
EPS = 1e-5
E0, I0, TOP0, CAP = 64, 96, 8, 128
NSLOT = E0 * CAP
NTOK = B * S
HX, KX, QX, RX = 16, 128, 192, 64
HQ = QX // 2
E1, I1, TOP1 = 16, 176, 4
NF, FH = E1 + 2, I1 // 2
RING = 4


class Chain:

    def __init__(self, eng, sem):
        self.eng, self.sem, self.n = eng, sem, 0

    def turn(self):
        self.eng.sem_clear(self.sem)
        self.n = 0

    def __call__(self, ins):
        self.n += 1
        ins.then_inc(self.sem, 1)
        self.eng.wait_ge(self.sem, self.n)


class Attention:

    def __init__(self, name, strips, dim, shared, causal, biased, scale):
        self.name, self.strips, self.dim, self.shared = name, strips, dim, shared
        self.causal, self.biased, self.scale = causal, biased, scale
        self.width = 128 // strips
        self.heads = 8 * strips
        self.jobs = [(half, row) for half in range(2) for row in range(strips)]
        self.kgroups = 2 if shared else 8
        self.kbanks = -(-self.kgroups // 4)
        self.banks = self.kbanks + 2
        self.bias = 3 * dim
        self.top = self.bias + (2 if biased else 0)
        self.rows = self.top + 2

    def head(self, half, row, g):
        return (self.strips * half + row) * 4 + g if self.shared else 4 * (4 * half + g) + row


L0 = Attention("a0", 4, 8, False, True, True, 8.0 ** -0.5)
X0 = Attention("x0", 4, 8, True, False, True, 8.0 ** -0.5)
L1 = Attention("a1", 2, 16, True, True, False, 16.0 ** -0.5)
XJ = HX // 4


class Phase:

    def __init__(self, sem, base, per):
        self.sem, self.base, self.per = sem, base, per

    def after(self):
        return {n: self.base.get(n, 0) + PAIRS * k for n, k in self.per.items()}

    def wait(self, eng, name, p, k):
        eng.wait_ge(self.sem[name], p * self.per[name] + (self.base.get(name, 0) + k))


PER_A = dict(stats=3, rstd=3, xn=2, xnt_ps=2, xnt_sb=2, qkv_ps=1, qkv_sb=2, kq_ps=L0.banks + X0.banks,
             kq_sb=L0.banks + X0.banks, s_ps=16, s_max=16, top=4, q2_ps=4, q2_sb=4, st_ps=16, st_exp=16, pv_ps=16,
             on_sb=1, ot_ps=1, ot_sb=1, pr_ps=1)
PER_B = dict(stats=3, rstd=3, xn=3, xnt_ps=3, xnt_sb=3, qkv_ps=1, qkv_sb=1, kq_ps=L1.banks, kq_sb=L1.banks,
             s_ps=4 + XJ, s_max=4 + XJ, top=2, q2_ps=2, q2_sb=2, st_ps=4 + XJ, st_exp=4 + XJ, pv_ps=4 + XJ,
             on_sb=1, ot_ps=1, ot_sb=1, pr_ps=2, kv_sb=1, kt_ps=1, kt_sb=1, qb_ps=XJ, rope=XJ, rsum=XJ, qk_ps=XJ, qk_sb=XJ,
             nm_ps=1, nm_sb=1, cn_sb=XJ, ct_ps=2, ct_sb=2)
OFF = {L0: dict(kq=0, s=0, q2=0), X0: dict(kq=L0.banks, s=8, q2=2), L1: dict(kq=0, s=0, q2=0)}


def attention_steps(a):
    half = len(a.jobs) // 2
    return ([("kq", a, n) for n in range(a.banks)]
            + [("s", a, n) for n in range(half)] + [("q2", a, 0)]
            + [("s", a, n) for n in range(half, 2 * half)] + [("q2", a, 1)]
            + [("st", a, n) for n in range(2 * half + 1)])


A_FIRST = [("norm", L0), ("turn", 0), ("qkv", L0), *attention_steps(L0), ("out", 0), ("proj", 0)]
A_SECOND = [("norm", X0), *attention_steps(X0), ("xout",), ("rnorm",), ("turn", 1), ("logits",), ("choose",),
            ("place",), ("weigh",)]
B_FIRST = [("sum",), ("norm", L1), ("turn", 0), ("qkv", L1), *attention_steps(L1), ("out", 0), ("proj", 0),
           ("xnorm",), ("turn", 1), ("queries", 0)]
B_SECOND = [*[("queries", n) for n in range(1, XJ + 1)], *[("xs", n) for n in range(XJ)], ("xmax",),
            *[("xst", n) for n in range(XJ + 1)], ("xct", 0), ("xct", 1), ("xproj",), ("rnorm",), ("turn", 2),
            ("logits",), ("choose",)]


def merged(a, b):
    marks = [((i + 0.5) / len(a), 0, x) for i, x in enumerate(a)] + [((i + 0.5) / len(b), 1, x) for i, x in enumerate(b)]
    return [(which, x) for _, which, x in sorted(marks, key=lambda m: m[:2])]


def two_streams(eng, first, second, do, turn=lambda: None):

    def both(a, sa, pa, b, sb_, pb):
        for which, step in merged(a, b):
            do(*((sa, pa) if which == 0 else (sb_, pb)), *step)

    turn()
    for step in first:
        do(0, 0, *step)
    with eng.Fori(0, PAIRS - 1) as p:
        turn()
        both(second, 0, p, first, 1, p)
        both(first, 0, p + 1, second, 1, p)
    turn()
    both(second, 0, PAIRS - 1, first, 1, PAIRS - 1)
    for step in second:
        do(1, PAIRS - 1, *step)


class Sems(dict):

    def __init__(self, nc, ctx, stage, names):
        self.make = lambda n: ctx.enter_context(nc.semaphore(f"{stage}_{n}"))
        self.names = names.split()

    def __missing__(self, n):
        assert n in self.names, n
        self[n] = self.make(n)
        return self[n]


sems = Sems


ROUTE_SEMS = "lg_ps top ex msk pos_ps idx xn_st scat done"
MOE_SEMS = ("credit xg0 xg1 xg2 xg3 wl0 wl1 wl2 wl3 xt_ps xt_sb h_ps sg a_sb y_ps y_sb yst0 yst1 yst2 yst3 slots")
FFN_SEMS = "credit wl0 wl1 g_ps sg a_sb y_ps y_sb x_new"


def program(nc, t, out, stages):
    with ExitStack() as ctx:
        def sb(name, shape, dt=F32):
            return ctx.enter_context(nc.sbuf_tensor(name, shape, dt))

        bank = [ctx.enter_context(nc.psum_tensor(f"bank{n}", [128, 512], F32)) for n in range(8)]
        PA, PB, PC, PD = ([bank[4 * u + n] for u in range(2)] for n in range(4))

        x = sb("x", [128, B, D])
        ctxt = sb("ctxt", [128, B, C])
        ident = sb("ident", [128, 128])
        identb = sb("identb", [128, 128], BF16)
        maskq = sb("maskq", [128, 128], BF16)
        maskk = sb("maskk", [128, 128], BF16)
        alibi = sb("alibi", [128, 1])
        neghalf = sb("neghalf", [128, 1])
        eps = sb("eps", [128, 1])
        area0 = sb("area0", [128, KC * 3 * D + 3 * D])
        w_qkv0 = area0[:, 0:KC * 3 * D].rearrange("p (c n) -> p c n", c=KC)
        b_qkv0 = area0[:, KC * 3 * D:]
        w_pr0 = sb("w_pr0", [128, KC, D])
        b_pr0 = sb("b_pr0", [128, D])

        def two(name, shape, dt=F32):
            return [sb(f"{name}{u}", shape, dt) for u in range(2)]

        never = sb("never", [128, 128])
        neverT = sb("neverT", [128, 128])
        stats, mv, var, rstd = two("stats", [128, 6]), two("mv", [128, 2]), two("var", [128, 1]), two("rstd", [128, 1])
        xn, xnT = two("xn", [128, D]), two("xnT", [128, KC, 128])
        nmx, nmr = two("nmx", [128, 32]), two("nmr", [128, 32], F32R)
        qarea = two("qarea", [128, 8 * 128])
        qpad = [q[:].rearrange("p (h w) -> p h w", w=32) for q in qarea]
        qpad1 = [q[:].rearrange("p (h w) -> p h w", w=64) for q in qarea]
        qT = two("qT", [128, 8, 128], F32R)
        karea = two("karea", [128, 2 * 8 * 128])
        kpad = [k[:, 0:1024].rearrange("p (h w) -> p h w", w=32) for k in karea]
        kT = two("kT", [128, 8, 128], F32R)
        kpadx, kpad1 = two("kpadx", [128, 8, 32]), two("kpad1", [128, 4, 64])
        qk0 = [k[:, 1024:1536] for k in karea]
        vx, vc, vx1 = two("vx", [128, 32, 9]), two("vc", [128, 8, 9]), two("vx1", [128, 4, 17])
        PT = two("PT", [128, 2, 4, 128])
        rden = two("rden", [128, 32])
        on, onT = two("on", [128, D]), two("onT", [128, KC, 128])
        tmp = on

        w_rt0 = sb("w_rt0", [128, KC, E0])
        tri = sb("tri", [128, 128])
        ones = sb("ones", [128, 128])
        eplus1 = sb("eplus1", [128, E0])
        tokall = sb("tokall", [128, B], I32)
        zrow = sb("zrow", [1, D])
        fillt = sb("fillt", [128, E0], I32)
        lg = sb("lg", [128, E0])
        lg2 = sb("lg2", [128, E0])
        top8 = sb("top8", [128, 8])
        nmax = sb("nmax", [128, 1])
        ex = sb("ex", [128, E0])
        msk = sb("msk", [128, E0])
        macc = sb("macc", [128, E0])
        keep = sb("keep", [128, E0])
        slm = sb("slm", [128, E0])
        s8 = sb("s8", [128, 8])
        zz = sb("zz", [128, 8])
        wk = sb("wk", [128, E0])
        den = sb("den", [128, 1])
        eq = sb("eq", [128, 8, E0])
        w8 = sb("w8", [128, B, 8])
        idx8 = sb("idx8", [128, B, 8], U32)
        idxw = sb("idxw", [128, 8], U32)
        tokw = sb("tokw", [128, 1], I32)
        slots = sb("slots", [128, E0], I32)
        ixe = sb("ixe", [128, RING, 1], U32)
        area1 = sb("area1", [128, RING * D + RING * KC * 2 * I0 + 2 * KC * 128])
        xe = area1[:, 0:RING * D].rearrange("p (r d) -> p r d", r=RING)
        wgu = area1[:, RING * D:RING * (D + KC * 2 * I0)].rearrange("p (r c n) -> p r c n", r=RING, c=KC)
        xeT = area1[:, RING * (D + KC * 2 * I0):].rearrange("p (v c t) -> p v c t", v=2, c=KC)
        wdn = sb("wdn", [I0, RING, D])
        sg = sb("sg", [I0, 2, 128])
        aT = sb("aT", [I0, 2, 128])
        ye = sb("ye", [128, RING, D])
        yg = two("yg", [128, 8, D])
        w8c = sb("w8c", [128, 8])
        w_qkv1 = sb("w_qkv1", [128, KC, 384])
        b_qkv1 = sb("b_qkv1", [128, 384])
        w_pr1 = sb("w_pr1", [128, KC, D])
        b_pr1 = sb("b_pr1", [128, D])
        cos1 = sb("cos1", [128, 16])
        sin1 = sb("sin1", [128, 16])
        qk1, ra1, rb1 = sb("qk1", [128, 320]), sb("ra1", [128, 320]), sb("rb1", [128, 320])
        wqc = sb("wqc", [128, KC, HX * QX])
        wqk = sb("wqk", [HQ, 2, HX, C])
        weff = sb("weff", [128, HX // 2, D])
        cosq = sb("cosq", [HQ, 2, 128])
        sinq = sb("sinq", [HQ, 2, 128])
        cosk = sb("cosk", [128, C])
        sink = sb("sink", [128, C])
        fq, fo = [y[:, 0:2, :] for y in yg], [ye[:, 2 * v:2 * v + 2, :] for v in range(2)]
        fc, fr = [y[:, 2:4, 0:QX] for y in yg], [y[0:RX, 4:6, 0:QX] for y in yg]
        fk, fv = [y[0:RX, 6:8, 0:C] for y in yg], [y[:, 6:8, C:2 * C] for y in yg]
        kvr, ka, kvT = two("kvr", [128, 128]), sb("ka", [128, C]), two("kvT", [C, 128])
        rp = [k[0:HQ, :].rearrange("p (k h t) -> p k h t", k=4, h=4) for k in karea]
        qk2 = two("qk2", [C, 8, 128])

        def qkT(u, n):
            tile = qarea[u][0:C, :].rearrange("p (h t) -> p h t", h=8) if n < 2 else qk2[u][:]
            return tile[:, 4 * (n % 2):4 * (n % 2) + 4, :]

        nmT = two("nmT", [HX, 128])
        cn = [k[:, 0:1024].rearrange("p (h c) -> p h c", c=C) for k in karea]
        cT = [k[:, 1024:2048].rearrange("p (h t) -> p h t", t=128) for k in karea]
        w_rt1 = sb("w_rt1", [128, KC, E1])
        lgp = sb("lgp", [128, E1 + 8])
        lgp2 = sb("lgp2", [128, E1 + 8])
        dw = sb("dw", [128, B, NF])
        dwc = sb("dwc", [128, 2, B])
        xT6 = area0[:, 0:KC * B * 128].rearrange("p (c b t) -> p c b t", c=KC, b=B)
        wf = area1[:, 0:2 * KC * 2 * I1].rearrange("p (v c n) -> p v c n", v=2, c=KC)
        wfd = ye[0:FH, :, :].rearrange("p (v f) d -> p v f d", v=2)
        sgf = cT[0][0:FH, :, :].rearrange("p (f a) t -> p f (a t)", f=2)
        af = cn[0][0:FH, :, :].rearrange("p (f a) t -> p f (a t)", f=2)

        xn3 = nc.dram_tensor("xn3", [NTOK + 1, D], F32).ap()
        table = nc.dram_tensor("table", [NSLOT, 1], I32).ap()
        yrows = nc.dram_tensor("yrows", [NSLOT + 1, D], F32).ap()

        loaded = sems(nc, ctx, "load", "x ctx const w0 w1 fill")
        chains = sems(nc, ctx, "chain", "dve pool act")
        ready = sems(nc, ctx, "ready", "pads masks")
        stream = [sems(nc, ctx, f"s{u}", " ".join({**PER_A, **PER_B})) for u in range(2)]
        SA = [Phase(stream[u], {}, PER_A) for u in range(2)]
        SB = [Phase(stream[u], SA[u].after(), PER_B) for u in range(2)]
        fold = sems(nc, ctx, "fold", "ld0 ld1 ps sb free")
        r0 = sems(nc, ctx, "r0", ROUTE_SEMS)
        m0 = sems(nc, ctx, "m0", MOE_SEMS)
        c0 = sems(nc, ctx, "c0", "credit0 credit1 yg0 yg1")
        r1 = sems(nc, ctx, "r1", ROUTE_SEMS)
        f1 = sems(nc, ctx, "f1", FFN_SEMS)
        stored = ctx.enter_context(nc.semaphore("stored"))

        consts1 = ((tri, "tri"), (ones, "ones"), (eplus1, "eplus1"), (tokall, "tokall"), (cos1, "cos1"),
                   (sin1, "sin1"), (cosq, "cosq"), (sinq, "sinq"), (cosk, "cosk"), (sink, "sink"),
                   )
        N_W0, N_W1 = 5, len(consts1) + 5

        def at(tile, u, p):
            return tile[:, bass.ds(p * 2 + u, 1), :].rearrange("p a d -> p (a d)")

        def xb(b):
            return x[:, bass.ds(b, 1), :].rearrange("p a d -> p (a d)")

        block = ctx.enter_context(nc.Block())

        @block.sync
        def _(sp):
            for dst, src in ((ident[:], "ident"), (never[:], "never"), (neverT[:], "neverT"), (alibi[:], "alibi")):
                sp.dma_start(dst, t[src]).then_inc(loaded["const"], 16)
            sp.dma_start(x[:], t["x"].rearrange("b s d -> s b d")).then_inc(loaded["x"], 16)
            sp.dma_start(w_qkv0, t["L0_attn_W_attn"].rearrange("(c p) n -> p c n", p=128)).then_inc(loaded["w0"], 16)
            sp.dma_start(b_qkv0, t["L0_attn_b_attn"].partition_broadcast(128)).then_inc(loaded["w0"], 16)
            sp.dma_start(w_pr0[:], t["L0_attn_W_proj"].rearrange("(c p) n -> p c n", p=128)).then_inc(loaded["w0"], 16)
            sp.dma_start(b_pr0[:], t["L0_attn_b_proj"].partition_broadcast(128)).then_inc(loaded["w0"], 16)
            sp.dma_start(ctxt[:], t["ctx_512"].rearrange("b s d -> s b d")).then_inc(loaded["ctx"], 16)
            sp.dma_start(w_rt0[:], t["L0_ffn_router_weight"].rearrange("(c p) n -> p c n", p=128)).then_inc(loaded["w0"], 16)
            for dst, src in consts1:
                sp.dma_start(dst[:], t[src]).then_inc(loaded["w1"], 16)
            sp.dma_start(w_qkv1[:], t["w_qkv1"].rearrange("(c p) n -> p c n", p=128)).then_inc(loaded["w1"], 16)
            sp.dma_start(b_qkv1[:], t["b_qkv1"].partition_broadcast(128)).then_inc(loaded["w1"], 16)
            sp.dma_start(w_pr1[:], t["w_o1"].rearrange("(c p) n -> p c n", p=128)).then_inc(loaded["w1"], 16)
            sp.dma_start(b_pr1[:], t["L1_attn_bo"].partition_broadcast(128)).then_inc(loaded["w1"], 16)
            sp.dma_start(w_rt1[:], t["w_rt1"].rearrange("(c p) n -> p c n", p=128)).then_inc(loaded["w1"], 16)
            sp.wait_ge(ready["pads"], 1)
            sp.dma_start(table.rearrange("(p e) a -> p (e a)", e=E0), fillt[:]).then_inc(loaded["fill"], 16)
            sp.dma_start(xn3[NTOK:NTOK + 1, :], zrow[:]).then_inc(loaded["fill"], 16)
            sp.dma_start(yrows[NSLOT:NSLOT + 1, :], zrow[:]).then_inc(loaded["fill"], 16)

            with sp.Fori(0, HX // 4) as hp:
                for v in range(2):
                    sp.wait_ge(fold["free"], hp * 2 + v + 1)
                    for dst, src in ((fq, "wq_x"), (fc, "w_kc_q"), (fr, "w_qr"), (fk, "w_kr"), (fv, "w_kc_kv"), (fo, "wo_x")):
                        sp.dma_start(dst[v], t[src][bass.ds(hp * 2 + v, 1)].rearrange("a p u n -> p (a u) n")) \
                            .then_inc(fold[f"ld{v}"], 16)

            def store_rows(u, p):
                SA[u].wait(sp, "xn", p, 2)
                sp.dma_start(xn3[0:NTOK, :].rearrange("(b p) d -> b p d", p=128)[bass.ds(p * 2 + u, 1)]
                             .rearrange("a p d -> (a p) d"), xn[u][:]).then_inc(r0["xn_st"], 16)

            with sp.Fori(0, PAIRS) as p:
                store_rows(0, p)
                store_rows(1, p)

            sp.wait_ge(r0["scat"], 16 * 8 * B)
            sp.wait_ge(loaded["fill"], 16 * 3)
            sp.dma_start(slots[:], table.rearrange("(p e) a -> p (e a)", e=E0)).then_inc(m0["slots"], 16)
            yv = yrows[0:NSLOT, :].rearrange("(p e) d -> e p d", e=E0)

            def load_expert(u, e):
                sp.dma_start(wgu[:, u, :, :], t["w_gu0"][bass.ds(e, 1)].rearrange("a (c p) n -> p (a c) n", p=128)) \
                    .then_inc(m0[f"wl{u}"], 16)
                sp.dma_start(wdn[:, u, :], t["L0_ffn_down_proj"][bass.ds(e, 1)].rearrange("a p d -> p (a d)")) \
                    .then_inc(m0[f"wl{u}"], 16)

            def store_expert(u, e):
                sp.wait_ge(m0["y_sb"], e + 1)
                sp.dma_start(yv[bass.ds(e, 1)].rearrange("a p d -> (a p) d"), ye[:, u, :]).then_inc(m0[f"yst{u}"], 16)

            for u in range(RING):
                load_expert(u, u)
            with sp.Fori(0, E0 // RING - 1) as i:
                for u in range(RING):
                    store_expert(u, i * RING + u)
                    load_expert(u, i * RING + u + RING)
            for u in range(RING):
                store_expert(u, E0 - RING + u)

            def load_ffn(u, e):
                sp.dma_start(wf[:, u], t["w_gu1"][bass.ds(e, 1)].rearrange("a (c p) n -> p (a c) n", p=128)) \
                    .then_inc(f1[f"wl{u}"], 16)
                sp.dma_start(wfd[:, u], t["w_d1"][bass.ds(e, 1)].rearrange("a (c p) n -> p (a c) n", p=FH)) \
                    .then_inc(f1[f"wl{u}"], 16)

            for u in range(RING):
                sp.wait_ge(m0[f"yst{u}"], 16 * (E0 // RING + 1))
            for u in range(2):
                load_ffn(u, u)
            with sp.Fori(0, NF // 2 - 1) as i:
                for u in range(2):
                    sp.wait_ge(f1["y_ps"], (i * 2 + u + 1) * 8)
                    load_ffn(u, i * 2 + u + 2)
            with sp.Fori(0, B) as b:
                sp.wait_ge(f1["x_new"], 1)
                sp.dma_start(out[bass.ds(b, 1)].rearrange("a p d -> (a p) d"), xb(b)).then_inc(stored, 16)
            sp.wait_ge(stored, 16 * B)

        @block.gpsimd
        def _(pool):
            chain = Chain(pool, chains["pool"])

            def norm_rstd(s, u, p, k):
                s[u].wait(pool, "stats", p, k)
                chain(pool.tensor_tensor(var[u][:], mv[u][:, 1:2], eps[:], ALU.add))
                pool.tensor_tensor(rstd[u][:], var[u][:], neghalf[:], ALU.pow).then_inc(stream[u]["rstd"], 1)

            chain(pool.memset(neghalf[:], -0.5))
            chain(pool.memset(eps[:], EPS))
            pool.wait_ge(loaded["fill"], 16 * 3)
            pool.wait_ge(loaded["w1"], 16 * N_W1)

            def step_a(u, p, what, a=None, n=None):
                if what == "norm":
                    norm_rstd(SA, u, p, 1 if a is L0 else 2)
                elif what == "rnorm":
                    norm_rstd(SA, u, p, 3)
                elif what == "weigh":
                    pool.wait_ge(r0["idx"], p * 2 + u + 1)
                    if not (isinstance(p, int) and p == 0 and u == 0):
                        pool.wait_ge(r0["scat"], (p * 2 + u) * (16 * TOP0))
                    chain(pool.tensor_copy(idxw[:], at(idx8, u, p)))
                    chain(pool.tensor_copy(tokw[:], tokall[:, bass.ds(p * 2 + u, 1)]))
                    for j in range(TOP0):
                        pool.indirect_dma_start(table[:, :], bass.IndirectOffsetOnAxis(idxw[:, j:j + 1], 0), tokw[:, :],
                                                None, bounds_check=NSLOT - 1, oob_is_err=False) \
                            .then_inc(r0["scat"], 16)

            two_streams(pool, A_FIRST, A_SECOND, step_a, chain.turn)

            pool.sem_inc(m0["credit"], RING)
            pool.wait_ge(m0["slots"], 16)
            pool.wait_ge(r0["xn_st"], 16 * B)
            with pool.Fori(0, E0 // RING) as i:
                chain.turn()
                for u in range(RING):
                    pool.wait_ge(m0["credit"], i * RING + u + 1)
                    chain(pool.tensor_copy(ixe[:, u, :], slots[:, bass.ds(i * RING + u, 1)]))
                    pool.indirect_dma_start(xe[:, u, :], None, xn3[:, :],
                                            bass.IndirectOffsetOnAxis(ixe[:, u, :], 0)).then_inc(m0[f"xg{u}"], 16)

            for u in range(RING):
                pool.wait_ge(m0[f"yst{u}"], 16 * (E0 // RING + 1))
            for u in range(2):
                pool.sem_inc(c0[f"credit{u}"], 1)

            def step_b(u, p, what, a=None, n=None):
                if what == "sum":
                    pool.wait_ge(c0[f"credit{u}"], p + 1)
                    if not (isinstance(p, int) and p == 0 and u == 0):
                        pool.wait_ge(c0[f"yg{1 - u}"], (p + u) * (16 * TOP0))
                    chain(pool.tensor_copy(idxw[:], at(idx8, u, p)))
                    for j in range(TOP0):
                        pool.indirect_dma_start(yg[u][:, j, :], None, yrows[:, :],
                                                bass.IndirectOffsetOnAxis(idxw[:, j:j + 1], 0)) \
                            .then_inc(c0[f"yg{u}"], 16)
                elif what == "norm":
                    norm_rstd(SB, u, p, 1)
                elif what == "xnorm":
                    norm_rstd(SB, u, p, 2)
                elif what == "rnorm":
                    norm_rstd(SB, u, p, 3)
                elif what == "queries" and a >= 1:
                    n = a - 1
                    SB[u].wait(pool, "rope", p, n + 1)
                    pool.tensor_tensor(rp[u][:, 0:4:2], rp[u][:, 0:4:2], rp[u][:, 1:4:2], ALU.add) \
                        .then_inc(stream[u]["rsum"], 1)

            two_streams(pool, B_FIRST, B_SECOND, step_b, chain.turn)

        @block.scalar
        def _(act):
            def copy(dst, src):
                return act.activation(dst, src, ACT.Copy)

            def turned(s, u, p, k):
                s[u].wait(act, "xnt_ps", p, k)
                copy(xnT[u][:], PD[u][:, 0:D].rearrange("p (c t) -> p c t", c=KC)).then_inc(stream[u]["xnt_sb"], 1)

            def attention(s, u, p, what, a, n):
                off, sg_ = OFF[a], stream[u]
                if what == "kq":
                    s[u].wait(act, "kq_ps", p, off["kq"] + n + 1)
                    g = min(4, a.kgroups) if n < a.kbanks else 4
                    dst = kT[u][:, 4 * n:4 * n + g, :] if n < a.kbanks else qT[u][:, 4 * (n - a.kbanks):4 * (n - a.kbanks) + 4, :]
                    copy(dst, (PC, PD)[n % 2][u][:, 0:128 * g].rearrange("p (g t) -> p g t", g=g)).then_inc(sg_["kq_sb"], 1)
                elif what == "q2":
                    s[u].wait(act, "q2_ps", p, off["q2"] + n + 1)
                    copy(qT[u][:, 4 * n:4 * n + 4, :], PD[u][:].rearrange("p (g t) -> p g t", g=4)).then_inc(sg_["q2_sb"], 1)
                elif what == "st" and n < len(a.jobs):
                    s[u].wait(act, "st_ps", p, off["s"] + n + 1)
                    if n >= 2:
                        s[u].wait(act, "pv_ps", p, off["s"] + n - 1)
                    act.activation(PT[u][:, n % 2], (PA, PB)[n % 2][u][:].rearrange("p (g t) -> p g t", g=4), ACT.Exp,
                                   scale=a.scale).then_inc(sg_["st_exp"], 1)

            def out_turned(s, u, p):
                s[u].wait(act, "ot_ps", p, 1)
                copy(onT[u][:], PD[u][:, 0:D].rearrange("p (c t) -> p c t", c=KC)).then_inc(stream[u]["ot_sb"], 1)

            chain = Chain(act, chains["act"])
            with act.Fori(0, HX // 2) as hp:
                for u in range(2):
                    act.wait_ge(fold["ps"], hp * 2 + u + 1)
                    copy(wqc[:, :, bass.ds(hp * (2 * QX) + u * QX, QX)],
                         bank[3 * u][:, 0:2 * QX].rearrange("p (c n) -> p c n", c=KC))
                    copy(wqk[:, :, bass.ds(hp * 2 + u, 1), :].rearrange("p f a c -> p f (a c)"),
                         bank[3 * u + 1][0:HQ, 0:2 * C].rearrange("p (f c) -> p f c", f=2))
                    copy(weff[64 * u:64 * u + 64, bass.ds(hp, 1), :].rearrange("p a d -> p (a d)"),
                         bank[3 * u + 2][64 * u:64 * u + 64, 0:D]).then_inc(fold["sb"], 1)

            def step_a(u, p, what, a=None, n=None):
                if what == "turn":
                    turned(SA, u, p, a + 1)
                elif what in ("kq", "q2", "st"):
                    attention(SA, u, p, what, a, n)
                elif what == "out":
                    out_turned(SA, u, p)
                elif what == "choose":
                    act.wait_ge(r0["top"], p * 2 + u + 1)
                    act.activation(ex[:], lg[:], ACT.Exp, bias=nmax[:]).then_inc(r0["ex"], 1)

            two_streams(act, A_FIRST, A_SECOND, step_a)

            def turned_expert(e, u):
                act.wait_ge(m0["xt_ps"], e + 1)
                copy(xeT[:, u % 2], bank[6 + u % 2][:, 0:D].rearrange("p (c t) -> p c t", c=KC)).then_inc(m0["xt_sb"], 1)

            def gate_expert(e, u):
                act.wait_ge(m0["h_ps"], e + 1)
                act.activation(sg[:, u % 2, :], bank[u % 2][0:I0, 0:128], ACT.Silu).then_inc(m0["sg"], 1)

            turned_expert(0, 0)
            with act.Fori(0, E0 // RING - 1) as i:
                for u in range(RING):
                    turned_expert(i * RING + u + 1, u + 1)
                    gate_expert(i * RING + u, u)
            for u in range(RING):
                if u < RING - 1:
                    turned_expert(E0 - RING + u + 1, u + 1)
                gate_expert(E0 - RING + u, u)

            def step_b(u, p, what, a=None, n=None):
                sg_, s = stream[u], SB[u]
                if what == "turn":
                    if a == 2:
                        s.wait(act, "xnt_ps", p, 3)
                        copy(xT6[:, :, bass.ds(p * 2 + u, 1), :].rearrange("p c a t -> p c (a t)"),
                             PD[u][:, 0:D].rearrange("p (c t) -> p c t", c=KC))
                    turned(SB, u, p, a + 1)
                    if a == 1:
                        s.wait(act, "kt_ps", p, 1)
                        copy(kvT[u][:], PC[u][0:C, 0:128]).then_inc(sg_["kt_sb"], 1)
                elif what in ("kq", "q2", "st"):
                    attention(SB, u, p, what, a, n)
                elif what == "out":
                    out_turned(SB, u, p)
                elif what == "queries" and a >= 1:
                    n = a - 1
                    s.wait(act, "qk_ps", p, n + 1)
                    copy(qkT(u, n), (PC, PD)[n % 2][u][0:C, :].rearrange("p (h t) -> p h t", h=4)) \
                        .then_inc(sg_["qk_sb"], 1)
                elif what == "xmax":
                    s.wait(act, "nm_ps", p, 1)
                    copy(nmT[u][:], PD[u][0:HX, 0:128]).then_inc(sg_["nm_sb"], 1)
                elif what == "xst" and a < XJ:
                    n = a
                    s.wait(act, "st_ps", p, 4 + n + 1)
                    if n >= 2:
                        s.wait(act, "pv_ps", p, 4 + n - 1)
                    act.activation(PT[u][:, n % 2], (PA, PB)[n % 2][u][:].rearrange("p (g t) -> p g t", g=4), ACT.Exp) \
                        .then_inc(sg_["st_exp"], 1)
                elif what == "xct":
                    n = a
                    s.wait(act, "ct_ps", p, n + 1)
                    copy(cT[u][:, 4 * n:4 * n + 4, :], (PC, PD)[n][u][:].rearrange("p (h t) -> p h t", h=4)) \
                        .then_inc(sg_["ct_sb"], 1)
                elif what == "choose":
                    act.wait_ge(r1["top"], p * 2 + u + 1)
                    act.activation(ex[:, 0:E1], lgp[:, 0:E1], ACT.Exp, bias=nmax[:]).then_inc(r1["ex"], 1)

            two_streams(act, B_FIRST, B_SECOND, step_b)

            with act.Fori(0, NF // 2) as i:
                for u in range(2):
                    for th in range(2):
                        for f in range(2):
                            act.wait_ge(f1["g_ps"], i * 8 + u * 4 + th * 2 + f + 1)
                            act.activation(sgf[:, f, :], bank[2 * f][0:FH, :], ACT.Silu).then_inc(f1["sg"], 1)

        @block.tensor
        def _(pe):
            def norm_turn(s, u, p, k):
                s[u].wait(pe, "xn", p, k)
                for c in range(KC):
                    last = pe.transpose(PD[u][:, 128 * c:128 * c + 128], xn[u][:, 128 * c:128 * c + 128], ident[:])
                last.then_inc(stream[u]["xnt_ps"], 1)

            def rows_times(dst, lhs, w, lo, n):
                for c in range(KC):
                    last = pe.matmul(dst, lhs[:, c, :], w[:, c, lo:lo + n], start=(c == 0), stop=(c == KC - 1))
                return last

            def attention(s, u, p, what, a, n, queries, keys, values):
                off, sg_, s = OFF[a], stream[u], s[u]
                kflat = keys.rearrange("p (g r) c -> p g (r c)", r=a.strips)
                qflat = queries.rearrange("p (g r) c -> p g (r c)", r=a.strips)
                jobs = len(a.jobs)
                if what == "kq":
                    if n == 0:
                        s.wait(pe, "qkv_sb", p, 2 if a is X0 else 1)
                    if n >= 2:
                        s.wait(pe, "kq_sb", p, off["kq"] + n - 1)
                    src, g0, g = (kflat, 4 * n, min(4, a.kgroups)) if n < a.kbanks else (qflat, 4 * (n - a.kbanks), 4)
                    for g1 in range(g):
                        last = pe.transpose((PC, PD)[n % 2][u][:, 128 * g1:128 * g1 + 128], src[:, g0 + g1, :], ident[:])
                    last.then_inc(sg_["kq_ps"], 1)
                elif what == "s":
                    half, row = a.jobs[n]
                    lo, hi = a.width * row, a.width * row + a.top
                    if n == 0:
                        s.wait(pe, "kq_sb", p, off["kq"] + a.banks)
                    if n >= 2:
                        s.wait(pe, "s_max", p, off["s"] + n - 1)
                    dst = (PA, PB)[n % 2][u]
                    if a.causal:
                        pe.matmul(dst[:].rearrange("p (g t) -> p g t", g=4), identb[:],
                                  maskq[:].unsqueeze(1).broadcast_to([128, 4, 128]), start=True, stop=True,
                                  skip_group_check=True)
                    for g in range(4):
                        kg = half if a.shared else 4 * half + g
                        last = pe.matmul(dst[:, 128 * g:128 * g + 128], qT[u][lo:hi, 4 * half + g, :], kT[u][lo:hi, kg, :],
                                         start=not a.causal, stop=True, skip_group_check=True)
                    last.then_inc(sg_["s_ps"], 1)
                elif what == "q2":
                    s.wait(pe, "top", p, off["q2"] + n + 1)
                    if n == 1:
                        s.wait(pe, "q2_sb", p, off["q2"] + 1)
                    for g in range(4):
                        last = pe.transpose(PD[u][:, 128 * g:128 * g + 128], qflat[:, 4 * n + g, :], ident[:])
                    last.then_inc(sg_["q2_ps"], 1)
                else:
                    if n < jobs:
                        half, row = a.jobs[n]
                        lo, hi = a.width * row, a.width * row + a.rows
                        if row == 0:
                            s.wait(pe, "q2_sb", p, off["q2"] + half + 1)
                        if n < 2:
                            s.wait(pe, "s_max", p, off["s"] + jobs - 1 + n)
                        else:
                            s.wait(pe, "st_exp", p, off["s"] + n - 1)
                        dst = (PA, PB)[n % 2][u]
                        if a.causal:
                            pe.matmul(dst[:].rearrange("p (g t) -> p g t", g=4), identb[:],
                                      maskk[:].unsqueeze(1).broadcast_to([128, 4, 128]), start=True, stop=True,
                                      skip_group_check=True)
                        if a.shared:
                            last = pe.matmul(dst[:].rearrange("p (g t) -> p g t", g=4), kT[u][lo:hi, half, :],
                                             qT[u][lo:hi, 4 * half:4 * half + 4, :], start=not a.causal, stop=True,
                                             skip_group_check=True)
                        else:
                            for g in range(4):
                                last = pe.matmul(dst[:, 128 * g:128 * g + 128], kT[u][lo:hi, 4 * half + g, :],
                                                 qT[u][lo:hi, 4 * half + g, :], start=not a.causal, stop=True,
                                                 skip_group_check=True)
                        last.then_inc(sg_["st_ps"], 1)
                    if n >= 1:
                        n = n - 1
                        half, row = a.jobs[n]
                        w = a.dim + 1
                        s.wait(pe, "st_exp", p, off["s"] + n + 1)
                        for g in range(4):
                            h = a.head(half, row, g)
                            kv = h // 4 if a.shared else h
                            last = pe.matmul(PC[u][:, w * h:w * h + w], PT[u][:, n % 2, g, :], values[:, kv, :],
                                             start=True, stop=True, skip_group_check=True)
                        last.then_inc(sg_["pv_ps"], 1)

            def out_turn(s, u, p):
                s[u].wait(pe, "on_sb", p, 1)
                for c in range(KC):
                    last = pe.transpose(PD[u][:, 128 * c:128 * c + 128], on[u][:, 128 * c:128 * c + 128], ident[:])
                last.then_inc(stream[u]["ot_ps"], 1)

            def project(s, u, p, w):
                s[u].wait(pe, "ot_sb", p, 1)
                rows_times(PA[u][:, 0:D], onT[u], w, 0, D).then_inc(stream[u]["pr_ps"], 1)

            pe.wait_ge(loaded["const"], 16 * 4)
            pe.wait_ge(ready["masks"], 3)
            pe.wait_ge(loaded["w0"], 16 * N_W0)
            pe.wait_ge(loaded["w1"], 16 * N_W1)
            pe.sem_inc(fold["free"], 2)

            def fold_pair(hp, v, turn):
                pe.wait_ge(fold[f"ld{v}"], turn * 96 + 96)
                for u in range(2):
                    if not (isinstance(hp, int) and hp == 0):
                        pe.wait_ge(fold["sb"], hp * 2 + u - 1)
                    for c in range(KC):
                        pe.matmul(bank[3 * u][:, QX * c:QX * c + QX], fq[v][:, u, 128 * c:128 * c + 128], fc[v][:, u, :],
                                  start=True, stop=True)
                    for half in range(2):
                        pe.matmul(bank[3 * u + 1][0:HQ, C * half:C * half + C], fr[v][:, u, HQ * half:HQ * half + HQ],
                                  fk[v][:, u, :], start=True, stop=True)
                    last = pe.matmul(bank[3 * u + 2][64 * u:64 * u + 64, 0:D], fv[v][:, u, :], fo[v][:, u, :],
                                     start=True, stop=True)
                    last.then_inc(fold["ps"], 1)
                pe.wait_ge(fold["ps"], hp * 2 + 2)
                pe.sem_inc(fold["free"], 1)

            for v in range(2):
                fold_pair(v, v, 0)
            with pe.Fori(1, HX // 4) as i:
                for v in range(2):
                    fold_pair(i * 2 + v, v, i)
            pe.wait_ge(fold["sb"], HX)

            def step_a(u, p, what, a=None, n=None):
                if what == "turn":
                    norm_turn(SA, u, p, a + 1)
                elif what == "qkv":
                    SA[u].wait(pe, "xnt_sb", p, 1)
                    rows_times(PA[u][:], xnT[u], w_qkv0, 0, 2 * D)
                    rows_times(PB[u][:, 0:D], xnT[u], w_qkv0, 2 * D, D).then_inc(stream[u]["qkv_ps"], 1)
                elif what in ("kq", "s", "q2", "st"):
                    attention(SA, u, p, what, a, n, qpad[u], kpad[u] if a is L0 else kpadx[u][:],
                              vx[u] if a is L0 else vc[u])
                elif what == "out":
                    out_turn(SA, u, p)
                elif what == "proj":
                    project(SA, u, p, w_pr0)
                elif what == "logits":
                    SA[u].wait(pe, "xnt_sb", p, 2)
                    rows_times(PA[u][:, 0:E0], xnT[u], w_rt0, 0, E0).then_inc(r0["lg_ps"], 1)
                elif what == "place":
                    pe.wait_ge(r0["msk"], p * 2 + u + 1)
                    pe.matmul(PB[u][:, 0:E0], tri[:], msk[:], start=True, stop=False)
                    pe.matmul(PB[u][:, 0:E0], ones[:], macc[:], start=False, stop=True).then_inc(r0["pos_ps"], 1)

            two_streams(pe, A_FIRST, A_SECOND, step_a)

            def turn_expert(e, u, i):
                v = u % 2
                pe.wait_ge(m0[f"xg{u % RING}"], (i + u // RING) * 16 + 16)
                if not (isinstance(e, int) and e < 2):
                    pe.wait_ge(m0["xt_sb"], e - 1)
                for c in range(KC):
                    last = pe.transpose(bank[6 + v][:, 128 * c:128 * c + 128], xe[:, u % RING, 128 * c:128 * c + 128], ident[:])
                last.then_inc(m0["xt_ps"], 1)

            def inner(e, u, i):
                v = u % 2
                pe.wait_ge(m0["xt_sb"], e + 1)
                pe.sem_inc(m0["credit"], 1)
                pe.wait_ge(m0[f"wl{u}"], i * 32 + 32)
                for k in range(2):
                    for c in range(KC):
                        last = pe.matmul(bank[v][0:I0, 128 * k:128 * k + 128], wgu[:, u, c, I0 * k:I0 * k + I0],
                                         xeT[:, v, c, :], start=(c == 0), stop=(c == KC - 1))
                last.then_inc(m0["h_ps"], 1)

            def outer(e, u):
                pe.wait_ge(m0["a_sb"], e + 1)
                if not (isinstance(e, int) and e < 2):
                    pe.wait_ge(m0["y_sb"], e - 1)
                pe.matmul(bank[2 + u % 2][:, 0:D], aT[:, u % 2, :], wdn[:, u % RING, :], start=True, stop=True) \
                    .then_inc(m0["y_ps"], 1)

            def experts(i):
                for u in range(RING):
                    first, last = isinstance(i, int) and i == 0, isinstance(i, int) and i == E0 // RING - 1
                    e = i * RING + u
                    if not (last and u == RING - 1):
                        turn_expert(e + 1, u + 1, i)
                    inner(e, u, i)
                    if not (first and u == 0):
                        outer(e - 1, (u - 1) % RING)

            turn_expert(0, 0, 0)
            experts(0)
            with pe.Fori(1, E0 // RING - 1) as i:
                experts(i)
            experts(E0 // RING - 1)
            outer(E0 - 1, RING - 1)

            def step_b(u, p, what, a=None, n=None):
                s, sg_ = SB[u], stream[u]
                if what == "turn":
                    norm_turn(SB, u, p, a + 1)
                    if a == 1:
                        s.wait(pe, "kv_sb", p, 1)
                        pe.transpose(PC[u][:, 0:128], kvr[u][:], ident[:]).then_inc(sg_["kt_ps"], 1)
                elif what == "qkv":
                    s.wait(pe, "xnt_sb", p, 1)
                    rows_times(PA[u][:, 0:384], xnT[u], w_qkv1, 0, 384).then_inc(sg_["qkv_ps"], 1)
                elif what in ("kq", "s", "q2", "st"):
                    attention(SB, u, p, what, a, n, qpad1[u], kpad1[u][:], vx1[u])
                elif what == "out":
                    out_turn(SB, u, p)
                elif what == "proj":
                    project(SB, u, p, w_pr1)
                elif what == "queries":
                    if a >= 1:
                        n = a - 1
                        s.wait(pe, "rsum", p, n + 1)
                        if n == 0:
                            s.wait(pe, "kt_sb", p, 1)
                        if n >= 2:
                            s.wait(pe, "qk_sb", p, n - 1)
                        for h in range(4):
                            for k in range(2):
                                last = pe.matmul((PC, PD)[n % 2][u][0:C, 128 * h:128 * h + 128], wqk[:, k, 4 * n + h, :],
                                                 rp[u][:, 2 * k, h, :], start=(k == 0), stop=(k == 1))
                        last.then_inc(sg_["qk_ps"], 1)
                    if a < XJ:
                        n = a
                        if n == 0:
                            s.wait(pe, "xnt_sb", p, 2)
                        else:
                            s.wait(pe, "rope", p, n)
                        for half in range(2):
                            for h in range(4):
                                lo = (4 * n + h) * QX + half * HQ
                                for c in range(KC):
                                    last = pe.matmul((PA, PB)[half][u][0:HQ, 128 * h:128 * h + 128],
                                                     wqc[:, c, lo:lo + HQ], xnT[u][:, c, :], start=(c == 0), stop=(c == KC - 1))
                        last.then_inc(sg_["qb_ps"], 1)
                elif what == "xs":
                    n = a
                    s.wait(pe, "qk_sb", p, n + 1)
                    if n >= 2:
                        s.wait(pe, "s_max", p, 4 + n - 1)
                    elif n == 0:
                        s.wait(pe, "rope", p, XJ)
                    for h in range(4):
                        last = pe.matmul((PA, PB)[n % 2][u][:, 128 * h:128 * h + 128], qkT(u, n)[:, h, :], kvT[u][:],
                                         start=True, stop=True)
                    last.then_inc(sg_["s_ps"], 1)
                elif what == "xmax":
                    s.wait(pe, "s_max", p, 4 + XJ)
                    pe.transpose(PD[u][0:HX, 0:128], nmx[u][:, 0:HX], ident[:]).then_inc(sg_["nm_ps"], 1)
                elif what == "xst":
                    if a < XJ:
                        n = a
                        if n == 0:
                            s.wait(pe, "nm_sb", p, 1)
                        if n >= 2:
                            s.wait(pe, "st_exp", p, 4 + n - 1)
                        dst = (PA, PB)[n % 2][u]
                        pe.matmul(dst[:].rearrange("p (g t) -> p g t", g=4), kvT[u][:], qkT(u, n),
                                  start=True, stop=True, skip_group_check=True)
                        for h in range(4):
                            last = pe.matmul(dst[:, 128 * h:128 * h + 128], ident[0:HX, 4 * n + h:4 * n + h + 1].broadcast_to([HX, 128]), nmT[u][:],
                                             start=False, stop=True, skip_group_check=True)
                        last.then_inc(sg_["st_ps"], 1)
                    if a >= 1:
                        n = a - 1
                        s.wait(pe, "st_exp", p, 4 + n + 1)
                        if n >= 2:
                            s.wait(pe, "cn_sb", p, n - 1)
                        for h in range(4):
                            last = pe.matmul((PC, PD)[n % 2][u][:, (C + 1) * h:(C + 1) * (h + 1)], PT[u][:, n % 2, h, :],
                                             kvr[u][:, 0:C + 1], start=True, stop=True)
                        last.then_inc(sg_["pv_ps"], 1)
                elif what == "xct":
                    n = a
                    s.wait(pe, "cn_sb", p, XJ)
                    for h in range(4):
                        last = pe.transpose((PC, PD)[n][u][:, 128 * h:128 * h + 128],
                                            cn[u][:, 8 * n + 2 * h:8 * n + 2 * h + 2, :].rearrange("p h c -> p (h c)"), ident[:])
                    last.then_inc(sg_["ct_ps"], 1)
                elif what == "xproj":
                    s.wait(pe, "ct_sb", p, 2)
                    for n in range(HX // 2):
                        last = pe.matmul(PA[u][:, 0:D], cT[u][:, n, :], weff[:, n, :], start=(n == 0), stop=(n == HX // 2 - 1))
                    last.then_inc(sg_["pr_ps"], 1)
                elif what == "logits":
                    s.wait(pe, "xnt_sb", p, 3)
                    rows_times(PB[u][:, 0:E1], xnT[u], w_rt1, 0, E1).then_inc(r1["lg_ps"], 1)

            two_streams(pe, B_FIRST, B_SECOND, step_b)

            pe.wait_ge(r1["done"], B)
            pe.sem_inc(f1["credit"], 1)
            with pe.Fori(0, NF // 2) as i:
                for u in range(2):
                    pe.wait_ge(f1[f"wl{u}"], (i + 1) * 32)
                    for th in range(2):
                        step = i * 4 + u * 2 + th
                        pe.wait_ge(f1["credit"], step + 1)
                        for f in range(2):
                            for k in range(2):
                                for c in range(KC):
                                    last = pe.matmul(bank[2 * f + k][0:FH, :], wf[:, u, c, I1 * k + FH * f:I1 * k + FH * f + FH],
                                                     xT6[:, c, 4 * th:4 * th + 4, :].rearrange("p b t -> p (b t)"),
                                                     start=(c == 0), stop=(c == KC - 1))
                            last.then_inc(f1["g_ps"], 1)
                        pe.wait_ge(f1["a_sb"], (step + 1) * 2)
                        for q in range(4):
                            if q >= 2:
                                pe.wait_ge(f1["y_sb"], step * 4 + q - 1)
                            for f in range(2):
                                last = pe.matmul(bank[4 + q % 2][:, 0:D], af[:, f, 128 * q:128 * q + 128], wfd[:, u, f, :],
                                                 start=(f == 0), stop=(f == 1))
                            last.then_inc(f1["y_ps"], 1)

        @block.vector
        def _(dve):
            chain = Chain(dve, chains["dve"])

            def norm(s, u, p, k):
                chain(dve.bn_stats(stats[u][:], at(x, u, p)))
                dve.bn_aggr(mv[u][:], stats[u][:]).then_inc(stream[u]["stats"], 1)
                s[u].wait(dve, "rstd", p, k)
                return (at(x, u, p), mv[u][:, 0:1], rstd[u][:], ALU.subtract, ALU.mult)

            def split(dst, src, dim, heads, highs, low, last_sem=None):
                step = highs[1] - highs[0]
                for at_ in highs:
                    high = dve.tensor_copy(dst[:, :, at_:at_ + dim].bitcast(F32R), src)
                chain(high)
                return dve.tensor_tensor(dst[:, :, low:low + dim], src, dst[:, :, highs[0]:highs[0] + dim], ALU.subtract)

            def maxima(s, u, p, a, n):
                half, row = a.jobs[n]
                off, w = OFF[a], a.strips
                nm = nmx[u][:, 0:8 * w].rearrange("p (g r) -> p g r", r=w)
                s[u].wait(dve, "s_ps", p, off["s"] + n + 1)
                m = dve.tensor_reduce(nm[:, 4 * half:4 * half + 4, row],
                                      (PA, PB)[n % 2][u][:].rearrange("p (g t) -> p g t", g=4), AX.X, ALU.max,
                                      negate=True)
                m.then_inc(stream[u]["s_max"], 1)
                if row == w - 1:
                    s[u].wait(dve, "s_max", p, off["s"] + n + 1)
                    q = (qpad1 if a is L1 else qpad)[u][:, 4 * w * half:4 * w * (half + 1), :]
                    m = nmx[u][:, 4 * w * half:4 * w * (half + 1)]
                    chain(dve.tensor_copy(q[:, :, a.top].bitcast(F32R), m))
                    dve.tensor_tensor(q[:, :, a.top + 1], m, q[:, :, a.top], ALU.subtract) \
                        .then_inc(stream[u]["top"], 1)

            def weighted(s, u, p, a, dst):
                w = a.dim + 1
                pv = PC[u][:, 0:w * a.heads].rearrange("p (h w) -> p h w", w=w)
                s[u].wait(dve, "pv_ps", p, OFF[a]["s"] + len(a.jobs))
                chain(dve.reciprocal(rden[u][:, 0:a.heads], pv[:, :, a.dim]))
                return dve.tensor_tensor(dst.rearrange("p (h d) -> p h d", d=a.dim), pv[:, :, 0:a.dim],
                                         rden[u][:, 0:a.heads].unsqueeze(2).broadcast_to([128, a.heads, a.dim]),
                                         ALU.mult)

            dve.wait_ge(loaded["const"], 16 * 4)
            for dst, src in ((identb, ident), (maskq, never), (maskk, neverT)):
                dve.tensor_copy(dst[:], src[:]).then_inc(ready["masks"], 1)
            for tile in (*qarea, *karea, *kpadx, *kpad1, *vx, *vc, zrow, macc, *kvr):
                chain(dve.memset(tile[:], 0.0))
            for u in range(2):
                chain(dve.memset(qpad[u][:, :, L0.bias:L0.bias + 2], 1.0))
                chain(dve.memset(kpad[u][:, :, L0.top:L0.top + 2], 1.0))
                chain(dve.memset(kpadx[u][:, :, X0.top:X0.top + 2], 1.0))
                chain(dve.memset(kpad1[u][:, :, L1.top:L1.top + 2], 1.0))
                ah, al = kpad[u][:, :, L0.bias], kpad[u][:, :, L0.bias + 1]
                chain(dve.tensor_copy(ah.bitcast(F32R), alibi[:].broadcast_to([128, 32])))
                chain(dve.tensor_tensor(al, alibi[:].broadcast_to([128, 32]), ah, ALU.subtract))
                chain(dve.memset(vx[u][:, :, 8:9], 1.0))
                chain(dve.memset(vc[u][:, :, 8:9], 1.0))
                chain(dve.memset(vx1[u][:, :, 16:17], 1.0))
                chain(dve.memset(kvr[u][:, C:C + 1], 1.0))
            chain(dve.memset(dw[:, :, E1:NF], 1.0))
            chain(dve.memset(lgp[:, E1:E1 + 8], -3e38))
            dve.memset(fillt[:], NTOK).then_inc(ready["pads"], 1)
            dve.wait_ge(ready["pads"], 1)
            dve.wait_ge(loaded["w1"], 16 * N_W1)
            dve.wait_ge(loaded["x"], 16)
            dve.wait_ge(loaded["ctx"], 16)
            dve.wait_ge(loaded["w0"], 16 * N_W0)

            def heads(ap, dim):
                return ap.rearrange("p (h c) -> p h c", c=dim)

            def step_a(u, p, what, a=None, n=None):
                s = SA
                if what == "norm" and a is L0:
                    ln = norm(s, u, p, 1)
                    dve.tensor_scalar(xn[u][:], *ln).then_inc(stream[u]["xn"], 1)
                elif what == "qkv":
                    s[u].wait(dve, "qkv_ps", p, 1)
                    chain(dve.tensor_tensor(qk0[u], PA[u][:], b_qkv0[:, 0:2 * D], ALU.add))
                    dve.tensor_tensor(vx[u][:, :, 0:8], heads(PB[u][:, 0:D], 8), heads(b_qkv0[:, 2 * D:3 * D], 8), ALU.add)
                    chain(split(kpad[u], heads(qk0[u][:, D:2 * D], 8), 8, 32, (0, 16), 8))
                    split(qpad[u], heads(qk0[u][:, 0:D], 8), 8, 32, (0, 8), 16).then_inc(stream[u]["qkv_sb"], 1)
                elif what == "s":
                    maxima(s, u, p, a, n)
                elif what == "out":
                    weighted(s, u, p, a=L0, dst=on[u][:]).then_inc(stream[u]["on_sb"], 1)
                elif what == "proj":
                    s[u].wait(dve, "pr_ps", p, 1)
                    chain(dve.tensor_tensor(tmp[u][:], PA[u][:, 0:D], b_pr0[:], ALU.add))
                    chain(dve.tensor_tensor(at(x, u, p), at(x, u, p), tmp[u][:], ALU.add))
                elif what == "norm":
                    cb = heads(at(ctxt, u, p), 8)
                    chain(split(kpadx[u], cb, 8, 8, (0, 16), 8))
                    chain(dve.tensor_copy(vc[u][:, :, 0:8], cb))
                    chain(dve.tensor_scalar(xn[u][:], *norm(s, u, p, 2)))
                    xv = xn[u][:].rearrange("p (h r g c) -> p h r g c", h=2, r=4, g=4)
                    qv = qpad[u].rearrange("p (h g r) c -> p h g r c", h=2, g=4)
                    for half in range(2):
                        src, dst = xv[:, half].rearrange("p r g c -> p g r c"), qv[:, half]
                        dve.tensor_copy(dst[:, :, :, 0:8].bitcast(F32R), src)
                        chain(dve.tensor_copy(dst[:, :, :, 8:16].bitcast(F32R), src))
                        last = dve.tensor_tensor(dst[:, :, :, 16:24], src, dst[:, :, :, 0:8], ALU.subtract)
                    last.then_inc(stream[u]["qkv_sb"], 1)
                elif what == "xout":
                    chain(weighted(s, u, p, X0, tmp[u][:]))
                    chain(dve.tensor_tensor(at(x, u, p), at(x, u, p), tmp[u][:], ALU.add))
                elif what == "rnorm":
                    dve.tensor_scalar(xn[u][:], *norm(s, u, p, 3)).then_inc(stream[u]["xn"], 1)
                elif what == "choose":
                    dve.wait_ge(r0["lg_ps"], p * 2 + u + 1)
                    chain(dve.tensor_copy(lg[:], PA[u][:, 0:E0]))
                    chain(dve.max(top8[:], lg[:]))
                    dve.tensor_scalar(nmax[:], top8[:, 0:1], -1.0, None, ALU.mult).then_inc(r0["top"], 1)
                    chain(dve.match_replace(lg2[:], top8[:], lg[:], -3e38))
                    dve.tensor_tensor(msk[:], lg[:], lg2[:], ALU.not_equal).then_inc(r0["msk"], 1)
                elif what == "weigh":
                    dve.wait_ge(r0["msk"], p * 2 + u + 1)
                    dve.wait_ge(r0["ex"], p * 2 + u + 1)
                    chain(dve.tensor_tensor(wk[:], ex[:], msk[:], ALU.mult))
                    chain(dve.tensor_reduce(den[:], wk[:], AX.X, ALU.add))
                    chain(dve.reciprocal(den[:], den[:]))
                    dve.wait_ge(r0["pos_ps"], p * 2 + u + 1)
                    chain(dve.scalar_tensor_tensor(keep[:], PB[u][:, 0:E0], float(CAP), msk[:], ALU.is_lt, ALU.mult))
                    chain(dve.scalar_tensor_tensor(slm[:], PB[u][:, 0:E0], float(E0), eplus1[:], ALU.mult, ALU.add))
                    chain(dve.tensor_tensor(slm[:], slm[:], keep[:], ALU.mult))
                    chain(dve.max(s8[:], slm[:]))
                    chain(dve.tensor_scalar(zz[:], s8[:], 0.0, float(NSLOT + 1), ALU.is_equal, ALU.mult))
                    dve.scalar_tensor_tensor(at(idx8, u, p), s8[:], -1.0, zz[:], ALU.add, ALU.add).then_inc(r0["idx"], 1)
                    chain(dve.scalar_tensor_tensor(wk[:], wk[:], den[:], keep[:], ALU.mult, ALU.mult))
                    chain(dve.tensor_tensor(eq[:], slm[:].unsqueeze(1).broadcast_to([128, 8, E0]),
                                            s8[:].unsqueeze(2).broadcast_to([128, 8, E0]), ALU.is_equal))
                    chain(dve.tensor_tensor(eq[:], eq[:], wk[:].unsqueeze(1).broadcast_to([128, 8, E0]), ALU.mult))
                    chain(dve.tensor_reduce(at(w8, u, p), eq[:], AX.X, ALU.add))
                    chain(dve.tensor_tensor(macc[:], macc[:], msk[:], ALU.add))
                    dve.wait_ge(r0["xn_st"], (p * 2 + u + 1) * 16)

            two_streams(dve, A_FIRST, A_SECOND, step_a, chain.turn)

            for u in range(RING):
                dve.sem_inc(m0[f"yst{u}"], 16)

            def gated(e, u):
                dve.wait_ge(m0["sg"], e + 1)
                dve.tensor_tensor(aT[:, u % 2, :], sg[:, u % 2, :], bank[u % 2][0:I0, 128:256], ALU.mult) \
                    .then_inc(m0["a_sb"], 1)

            def result(e, u, i):
                dve.wait_ge(m0["y_ps"], e + 1)
                dve.wait_ge(m0[f"yst{u}"], i * 16 + 16)
                dve.tensor_copy(ye[:, u, :], bank[2 + u % 2][:, 0:D]).then_inc(m0["y_sb"], 1)

            for u in range(RING):
                gated(u, u)
                if u >= 1:
                    result(u - 1, u - 1, 0)
            with dve.Fori(1, E0 // RING) as i:
                for u in range(RING):
                    e = i * RING + u
                    gated(e, u)
                    result(e - 1, (u - 1) % RING, i if u >= 1 else i - 1)
            result(E0 - 1, RING - 1, E0 // RING - 1)

            def step_b(u, p, what, a=None, n=None):
                s, sg_ = SB, stream[u]
                if what == "sum":
                    chain(dve.tensor_copy(w8c[:], at(w8, u, p)))
                    dve.wait_ge(c0[f"yg{u}"], (p + 1) * (16 * TOP0))
                    for j in range(TOP0):
                        chain(dve.scalar_tensor_tensor(at(x, u, p), yg[u][:, j, :], w8c[:, j:j + 1], at(x, u, p), ALU.mult,
                                                       ALU.add))
                    dve.sem_inc(c0[f"credit{u}"], 1)
                elif what == "norm":
                    dve.tensor_scalar(xn[u][:], *norm(s, u, p, 1)).then_inc(sg_["xn"], 1)
                elif what == "qkv":
                    s[u].wait(dve, "qkv_ps", p, 1)
                    chain(dve.tensor_tensor(qk1[:], PA[u][:, 0:320], b_qkv1[:, 0:320], ALU.add))
                    dve.tensor_tensor(vx1[u][:, :, 0:16], heads(PA[u][:, 320:384], 16), heads(b_qkv1[:, 320:384], 16), ALU.add)
                    dve.tensor_tensor(heads(ra1[:], 16), heads(qk1[:], 16),
                                      cos1[:].unsqueeze(1).broadcast_to([128, 20, 16]), ALU.mult)
                    pairs = qk1[:].rearrange("p (h c t) -> p h c t", c=8, t=2)
                    rpairs = rb1[:].rearrange("p (h c t) -> p h c t", c=8, t=2)
                    spairs = sin1[:].rearrange("p (c t) -> p c t", t=2)
                    dve.tensor_tensor(rpairs[:, :, :, 0], pairs[:, :, :, 1],
                                      spairs[:, :, 0].unsqueeze(1).broadcast_to([128, 20, 8]), ALU.mult)
                    chain(dve.tensor_tensor(rpairs[:, :, :, 1], pairs[:, :, :, 0],
                                            spairs[:, :, 1].unsqueeze(1).broadcast_to([128, 20, 8]), ALU.mult))
                    chain(dve.tensor_tensor(qk1[:], ra1[:], rb1[:], ALU.add))
                    chain(split(kpad1[u], heads(qk1[:, 256:320], 16), 16, 4, (0, 32), 16))
                    split(qpad1[u], heads(qk1[:, 0:256], 16), 16, 16, (0, 16), 32).then_inc(sg_["qkv_sb"], 1)
                elif what == "s":
                    maxima(s, u, p, a, n)
                elif what == "out":
                    weighted(s, u, p, a=L1, dst=on[u][:]).then_inc(sg_["on_sb"], 1)
                elif what == "proj":
                    s[u].wait(dve, "pr_ps", p, 1)
                    chain(dve.tensor_tensor(tmp[u][:], PA[u][:, 0:D], b_pr1[:], ALU.add))
                    chain(dve.tensor_tensor(at(x, u, p), at(x, u, p), tmp[u][:], ALU.add))
                elif what == "xnorm":
                    dve.tensor_scalar(xn[u][:], *norm(s, u, p, 2)).then_inc(sg_["xn"], 1)
                    cb = at(ctxt, u, p)
                    dve.tensor_tensor(kvr[u][:, 0:C], cb, cosk[:], ALU.mult)
                    dve.tensor_tensor(ka[:, 0:C // 2], cb[:, C // 2:C], sink[:, 0:C // 2], ALU.mult)
                    chain(dve.tensor_tensor(ka[:, C // 2:C], cb[:, 0:C // 2], sink[:, C // 2:C], ALU.mult))
                    dve.tensor_tensor(kvr[u][:, 0:C], kvr[u][:, 0:C], ka[:], ALU.add).then_inc(sg_["kv_sb"], 1)
                elif what == "queries" and a < XJ:
                    n = a
                    s[u].wait(dve, "qb_ps", p, n + 1)
                    if n >= 1:
                        s[u].wait(dve, "qk_ps", p, n)
                    lo, hi = (m[u][0:HQ, :].rearrange("p (h t) -> p h t", h=4) for m in (PA, PB))
                    for k, (src, tab) in enumerate(((lo, cosq[:, 0]), (hi, sinq[:, 0]), (hi, cosq[:, 1]), (lo, sinq[:, 1]))):
                        last = dve.tensor_tensor(rp[u][:, k], src, tab.unsqueeze(1).broadcast_to([HQ, 4, 128]), ALU.mult)
                    last.then_inc(sg_["rope"], 1)
                elif what == "xs":
                    n = a
                    s[u].wait(dve, "s_ps", p, 4 + n + 1)
                    dve.tensor_reduce(nmx[u][:, 4 * n:4 * n + 4], (PA, PB)[n % 2][u][:].rearrange("p (g t) -> p g t", g=4),
                                      AX.X, ALU.max, negate=True).then_inc(sg_["s_max"], 1)
                elif what == "xst" and a >= 1:
                    n = a - 1
                    s[u].wait(dve, "pv_ps", p, 4 + n + 1)
                    pv = (PC, PD)[n % 2][u][:, 0:4 * (C + 1)].rearrange("p (h w) -> p h w", w=C + 1)
                    chain(dve.reciprocal(rden[u][:, 4 * n:4 * n + 4], pv[:, :, C]))
                    dve.tensor_tensor(cn[u][:, 4 * n:4 * n + 4, :], pv[:, :, 0:C],
                                      rden[u][:, 4 * n:4 * n + 4].unsqueeze(2).broadcast_to([128, 4, C]), ALU.mult) \
                        .then_inc(sg_["cn_sb"], 1)
                elif what == "xproj":
                    s[u].wait(dve, "pr_ps", p, 2)
                    chain(dve.tensor_tensor(at(x, u, p), PA[u][:, 0:D], at(x, u, p), ALU.add))
                elif what == "rnorm":
                    dve.tensor_scalar(xn[u][:], *norm(s, u, p, 3)).then_inc(sg_["xn"], 1)
                elif what == "choose":
                    dve.wait_ge(r1["lg_ps"], p * 2 + u + 1)
                    chain(dve.tensor_copy(lgp[:, 0:E1], PB[u][:, 0:E1]))
                    chain(dve.max(top8[:], lgp[:, 0:E1]))
                    chain(dve.memset(top8[:, TOP1:8], -3e38))
                    dve.tensor_scalar(nmax[:], top8[:, 0:1], -1.0, None, ALU.mult).then_inc(r1["top"], 1)
                    chain(dve.match_replace(lgp2[:], top8[:], lgp[:], -2e38))
                    chain(dve.tensor_tensor(msk[:, 0:E1], lgp[:, 0:E1], lgp2[:, 0:E1], ALU.not_equal))
                    dve.wait_ge(r1["ex"], p * 2 + u + 1)
                    chain(dve.tensor_reduce(den[:], ex[:, 0:E1], AX.X, ALU.add))
                    chain(dve.reciprocal(den[:], den[:]))
                    dve.scalar_tensor_tensor(at(dw[:, :, 0:E1], u, p), ex[:, 0:E1], den[:],
                                             msk[:, 0:E1], ALU.mult, ALU.mult).then_inc(r1["done"], 1)

            two_streams(dve, B_FIRST, B_SECOND, step_b, chain.turn)

            dve.wait_ge(r1["done"], B)
            chain.turn()
            with dve.Fori(0, NF // 2) as i:
                for u in range(2):
                    chain.turn()
                    chain(dve.tensor_copy(dwc[:, u, :], dw[:, :, bass.ds(i * 2 + u, 1)].rearrange("p b a -> p (b a)")))
                    for th in range(2):
                        step = i * 4 + u * 2 + th
                        for f in range(2):
                            dve.wait_ge(f1["sg"], step * 2 + f + 1)
                            dve.tensor_tensor(af[:, f, :], sgf[:, f, :], bank[2 * f + 1][0:FH, :], ALU.mult) \
                                .then_inc(f1["a_sb"], 1)
                        dve.sem_inc(f1["credit"], 1)
                        for q in range(4):
                            dve.wait_ge(f1["y_ps"], step * 4 + q + 1)
                            dve.scalar_tensor_tensor(x[:, 4 * th + q, :], bank[4 + q % 2][:, 0:D], dwc[:, u, 4 * th + q:4 * th + q + 1],
                                                     x[:, 4 * th + q, :], ALU.mult, ALU.add).then_inc(f1["y_sb"], 1)
            dve.wait_ge(f1["y_sb"], NF * 8)
            dve.sem_inc(f1["x_new"], 1)


def constants():
    import numpy as np
    q, k = np.arange(128)[:, None], np.arange(128)[None, :]
    never = np.where(k > q, -1e30, 0.0)
    slope = 2.0 ** (-8.0 / 32.0)
    e = np.arange(E0)[None, :]

    def angles(n, dim):
        inv = (1.0 / 10000.0 ** (np.arange(0, dim, 2, dtype=np.float32) / np.float32(dim))).astype(np.float32)
        return np.repeat((np.arange(n, dtype=np.float32)[:, None] * inv[None, :]).astype(np.float32), 2, axis=1)

    f1, fq, fk = angles(S, 16), angles(S, QX), angles(S, C)
    sign = np.where(np.arange(16) % 2 == 0, -1.0, 1.0)
    halves = lambda a: np.ascontiguousarray(a.T.reshape(2, HQ, S).transpose(1, 0, 2)).astype(np.float32)
    first = lambda w: np.where(np.arange(w) < w // 2, -1.0, 1.0)
    f = lambda a: np.ascontiguousarray(a).astype(np.float32)
    return {
        "tri": f(q < k), "ones": np.ones((128, 128), np.float32), "eplus1": f(np.broadcast_to(e + 1, (128, E0))),
        "tokall": (np.arange(B)[None, :] * S + np.arange(128)[:, None]).astype(np.int32),
        "cos1": f(np.cos(f1)), "sin1": f(np.sin(f1) * sign),
        "cosq": halves(np.cos(fq)), "sinq": halves(np.sin(fq) * first(QX)),
        "cosk": f(np.cos(fk)), "sink": f(np.sin(fk) * first(C)),
        "ident": np.eye(128, dtype=np.float32),
        "never": never.astype(np.float32),
        "neverT": np.ascontiguousarray(never.T).astype(np.float32),
        "alibi": (slope * np.arange(128) * np.sqrt(8.0)).astype(np.float32)[:, None],
    }


def laid_out(w):
    import numpy as np

    def by_group(a):
        return a.reshape(*a.shape[:-1], 2, 2, 4, 16).swapaxes(-3, -2).reshape(*a.shape)

    def pairs(a):
        return a.reshape(HX // 2, 2, *a.shape[1:]).transpose(0, 2, 1, 3)

    shared = lambda a: a.reshape(D, 2, I1).transpose(1, 0, 2)
    return {
        "w_gu0": np.concatenate([w["L0_ffn_gate_proj"], w["L0_ffn_up_proj"]], axis=2),
        "w_qkv1": np.concatenate([by_group(w["L1_attn_Wq"].T), w["L1_attn_Wk"].T, w["L1_attn_Wv"].T], axis=1),
        "b_qkv1": np.concatenate([by_group(w["L1_attn_bq"]), w["L1_attn_bk"], w["L1_attn_bv"]]),
        "w_o1": w["L1_attn_Wo"].T,
        "w_rt1": w["L1_ffn_gate_weight"].T,
        "wq_x": pairs(w["L1_xattn_Wq"].reshape(HX, KX, D)),
        "w_kc_q": pairs(w["L1_xattn_w_kc_q"]),
        "w_qr": pairs(w["L1_xattn_W_qr"].transpose(0, 2, 1)),
        "w_kr": pairs(w["L1_xattn_W_kr"].transpose(0, 2, 1)),
        "w_kc_kv": pairs(w["L1_xattn_w_kc_kv"]),
        "wo_x": pairs(w["L1_xattn_Wo"].T.reshape(HX, KX, D)),
        "w_gu1": np.concatenate([
            np.concatenate([w["L1_ffn_w_gate"], shared(w["L1_ffn_ws_gate"])], axis=0),
            np.concatenate([w["L1_ffn_w_up"], shared(w["L1_ffn_ws_up"])], axis=0)], axis=2),
        "w_d1": np.concatenate([w["L1_ffn_w_down"], w["L1_ffn_ws_down"].reshape(2, I1, D)], axis=0),
    }


def kernel(**inputs):
    import numpy as _np
    import concourse.bacc as _bacc
    from concourse import mybir as _mybir
    from concourse.bass_utils import run_bass_kernel_spmd as _run

    nc = _bacc.Bacc("TRN2", target_bir_lowering=False, num_devices=1)
    host = {n: inputs[n] for n in ("x", "ctx_512", "L0_attn_W_attn", "L0_attn_b_attn", "L0_attn_W_proj",
                                   "L0_attn_b_proj", "L0_ffn_router_weight", "L0_ffn_down_proj", "L1_attn_bo")}
    host.update(laid_out({k: _np.asarray(v) for k, v in inputs.items()}))
    host = {k: _np.ascontiguousarray(v) for k, v in host.items()}
    host.update(constants())
    arrays, t = {}, {}
    for name, a in host.items():
        arrays[f"in_{name}"] = a
        t[name] = nc.dram_tensor(f"in_{name}", a.shape, _mybir.dt.from_np(a.dtype), kind="ExternalInput").ap()
    out = nc.dram_tensor("out_x", (B, S, D), F32, kind="ExternalOutput").ap()
    program(nc, t, out, None)
    r = _run(nc, [arrays], core_ids=[0])
    return r.results[0]["out_x"]
```

```python
from contextlib import ExitStack

import concourse.bass as bass
from concourse import mybir

F32 = mybir.dt.float32
F32R = mybir.dt.float32r
BF16 = mybir.dt.bfloat16
I32 = mybir.dt.int32
U32 = mybir.dt.uint32
ALU = mybir.AluOpType
ACT = mybir.ActivationFunctionType
AX = mybir.AxisListType

B, S, D = 8, 128, 256
C = 64
KC = D // 128
PAIRS = B // 2
EPS = 1e-5
E0, I0, TOP0, CAP = 64, 96, 8, 128
NSLOT = E0 * CAP
NTOK = B * S
HX, KX, QX, RX = 16, 128, 192, 64
HQ = QX // 2
E1, I1, TOP1 = 16, 176, 4
NF, FH = E1 + 2, I1 // 2
RING = 4


class Chain:

    def __init__(self, eng, sem):
        self.eng, self.sem, self.n = eng, sem, 0

    def turn(self):
        self.eng.sem_clear(self.sem)
        self.n = 0

    def __call__(self, ins):
        self.n += 1
        ins.then_inc(self.sem, 1)
        self.eng.wait_ge(self.sem, self.n)


class Attention:

    def __init__(self, name, strips, dim, shared, causal, biased, scale):
        self.name, self.strips, self.dim, self.shared = name, strips, dim, shared
        self.causal, self.biased, self.scale = causal, biased, scale
        self.width = 128 // strips
        self.heads = 8 * strips
        self.jobs = [(half, row) for half in range(2) for row in range(strips)]
        self.kgroups = 2 if shared else 8
        self.kbanks = -(-self.kgroups // 4)
        self.banks = self.kbanks + 2
        self.bias = 3 * dim
        self.top = self.bias + (2 if biased else 0)
        self.rows = self.top + 2

    def head(self, half, row, g):
        return (self.strips * half + row) * 4 + g if self.shared else 4 * (4 * half + g) + row


L0 = Attention("a0", 4, 8, False, True, True, 8.0 ** -0.5)
X0 = Attention("x0", 4, 8, True, False, True, 8.0 ** -0.5)
L1 = Attention("a1", 2, 16, True, True, False, 16.0 ** -0.5)
XJ = HX // 4


class Phase:

    def __init__(self, sem, base, per):
        self.sem, self.base, self.per = sem, base, per

    def after(self):
        return {n: self.base.get(n, 0) + PAIRS * k for n, k in self.per.items()}

    def wait(self, eng, name, p, k):
        eng.wait_ge(self.sem[name], p * self.per[name] + (self.base.get(name, 0) + k))


PER_A = dict(stats=3, rstd=3, xn=2, xnt_ps=2, xnt_sb=2, qkv_ps=1, qkv_sb=2, kq_ps=L0.banks + X0.banks,
             kq_sb=L0.banks + X0.banks, s_ps=16, s_max=16, top=4, q2_ps=4, q2_sb=4, st_ps=16, st_exp=16, pv_ps=16,
             on_sb=1, ot_ps=1, ot_sb=1, pr_ps=1)
PER_B = dict(stats=3, rstd=3, xn=3, xnt_ps=3, xnt_sb=3, qkv_ps=1, qkv_sb=1, kq_ps=L1.banks, kq_sb=L1.banks,
             s_ps=4 + XJ, s_max=4 + XJ, top=2, q2_ps=2, q2_sb=2, st_ps=4 + XJ, st_exp=4 + XJ, pv_ps=4 + XJ,
             on_sb=1, ot_ps=1, ot_sb=1, pr_ps=2, kv_sb=1, kt_ps=1, kt_sb=1, qb_ps=2 * XJ, rope=2 * XJ, rsum=2 * XJ, qk_ps=XJ, qk_sb=XJ,
             nm_ps=1, nm_sb=1, cn_sb=XJ, ct_ps=2, ct_sb=2)
OFF = {L0: dict(kq=0, s=0, q2=0), X0: dict(kq=L0.banks, s=8, q2=2), L1: dict(kq=0, s=0, q2=0)}


def attention_steps(a):
    half = len(a.jobs) // 2
    return ([("kq", a, n) for n in range(a.banks)]
            + [("s", a, n) for n in range(half + 1)] + [("q2", a, 0)]
            + [("s", a, n) for n in range(half + 1, 2 * half)]
            + [("st", a, 0), ("q2", a, 1)] + [("st", a, n) for n in range(1, 2 * half + 1)])


A_HEAD = [("prenorm",)]
A_STEPS = [("turn", 0), ("qkv", L0), *attention_steps(L0), ("out", 0), ("proj", 0), ("norm", X0),
           *attention_steps(X0), ("xout",), ("rnorm",), ("turn", 1), ("logits",), ("choose",), ("prenorm",),
           ("place",), ("weigh",), *[("scatter", j) for j in range(TOP0)]]
GATHERS = [("gather", j) for j in range(TOP0)]
SUMS = [("sum", j) for j in range(TOP0)]
B_HEAD = [*GATHERS, *SUMS, ("prenorm",)]
QUERIES = [("big", 0, 0), ("big", 0, 1),
           *[step for n in range(1, XJ) for step in (("big", n, 0), ("keys", n - 1), ("big", n, 1))], ("keys", XJ - 1)]
B_STEPS = [("turn", 0), ("qkv", L1), *attention_steps(L1), ("out", 0), ("proj", 0),
           ("xnorm",), ("turn", 1), *QUERIES, *[("xs", n) for n in range(XJ)],
           ("xmax",), *[("xst", n) for n in range(XJ + 1)], ("xct", 0), ("xct", 1), ("xproj",), ("rnorm",),
           ("turn", 2), ("prenorm",), ("logits",), ("choose",)]
B_STEPS[-20:-12] = [x for pair in zip(B_STEPS[-20:-12], GATHERS) for x in pair]
B_STEPS[-15:-7] = [x for pair in zip(B_STEPS[-15:-7], SUMS) for x in pair]
LENGTH_A = dict(turn=1.5, qkv=7, kq=1.2, s=1.4, q2=1.8, st=2.2, out=2.5, proj=3, norm=4, xout=2, rnorm=2.5, logits=1.5,
                choose=2, place=1, weigh=4, prenorm=1.5, scatter=0.1, gather=0.1, sum=0.3, xnorm=3, big=2.2, keys=2.5,
                xs=2, xmax=1.5, xst=2.8, xct=1.5, xproj=3.5)
LENGTH_B = dict(LENGTH_A, st=1.8)
LAG_A, LAG_B = 0.3, 0.3


def spans(steps, length):
    ends, t = [], 0.0
    for step in steps:
        t += length[step[0]]
        ends.append(t)
    return [(e - length[x[0]] / 2) / t for e, x in zip(ends, steps)], [e / t for e in ends]


def merged(a, b, length):
    marks = [(m, 0, x) for m, x in zip(spans(a, length)[0], a)] + [(m, 1, x) for m, x in zip(spans(b, length)[0], b)]
    return [(which, x) for _, which, x in sorted(marks, key=lambda m: m[:2])]


def two_streams(eng, head, steps, length, lag, do, turn=lambda: None):
    ends = spans(steps, length)[1]
    lead, tail = (sum(e <= at for e in ends) for at in (lag, 1 - lag))

    def both(a, pa, b, pb):
        for which, step in merged(a, b, length):
            do(*((0, pa) if which == 0 else (1, pb)), *step)

    turn()
    for u in range(2):
        for step in head:
            do(u, -1, *step)
    for step in steps[:lead]:
        do(0, 0, *step)
    with eng.Fori(0, PAIRS - 1) as p:
        turn()
        both(steps[lead:], p, steps[:tail], p)
        both(steps[:lead], p + 1, steps[tail:], p)
    turn()
    both(steps[lead:], PAIRS - 1, steps[:tail], PAIRS - 1)
    for step in steps[tail:]:
        do(1, PAIRS - 1, *step)


def next_batch(p):
    return None if isinstance(p, int) and p == PAIRS - 1 else p + 1


class Sems(dict):

    def __init__(self, nc, ctx, stage, names):
        self.make = lambda n: ctx.enter_context(nc.semaphore(f"{stage}_{n}"))
        self.names = names.split()

    def __missing__(self, n):
        assert n in self.names, n
        self[n] = self.make(n)
        return self[n]


sems = Sems


ROUTE_SEMS = "free0 free1 lg_ps top ex msk pos_ps idx xn_st scat done"
MOE_SEMS = ("credit xg0 xg1 xg2 xg3 wl0 wl1 wl2 wl3 xt_ps xt_sb h_ps sg a_sb y_ps y_sb yst0 yst1 yst2 yst3 slots")
FFN_SEMS = "free wl0 wl1 wd0 wd1 w_high w_low x_high x_low g_ps sg a_sb y_ps y_sb x_new"


def program(nc, t, out, stages):
    with ExitStack() as ctx:
        def sb(name, shape, dt=F32):
            return ctx.enter_context(nc.sbuf_tensor(name, shape, dt))

        bank = [ctx.enter_context(nc.psum_tensor(f"bank{n}", [128, 512], F32)) for n in range(8)]
        PA, PB, PC, PD = ([bank[4 * u + n] for u in range(2)] for n in range(4))

        x = sb("x", [128, B, D])
        ctxt = sb("ctxt", [128, B, C])
        ident = sb("ident", [128, 128])
        identb = sb("identb", [128, 128], BF16)
        maskq = sb("maskq", [128, 128], BF16)
        maskk = sb("maskk", [128, 128], BF16)
        alibi = sb("alibi", [128, 1])
        neghalf = sb("neghalf", [128, 1])
        eps = sb("eps", [128, 1])
        area0 = sb("area0", [128, KC * 3 * D + 3 * D])
        w_qkv0 = area0[:, 0:KC * 3 * D].rearrange("p (c n) -> p c n", c=KC)
        b_qkv0 = area0[:, KC * 3 * D:]
        w_pr0 = sb("w_pr0", [128, KC, D])
        b_pr0 = sb("b_pr0", [128, D])

        def two(name, shape, dt=F32):
            return [sb(f"{name}{u}", shape, dt) for u in range(2)]

        never = sb("never", [128, 128])
        neverT = sb("neverT", [128, 128])
        stats, mv, var, rstd = two("stats", [128, 6]), two("mv", [128, 2]), two("var", [128, 1]), two("rstd", [128, 1])
        xn, xnT = two("xn", [128, D]), two("xnT", [128, KC, 128])
        nmx = two("nmx", [128, 32])
        qarea = two("qarea", [128, 8 * 128])
        qpad = [q[:].rearrange("p (h w) -> p h w", w=32) for q in qarea]
        qpad1 = [q[:].rearrange("p (h w) -> p h w", w=64) for q in qarea]
        qT = two("qT", [128, 8, 128], F32R)
        karea = two("karea", [128, 2 * 8 * 128])
        kpad = [k[:, 0:1024].rearrange("p (h w) -> p h w", w=32) for k in karea]
        kT = two("kT", [128, 8, 128], F32R)
        kpadx, kpad1 = two("kpadx", [128, 8, 32]), two("kpad1", [128, 4, 64])
        qk0 = [k[:, 1024:1536] for k in karea]
        vx, vc, vx1 = two("vx", [128, 32, 9]), two("vc", [128, 8, 9]), two("vx1", [128, 4, 17])
        PT = two("PT", [128, 2, 4, 128])
        rden = two("rden", [128, 32])
        on, onT = two("on", [128, D]), two("onT", [128, KC, 128])
        tmp = on

        w_rt0 = sb("w_rt0", [128, KC, E0])
        tri = sb("tri", [128, 128])
        ones = sb("ones", [128, 128])
        eplus1 = sb("eplus1", [128, E0])
        tokall = sb("tokall", [128, B], I32)
        zrow = sb("zrow", [1, D])
        fillt = sb("fillt", [128, E0], I32)
        lg = sb("lg", [128, E0])
        lg2 = sb("lg2", [128, E0])
        top8 = sb("top8", [128, 8])
        nmax = sb("nmax", [128, 1])
        ex = sb("ex", [128, E0])
        msk = sb("msk", [128, E0])
        macc = sb("macc", [128, E0])
        keep = sb("keep", [128, E0])
        slm = sb("slm", [128, E0])
        s8 = sb("s8", [128, 8])
        zz = sb("zz", [128, 8])
        wk = sb("wk", [128, E0])
        den = sb("den", [128, 1])
        eq = sb("eq", [128, 8, E0])
        w8 = sb("w8", [128, B, 8])
        idx8 = sb("idx8", [128, B, 8], U32)
        idxw = sb("idxw", [128, 8], U32)
        tokw = sb("tokw", [128, 1], I32)
        slots = sb("slots", [128, E0], I32)
        ixe = sb("ixe", [128, RING, 1], U32)
        area1 = sb("area1", [128, RING * D + RING * KC * 2 * I0 + 2 * KC * 128])
        xe = area1[:, 0:RING * D].rearrange("p (r d) -> p r d", r=RING)
        wgu = area1[:, RING * D:RING * (D + KC * 2 * I0)].rearrange("p (r c n) -> p r c n", r=RING, c=KC)
        xeT = area1[:, RING * (D + KC * 2 * I0):].rearrange("p (v c t) -> p v c t", v=2, c=KC)
        wdn = sb("wdn", [I0, RING, D])
        sg, aT = (PT[0][0:I0, n, 0:2, :] for n in range(2))
        ye = sb("ye", [128, RING, D])
        yg = two("yg", [128, 8, D])
        w8c = two("w8c", [128, 8])
        w_qkv1 = sb("w_qkv1", [128, KC, 384])
        b_qkv1 = sb("b_qkv1", [128, 384])
        w_pr1 = sb("w_pr1", [128, KC, D])
        b_pr1 = sb("b_pr1", [128, D])
        cos1 = sb("cos1", [128, 16])
        sin1 = sb("sin1", [128, 16])
        qk1, ka = (eq[:].rearrange("p a e -> p (a e)")[:, lo:lo + n] for lo, n in ((0, 320), (320, C)))
        ra1, rb1 = (area1[:, lo:lo + 320] for lo in (2432, 2752))
        wqc = sb("wqc", [128, KC, HX * QX])
        wqk = sb("wqk", [HQ, 2, HX, C])
        weff = sb("weff", [128, HX // 2, D])
        cosq = sb("cosq", [HQ, 2, 128])
        sinq = sb("sinq", [HQ, 2, 128])
        cosk = sb("cosk", [128, C])
        sink = sb("sink", [128, C])
        fq, fo = [y[:, 0:2, :] for y in yg], [ye[:, 2 * v:2 * v + 2, :] for v in range(2)]
        fc, fr = [y[:, 2:4, 0:QX] for y in yg], [y[0:RX, 4:6, 0:QX] for y in yg]
        fk, fv = [y[0:RX, 6:8, 0:C] for y in yg], [y[:, 6:8, C:2 * C] for y in yg]
        kvr, kvT = two("kvr", [128, 128]), two("kvT", [C, 128])
        rp = [k[0:HQ, :].rearrange("p (k h t) -> p k h t", k=4, h=4) for k in karea]
        qk2 = two("qk2", [C, 8, 128])

        def qkT(u, n):
            tile = qarea[u][0:C, :].rearrange("p (h t) -> p h t", h=8) if n < 2 else qk2[u][:]
            return tile[:, 4 * (n % 2):4 * (n % 2) + 4, :]

        nmT = two("nmT", [HX, 128])
        cn = [k[:, 0:1024].rearrange("p (h c) -> p h c", c=C) for k in karea]
        cT = [k[:, 1024:2048].rearrange("p (h t) -> p h t", t=128) for k in karea]
        w_rt1 = sb("w_rt1", [128, KC, E1])
        lgp = sb("lgp", [128, E1 + 8])
        lgp2 = sb("lgp2", [128, E1 + 8])
        dw = sb("dw", [128, B, NF])
        dwc = sb("dwc", [128, 2, B])
        xT6 = area0[:, 0:KC * B * 128].rearrange("p (c b t) -> p c b t", c=KC, b=B)
        wf = area1[:, 0:2 * KC * 2 * I1].rearrange("p (v c n) -> p v c n", v=2, c=KC)
        wfd = ye[0:FH, :, :].rearrange("p (v f) d -> p v f d", v=2)
        wh, wl = sb("wh", [128, 2, KC, 2 * I1], F32R), sb("wl", [128, 2, KC, 2 * I1], F32R)
        xh, xl = qT, kT
        sgf = cT[0][0:FH, :, :].rearrange("p (f a) t -> p f (a t)", f=2)
        af = [c[0:FH, :, :].rearrange("p (f a) t -> p f (a t)", f=2) for c in cn]

        xn3 = nc.dram_tensor("xn3", [NTOK + 1, D], F32).ap()
        table = nc.dram_tensor("table", [NSLOT, 1], I32).ap()
        yrows = nc.dram_tensor("yrows", [NSLOT + 1, D], F32).ap()

        loaded = sems(nc, ctx, "load", "x ctx const w0 w1 fill")
        chains = sems(nc, ctx, "chain", "dve pool act")
        ready = sems(nc, ctx, "ready", "pads masks")
        stream = [sems(nc, ctx, f"s{u}", " ".join({**PER_A, **PER_B})) for u in range(2)]
        SA = [Phase(stream[u], {}, PER_A) for u in range(2)]
        SB = [Phase(stream[u], SA[u].after(), PER_B) for u in range(2)]
        fold = sems(nc, ctx, "fold", "ld0 ld1 ps sb free")
        r0 = sems(nc, ctx, "r0", ROUTE_SEMS)
        m0 = sems(nc, ctx, "m0", MOE_SEMS)
        c0 = sems(nc, ctx, "c0", "credit0 credit1 yg0 yg1")
        r1 = sems(nc, ctx, "r1", ROUTE_SEMS)
        f1 = sems(nc, ctx, "f1", FFN_SEMS)
        stored = ctx.enter_context(nc.semaphore("stored"))

        consts1 = ((tri, "tri"), (ones, "ones"), (eplus1, "eplus1"), (tokall, "tokall"), (cos1, "cos1"),
                   (sin1, "sin1"), (cosq, "cosq"), (sinq, "sinq"), (cosk, "cosk"), (sink, "sink"),
                   )
        N_W0, N_W1 = 5, len(consts1) + 5

        def at(tile, u, p):
            return tile[:, bass.ds(p * 2 + u, 1), :].rearrange("p a d -> p (a d)")

        def xb(b):
            return x[:, bass.ds(b, 1), :].rearrange("p a d -> p (a d)")

        block = ctx.enter_context(nc.Block())

        @block.sync
        def _(sp):
            for dst, src in ((ident[:], "ident"), (never[:], "never"), (neverT[:], "neverT"), (alibi[:], "alibi")):
                sp.dma_start(dst, t[src]).then_inc(loaded["const"], 16)
            sp.dma_start(x[:], t["x"].rearrange("b s d -> s b d")).then_inc(loaded["x"], 16)
            sp.dma_start(w_qkv0, t["L0_attn_W_attn"].rearrange("(c p) n -> p c n", p=128)).then_inc(loaded["w0"], 16)
            sp.dma_start(b_qkv0, t["L0_attn_b_attn"].partition_broadcast(128)).then_inc(loaded["w0"], 16)
            sp.dma_start(w_pr0[:], t["L0_attn_W_proj"].rearrange("(c p) n -> p c n", p=128)).then_inc(loaded["w0"], 16)
            sp.dma_start(b_pr0[:], t["L0_attn_b_proj"].partition_broadcast(128)).then_inc(loaded["w0"], 16)
            sp.dma_start(ctxt[:], t["ctx_512"].rearrange("b s d -> s b d")).then_inc(loaded["ctx"], 16)
            sp.dma_start(w_rt0[:], t["L0_ffn_router_weight"].rearrange("(c p) n -> p c n", p=128)).then_inc(loaded["w0"], 16)
            for dst, src in consts1:
                sp.dma_start(dst[:], t[src]).then_inc(loaded["w1"], 16)
            sp.dma_start(w_qkv1[:], t["w_qkv1"].rearrange("(c p) n -> p c n", p=128)).then_inc(loaded["w1"], 16)
            sp.dma_start(b_qkv1[:], t["b_qkv1"].partition_broadcast(128)).then_inc(loaded["w1"], 16)
            sp.dma_start(w_pr1[:], t["w_o1"].rearrange("(c p) n -> p c n", p=128)).then_inc(loaded["w1"], 16)
            sp.dma_start(b_pr1[:], t["L1_attn_bo"].partition_broadcast(128)).then_inc(loaded["w1"], 16)
            sp.dma_start(w_rt1[:], t["w_rt1"].rearrange("(c p) n -> p c n", p=128)).then_inc(loaded["w1"], 16)
            sp.wait_ge(ready["pads"], 1)
            sp.dma_start(table.rearrange("(p e) a -> p (e a)", e=E0), fillt[:]).then_inc(loaded["fill"], 16)
            sp.dma_start(xn3[NTOK:NTOK + 1, :], zrow[:]).then_inc(loaded["fill"], 16)
            sp.dma_start(yrows[NSLOT:NSLOT + 1, :], zrow[:]).then_inc(loaded["fill"], 16)

            with sp.Fori(0, HX // 4) as hp:
                for v in range(2):
                    sp.wait_ge(fold["free"], hp * 2 + v + 1)
                    for dst, src in ((fq, "wq_x"), (fc, "w_kc_q"), (fr, "w_qr"), (fk, "w_kr"), (fv, "w_kc_kv"), (fo, "wo_x")):
                        sp.dma_start(dst[v], t[src][bass.ds(hp * 2 + v, 1)].rearrange("a p u n -> p (a u) n")) \
                            .then_inc(fold[f"ld{v}"], 16)

            def store_rows(u, p):
                SA[u].wait(sp, "xn", p, 2)
                sp.dma_start(xn3[0:NTOK, :].rearrange("(b p) d -> b p d", p=128)[bass.ds(p * 2 + u, 1)]
                             .rearrange("a p d -> (a p) d"), xn[u][:]).then_inc(r0["xn_st"], 16)

            with sp.Fori(0, PAIRS) as p:
                store_rows(0, p)
                store_rows(1, p)

            sp.wait_ge(r0["scat"], 16 * 8 * B)
            sp.wait_ge(loaded["fill"], 16 * 3)
            sp.dma_start(slots[:], table.rearrange("(p e) a -> p (e a)", e=E0)).then_inc(m0["slots"], 16)
            yv = yrows[0:NSLOT, :].rearrange("(p e) d -> e p d", e=E0)

            def load_expert(u, e):
                sp.dma_start(wgu[:, u, :, :], t["w_gu0"][bass.ds(e, 1)].rearrange("a (c p) n -> p (a c) n", p=128)) \
                    .then_inc(m0[f"wl{u}"], 16)
                sp.dma_start(wdn[:, u, :], t["L0_ffn_down_proj"][bass.ds(e, 1)].rearrange("a p d -> p (a d)")) \
                    .then_inc(m0[f"wl{u}"], 16)

            def store_expert(u, e):
                sp.wait_ge(m0["y_sb"], e + 1)
                sp.dma_start(yv[bass.ds(e, 1)].rearrange("a p d -> (a p) d"), ye[:, u, :]).then_inc(m0[f"yst{u}"], 16)

            for u in range(RING):
                load_expert(u, u)
            with sp.Fori(0, E0 // RING - 1) as i:
                for u in range(RING):
                    store_expert(u, i * RING + u)
                    load_expert(u, i * RING + u + RING)
            for u in range(RING):
                store_expert(u, E0 - RING + u)

            def load_inner(u, e):
                sp.dma_start(wf[:, u], t["w_gu1"][bass.ds(e, 1)].rearrange("a (c p) n -> p (a c) n", p=128)) \
                    .then_inc(f1[f"wl{u}"], 16)

            def load_outer(u, e):
                sp.dma_start(wfd[:, u], t["w_d1"][bass.ds(e, 1)].rearrange("a (c p) n -> p (a c) n", p=FH)) \
                    .then_inc(f1[f"wd{u}"], 16)

            for u in range(RING):
                sp.wait_ge(m0[f"yst{u}"], 16 * (E0 // RING + 1))
            for u in range(2):
                load_inner(u, u)
                load_outer(u, u)
            with sp.Fori(0, NF // 2 - 1) as i:
                for u in range(2):
                    sp.wait_ge(f1["w_low"], i * 2 + u + 1)
                    load_inner(u, i * 2 + u + 2)
                    sp.wait_ge(f1["y_ps"], (i * 2 + u + 1) * 8)
                    load_outer(u, i * 2 + u + 2)
            with sp.Fori(0, B) as b:
                sp.wait_ge(f1["x_new"], 1)
                sp.dma_start(out[bass.ds(b, 1)].rearrange("a p d -> (a p) d"), xb(b)).then_inc(stored, 16)
            sp.wait_ge(stored, 16 * B)

        @block.gpsimd
        def _(pool):
            chain = Chain(pool, chains["pool"])

            def norm_rstd(s, u, p, k):
                s[u].wait(pool, "stats", p, k)
                chain(pool.tensor_tensor(var[u][:], mv[u][:, 1:2], eps[:], ALU.add))
                pool.tensor_tensor(rstd[u][:], var[u][:], neghalf[:], ALU.pow).then_inc(stream[u]["rstd"], 1)

            chain(pool.memset(neghalf[:], -0.5))
            chain(pool.memset(eps[:], EPS))
            pool.wait_ge(loaded["fill"], 16 * 3)
            pool.wait_ge(loaded["w1"], 16 * N_W1)

            def step_a(u, p, what, a=None, n=None):
                if what == "prenorm":
                    if next_batch(p) is not None:
                        norm_rstd(SA, u, next_batch(p), 1)
                elif what == "norm":
                    norm_rstd(SA, u, p, 2)
                elif what == "rnorm":
                    norm_rstd(SA, u, p, 3)
                elif what == "scatter":
                    if a == 0:
                        pool.wait_ge(r0["idx"], p * 2 + u + 1)
                        if not (isinstance(p, int) and p == 0 and u == 0):
                            pool.wait_ge(r0["scat"], (p * 2 + u) * (16 * TOP0))
                        chain(pool.tensor_copy(idxw[:], at(idx8, u, p)))
                        chain(pool.tensor_copy(tokw[:], tokall[:, bass.ds(p * 2 + u, 1)]))
                    pool.indirect_dma_start(table[:, :], bass.IndirectOffsetOnAxis(idxw[:, a:a + 1], 0), tokw[:, :],
                                            None, bounds_check=NSLOT - 1, oob_is_err=False) \
                        .then_inc(r0["scat"], 16)

            two_streams(pool, A_HEAD, A_STEPS, LENGTH_A, LAG_A, step_a, chain.turn)

            pool.sem_inc(m0["credit"], RING)
            pool.wait_ge(m0["slots"], 16)
            pool.wait_ge(r0["xn_st"], 16 * B)
            with pool.Fori(0, E0 // RING) as i:
                chain.turn()
                for u in range(RING):
                    pool.wait_ge(m0["credit"], i * RING + u + 1)
                    chain(pool.tensor_copy(ixe[:, u, :], slots[:, bass.ds(i * RING + u, 1)]))
                    pool.indirect_dma_start(xe[:, u, :], None, xn3[:, :],
                                            bass.IndirectOffsetOnAxis(ixe[:, u, :], 0)).then_inc(m0[f"xg{u}"], 16)

            for u in range(RING):
                pool.wait_ge(m0[f"yst{u}"], 16 * (E0 // RING + 1))
            for u in range(2):
                pool.sem_inc(c0[f"credit{u}"], 1)

            def step_b(u, p, what, a=None, n=None):
                if what == "gather":
                    q = next_batch(p)
                    if q is None:
                        return
                    if a == 0:
                        pool.wait_ge(c0[f"credit{u}"], q + 1)
                        if not (isinstance(q, int) and q == 0 and u == 0):
                            pool.wait_ge(c0[f"yg{1 - u}"], (q + u) * (16 * TOP0))
                        chain(pool.tensor_copy(idxw[:], at(idx8, u, q)))
                    pool.indirect_dma_start(yg[u][:, a, :], None, yrows[:, :],
                                            bass.IndirectOffsetOnAxis(idxw[:, a:a + 1], 0)) \
                        .then_inc(c0[f"yg{u}"], 16)
                elif what == "prenorm":
                    if next_batch(p) is not None:
                        norm_rstd(SB, u, next_batch(p), 1)
                elif what == "xnorm":
                    norm_rstd(SB, u, p, 2)
                elif what == "rnorm":
                    norm_rstd(SB, u, p, 3)
                elif what == "keys":
                    SB[u].wait(pool, "rope", p, 2 * a + 2)
                    for k in range(2):
                        pool.tensor_tensor(rp[u][:, 2 * k], rp[u][:, 2 * k], rp[u][:, 2 * k + 1], ALU.add) \
                            .then_inc(stream[u]["rsum"], 1)

            two_streams(pool, B_HEAD, B_STEPS, LENGTH_B, LAG_B, step_b, chain.turn)

        @block.scalar
        def _(act):
            def copy(dst, src):
                return act.activation(dst, src, ACT.Copy)

            def turned(s, u, p, k):
                s[u].wait(act, "xnt_ps", p, k)
                copy(xnT[u][:], PD[u][:, 0:D].rearrange("p (c t) -> p c t", c=KC)).then_inc(stream[u]["xnt_sb"], 1)

            def attention(s, u, p, what, a, n):
                off, sg_ = OFF[a], stream[u]
                if what == "kq":
                    s[u].wait(act, "kq_ps", p, off["kq"] + n + 1)
                    g = min(4, a.kgroups) if n < a.kbanks else 4
                    dst = kT[u][:, 4 * n:4 * n + g, :] if n < a.kbanks else qT[u][:, 4 * (n - a.kbanks):4 * (n - a.kbanks) + 4, :]
                    copy(dst, (PC, PD)[n % 2][u][:, 0:128 * g].rearrange("p (g t) -> p g t", g=g)).then_inc(sg_["kq_sb"], 1)
                elif what == "q2":
                    s[u].wait(act, "q2_ps", p, off["q2"] + n + 1)
                    copy(qT[u][:, 4 * n:4 * n + 4, :], PD[u][:].rearrange("p (g t) -> p g t", g=4)).then_inc(sg_["q2_sb"], 1)
                elif what == "st" and n < len(a.jobs):
                    s[u].wait(act, "st_ps", p, off["s"] + n + 1)
                    if n >= 2:
                        s[u].wait(act, "pv_ps", p, off["s"] + n - 1)
                    act.activation(PT[u][:, n % 2], (PA, PB)[n % 2][u][:].rearrange("p (g t) -> p g t", g=4), ACT.Exp,
                                   scale=a.scale).then_inc(sg_["st_exp"], 1)

            def out_turned(s, u, p):
                s[u].wait(act, "ot_ps", p, 1)
                copy(onT[u][:], PD[u][:, 0:D].rearrange("p (c t) -> p c t", c=KC)).then_inc(stream[u]["ot_sb"], 1)

            chain = Chain(act, chains["act"])
            with act.Fori(0, HX // 2) as hp:
                for u in range(2):
                    act.wait_ge(fold["ps"], hp * 2 + u + 1)
                    copy(wqc[:, :, bass.ds(hp * (2 * QX) + u * QX, QX)],
                         bank[3 * u][:, 0:2 * QX].rearrange("p (c n) -> p c n", c=KC))
                    copy(wqk[:, :, bass.ds(hp * 2 + u, 1), :].rearrange("p f a c -> p f (a c)"),
                         bank[3 * u + 1][0:HQ, 0:2 * C].rearrange("p (f c) -> p f c", f=2))
                    copy(weff[64 * u:64 * u + 64, bass.ds(hp, 1), :].rearrange("p a d -> p (a d)"),
                         bank[3 * u + 2][64 * u:64 * u + 64, 0:D]).then_inc(fold["sb"], 1)

            def step_a(u, p, what, a=None, n=None):
                if what == "turn":
                    turned(SA, u, p, a + 1)
                elif what in ("kq", "q2", "st"):
                    attention(SA, u, p, what, a, n)
                elif what == "out":
                    out_turned(SA, u, p)
                elif what == "choose":
                    act.wait_ge(r0["top"], p * 2 + u + 1)
                    act.activation(ex[:], lg[:], ACT.Exp, bias=nmax[:]).then_inc(r0["ex"], 1)

            two_streams(act, A_HEAD, A_STEPS, LENGTH_A, LAG_A, step_a)

            def gate_expert(e, u):
                act.wait_ge(m0["h_ps"], e + 1)
                act.activation(sg[:, u % 2, :], bank[u % 2][0:I0, 0:128], ACT.Silu).then_inc(m0["sg"], 1)

            with act.Fori(0, E0 // RING) as i:
                for u in range(RING):
                    gate_expert(i * RING + u, u)

            def step_b(u, p, what, a=None, n=None):
                sg_, s = stream[u], SB[u]
                if what == "turn":
                    if a == 2:
                        s.wait(act, "xnt_ps", p, 3)
                        copy(xT6[:, :, bass.ds(p * 2 + u, 1), :].rearrange("p c a t -> p c (a t)"),
                             PD[u][:, 0:D].rearrange("p (c t) -> p c t", c=KC))
                    turned(SB, u, p, a + 1)
                    if a == 1:
                        s.wait(act, "kt_ps", p, 1)
                        copy(kvT[u][:], PC[u][0:C, 0:128]).then_inc(sg_["kt_sb"], 1)
                elif what in ("kq", "q2", "st"):
                    attention(SB, u, p, what, a, n)
                elif what == "out":
                    out_turned(SB, u, p)
                elif what == "keys":
                    n = a
                    s.wait(act, "qk_ps", p, n + 1)
                    copy(qkT(u, n), (PC, PD)[n % 2][u][0:C, :].rearrange("p (h t) -> p h t", h=4)) \
                        .then_inc(sg_["qk_sb"], 1)
                elif what == "xmax":
                    s.wait(act, "nm_ps", p, 1)
                    copy(nmT[u][:], PD[u][0:HX, 0:128]).then_inc(sg_["nm_sb"], 1)
                elif what == "xst" and a < XJ:
                    n = a
                    s.wait(act, "st_ps", p, 4 + n + 1)
                    if n >= 2:
                        s.wait(act, "pv_ps", p, 4 + n - 1)
                    act.activation(PT[u][:, n % 2], (PA, PB)[n % 2][u][:].rearrange("p (g t) -> p g t", g=4), ACT.Exp) \
                        .then_inc(sg_["st_exp"], 1)
                elif what == "xct":
                    n = a
                    s.wait(act, "ct_ps", p, n + 1)
                    copy(cT[u][:, 4 * n:4 * n + 4, :], (PC, PD)[n][u][:].rearrange("p (h t) -> p h t", h=4)) \
                        .then_inc(sg_["ct_sb"], 1)
                elif what == "choose":
                    act.wait_ge(r1["top"], p * 2 + u + 1)
                    act.activation(ex[:, 0:E1], lgp[:, 0:E1], ACT.Exp, bias=nmax[:]).then_inc(r1["ex"], 1)

            two_streams(act, B_HEAD, B_STEPS, LENGTH_B, LAG_B, step_b)

            for c in range(KC):
                copy(xh[c][:], xT6[:, c]).then_inc(f1["x_high"], 1)

            def weights_high(u, turn):
                act.wait_ge(f1[f"wl{u}"], turn * 16 + 16)
                copy(wh[:, u], wf[:, u]).then_inc(f1["w_high"], 1)

            def ffn_turn(i, last=False):
                for u in range(2):
                    for th in range(2):
                        for f in range(2):
                            step = i * 8 + u * 4 + th * 2 + f
                            act.wait_ge(f1["g_ps"], step + 1)
                            act.wait_ge(f1["free"], step + 1)
                            act.activation(sgf[:, f, :], bank[2 * f][0:FH, :], ACT.Silu).then_inc(f1["sg"], 1)
                            if th == 0 and f == 0 and not (last and u == 1):
                                weights_high(1 - u, i + u)

            weights_high(0, 0)
            with act.Fori(0, NF // 2 - 1) as i:
                ffn_turn(i)
            ffn_turn(NF // 2 - 1, last=True)

        @block.tensor
        def _(pe):
            def norm_turn(s, u, p, k):
                s[u].wait(pe, "xn", p, k)
                for c in range(KC):
                    last = pe.transpose(PD[u][:, 128 * c:128 * c + 128], xn[u][:, 128 * c:128 * c + 128], ident[:])
                last.then_inc(stream[u]["xnt_ps"], 1)

            def rows_times(dst, lhs, w, lo, n):
                for c in range(KC):
                    last = pe.matmul(dst, lhs[:, c, :], w[:, c, lo:lo + n], start=(c == 0), stop=(c == KC - 1))
                return last

            def attention(s, u, p, what, a, n, queries, keys, values):
                off, sg_, s = OFF[a], stream[u], s[u]
                kflat = keys.rearrange("p (g r) c -> p g (r c)", r=a.strips)
                qflat = queries.rearrange("p (g r) c -> p g (r c)", r=a.strips)
                jobs = len(a.jobs)
                if what == "kq":
                    if n == 0:
                        s.wait(pe, "qkv_sb", p, 2 if a is X0 else 1)
                    if n >= 2:
                        s.wait(pe, "kq_sb", p, off["kq"] + n - 1)
                    src, g0, g = (kflat, 4 * n, min(4, a.kgroups)) if n < a.kbanks else (qflat, 4 * (n - a.kbanks), 4)
                    for g1 in range(g):
                        last = pe.transpose((PC, PD)[n % 2][u][:, 128 * g1:128 * g1 + 128], src[:, g0 + g1, :], ident[:])
                    last.then_inc(sg_["kq_ps"], 1)
                elif what == "s":
                    half, row = a.jobs[n]
                    lo, hi = a.width * row, a.width * row + a.top
                    if n == 0:
                        s.wait(pe, "kq_sb", p, off["kq"] + a.banks)
                    if n >= 2:
                        s.wait(pe, "s_max", p, off["s"] + n - 1)
                    dst = (PA, PB)[n % 2][u]
                    if a.causal:
                        pe.matmul(dst[:].rearrange("p (g t) -> p g t", g=4), identb[:],
                                  maskq[:].unsqueeze(1).broadcast_to([128, 4, 128]), start=True, stop=True,
                                  skip_group_check=True)
                    for g in range(4):
                        kg = half if a.shared else 4 * half + g
                        last = pe.matmul(dst[:, 128 * g:128 * g + 128], qT[u][lo:hi, 4 * half + g, :], kT[u][lo:hi, kg, :],
                                         start=not a.causal, stop=True, skip_group_check=True)
                    last.then_inc(sg_["s_ps"], 1)
                elif what == "q2":
                    s.wait(pe, "top", p, off["q2"] + n + 1)
                    if n == 1:
                        s.wait(pe, "q2_sb", p, off["q2"] + 1)
                    for g in range(4):
                        last = pe.transpose(PD[u][:, 128 * g:128 * g + 128], qflat[:, 4 * n + g, :], ident[:])
                    last.then_inc(sg_["q2_ps"], 1)
                else:
                    if n < jobs:
                        half, row = a.jobs[n]
                        lo, hi = a.width * row, a.width * row + a.rows
                        if row == 0:
                            s.wait(pe, "q2_sb", p, off["q2"] + half + 1)
                        if n < 2:
                            s.wait(pe, "s_max", p, off["s"] + jobs - 1 + n)
                        else:
                            s.wait(pe, "st_exp", p, off["s"] + n - 1)
                        dst = (PA, PB)[n % 2][u]
                        if a.causal:
                            pe.matmul(dst[:].rearrange("p (g t) -> p g t", g=4), identb[:],
                                      maskk[:].unsqueeze(1).broadcast_to([128, 4, 128]), start=True, stop=True,
                                      skip_group_check=True)
                        if a.shared:
                            last = pe.matmul(dst[:].rearrange("p (g t) -> p g t", g=4), kT[u][lo:hi, half, :],
                                             qT[u][lo:hi, 4 * half:4 * half + 4, :], start=not a.causal, stop=True,
                                             skip_group_check=True)
                        else:
                            for g in range(4):
                                last = pe.matmul(dst[:, 128 * g:128 * g + 128], kT[u][lo:hi, 4 * half + g, :],
                                                 qT[u][lo:hi, 4 * half + g, :], start=not a.causal, stop=True,
                                                 skip_group_check=True)
                        last.then_inc(sg_["st_ps"], 1)
                    if n >= 1:
                        n = n - 1
                        half, row = a.jobs[n]
                        w = a.dim + 1
                        s.wait(pe, "st_exp", p, off["s"] + n + 1)
                        for g in range(4):
                            h = a.head(half, row, g)
                            kv = h // 4 if a.shared else h
                            last = pe.matmul(PC[u][:, w * h:w * h + w], PT[u][:, n % 2, g, :], values[:, kv, :],
                                             start=True, stop=True, skip_group_check=True)
                        last.then_inc(sg_["pv_ps"], 1)

            def out_turn(s, u, p):
                s[u].wait(pe, "on_sb", p, 1)
                for c in range(KC):
                    last = pe.transpose(PD[u][:, 128 * c:128 * c + 128], on[u][:, 128 * c:128 * c + 128], ident[:])
                last.then_inc(stream[u]["ot_ps"], 1)

            def project(s, u, p, w):
                s[u].wait(pe, "ot_sb", p, 1)
                rows_times(PA[u][:, 0:D], onT[u], w, 0, D).then_inc(stream[u]["pr_ps"], 1)

            pe.wait_ge(loaded["const"], 16 * 4)
            pe.wait_ge(ready["masks"], 3)
            pe.wait_ge(loaded["w0"], 16 * N_W0)
            pe.wait_ge(loaded["w1"], 16 * N_W1)
            pe.sem_inc(fold["free"], 2)

            def fold_pair(hp, v, turn):
                pe.wait_ge(fold[f"ld{v}"], turn * 96 + 96)
                for u in range(2):
                    if not (isinstance(hp, int) and hp == 0):
                        pe.wait_ge(fold["sb"], hp * 2 + u - 1)
                    for c in range(KC):
                        pe.matmul(bank[3 * u][:, QX * c:QX * c + QX], fq[v][:, u, 128 * c:128 * c + 128], fc[v][:, u, :],
                                  start=True, stop=True)
                    for half in range(2):
                        pe.matmul(bank[3 * u + 1][0:HQ, C * half:C * half + C], fr[v][:, u, HQ * half:HQ * half + HQ],
                                  fk[v][:, u, :], start=True, stop=True)
                    last = pe.matmul(bank[3 * u + 2][64 * u:64 * u + 64, 0:D], fv[v][:, u, :], fo[v][:, u, :],
                                     start=True, stop=True)
                    last.then_inc(fold["ps"], 1)
                pe.wait_ge(fold["ps"], hp * 2 + 2)
                pe.sem_inc(fold["free"], 1)

            for v in range(2):
                fold_pair(v, v, 0)
            with pe.Fori(1, HX // 4) as i:
                for v in range(2):
                    fold_pair(i * 2 + v, v, i)
            pe.wait_ge(fold["sb"], HX)

            def step_a(u, p, what, a=None, n=None):
                if what == "turn":
                    norm_turn(SA, u, p, a + 1)
                elif what == "qkv":
                    SA[u].wait(pe, "xnt_sb", p, 1)
                    pe.wait_ge(r0[f"free{u}"], p + 1)
                    rows_times(PA[u][:], xnT[u], w_qkv0, 0, 2 * D)
                    rows_times(PB[u][:, 0:D], xnT[u], w_qkv0, 2 * D, D).then_inc(stream[u]["qkv_ps"], 1)
                elif what in ("kq", "s", "q2", "st"):
                    attention(SA, u, p, what, a, n, qpad[u], kpad[u] if a is L0 else kpadx[u][:],
                              vx[u] if a is L0 else vc[u])
                elif what == "out":
                    out_turn(SA, u, p)
                elif what == "proj":
                    project(SA, u, p, w_pr0)
                elif what == "logits":
                    SA[u].wait(pe, "xnt_sb", p, 2)
                    rows_times(PA[u][:, 0:E0], xnT[u], w_rt0, 0, E0).then_inc(r0["lg_ps"], 1)
                elif what == "place":
                    pe.wait_ge(r0["msk"], p * 2 + u + 1)
                    pe.matmul(PB[u][:, 0:E0], tri[:], msk[:], start=True, stop=False)
                    pe.matmul(PB[u][:, 0:E0], ones[:], macc[:], start=False, stop=True).then_inc(r0["pos_ps"], 1)

            two_streams(pe, A_HEAD, A_STEPS, LENGTH_A, LAG_A, step_a)

            def turn_expert(e, u, i):
                v = u % 2
                pe.wait_ge(m0[f"xg{u % RING}"], (i + u // RING) * 16 + 16)
                if not (isinstance(e, int) and e < 2):
                    pe.wait_ge(m0["xt_sb"], e - 1)
                for c in range(KC):
                    last = pe.transpose(bank[6 + v][:, 128 * c:128 * c + 128], xe[:, u % RING, 128 * c:128 * c + 128], ident[:])
                last.then_inc(m0["xt_ps"], 1)

            def inner(e, u, i):
                v = u % 2
                pe.wait_ge(m0["xt_sb"], e + 1)
                pe.sem_inc(m0["credit"], 1)
                pe.wait_ge(m0[f"wl{u}"], i * 32 + 32)
                for k in range(2):
                    for c in range(KC):
                        last = pe.matmul(bank[v][0:I0, 128 * k:128 * k + 128], wgu[:, u, c, I0 * k:I0 * k + I0],
                                         xeT[:, v, c, :], start=(c == 0), stop=(c == KC - 1))
                last.then_inc(m0["h_ps"], 1)

            def outer(e, u):
                pe.wait_ge(m0["a_sb"], e + 1)
                if not (isinstance(e, int) and e < 2):
                    pe.wait_ge(m0["y_sb"], e - 1)
                pe.matmul(bank[2 + u % 2][:, 0:D], aT[:, u % 2, :], wdn[:, u % RING, :], start=True, stop=True) \
                    .then_inc(m0["y_ps"], 1)

            def experts(i):
                for u in range(RING):
                    first, last = isinstance(i, int) and i == 0, isinstance(i, int) and i == E0 // RING - 1
                    e = i * RING + u
                    if not (last and u == RING - 1):
                        turn_expert(e + 1, u + 1, i)
                    inner(e, u, i)
                    if not (first and u == 0):
                        outer(e - 1, (u - 1) % RING)

            turn_expert(0, 0, 0)
            experts(0)
            with pe.Fori(1, E0 // RING - 1) as i:
                experts(i)
            experts(E0 // RING - 1)
            outer(E0 - 1, RING - 1)

            def step_b(u, p, what, a=None, n=None):
                s, sg_ = SB[u], stream[u]
                if what == "turn":
                    norm_turn(SB, u, p, a + 1)
                    if a == 1:
                        s.wait(pe, "kv_sb", p, 1)
                        pe.transpose(PC[u][:, 0:128], kvr[u][:], ident[:]).then_inc(sg_["kt_ps"], 1)
                elif what == "qkv":
                    s.wait(pe, "xnt_sb", p, 1)
                    rows_times(PA[u][:, 0:384], xnT[u], w_qkv1, 0, 384).then_inc(sg_["qkv_ps"], 1)
                elif what in ("kq", "s", "q2", "st"):
                    attention(SB, u, p, what, a, n, qpad1[u], kpad1[u][:], vx1[u])
                elif what == "out":
                    out_turn(SB, u, p)
                elif what == "proj":
                    project(SB, u, p, w_pr1)
                elif what == "keys":
                    s.wait(pe, "rsum", p, 2 * a + 2)
                    if a == 0:
                        s.wait(pe, "kt_sb", p, 1)
                    if a >= 2:
                        s.wait(pe, "qk_sb", p, a - 1)
                    for h in range(4):
                        for k in range(2):
                            last = pe.matmul((PC, PD)[a % 2][u][0:C, 128 * h:128 * h + 128], wqk[:, k, 4 * a + h, :],
                                             rp[u][:, 2 * k, h, :], start=(k == 0), stop=(k == 1))
                    last.then_inc(sg_["qk_ps"], 1)
                elif what == "big":
                    half = n
                    if a == 0 and half == 0:
                        s.wait(pe, "xnt_sb", p, 2)
                    elif a >= 1:
                        s.wait(pe, "rope", p, 2 * a - 1 + half)
                    for h in range(4):
                        lo = (4 * a + h) * QX + half * HQ
                        for c in range(KC):
                            last = pe.matmul((PA, PB)[half][u][0:HQ, 128 * h:128 * h + 128],
                                             wqc[:, c, lo:lo + HQ], xnT[u][:, c, :], start=(c == 0), stop=(c == KC - 1))
                    last.then_inc(sg_["qb_ps"], 1)
                elif what == "xs":
                    n = a
                    s.wait(pe, "qk_sb", p, n + 1)
                    if n >= 2:
                        s.wait(pe, "s_max", p, 4 + n - 1)
                    elif n == 0:
                        s.wait(pe, "rope", p, 2 * XJ)
                    for h in range(4):
                        last = pe.matmul((PA, PB)[n % 2][u][:, 128 * h:128 * h + 128], qkT(u, n)[:, h, :], kvT[u][:],
                                         start=True, stop=True)
                    last.then_inc(sg_["s_ps"], 1)
                elif what == "xmax":
                    s.wait(pe, "s_max", p, 4 + XJ)
                    pe.transpose(PD[u][0:HX, 0:128], nmx[u][:, 0:HX], ident[:]).then_inc(sg_["nm_ps"], 1)
                elif what == "xst":
                    if a < XJ:
                        n = a
                        if n == 0:
                            s.wait(pe, "nm_sb", p, 1)
                        if n >= 2:
                            s.wait(pe, "st_exp", p, 4 + n - 1)
                        dst = (PA, PB)[n % 2][u]
                        pe.matmul(dst[:].rearrange("p (g t) -> p g t", g=4), kvT[u][:], qkT(u, n),
                                  start=True, stop=True, skip_group_check=True)
                        for h in range(4):
                            last = pe.matmul(dst[:, 128 * h:128 * h + 128], ident[0:HX, 4 * n + h:4 * n + h + 1].broadcast_to([HX, 128]), nmT[u][:],
                                             start=False, stop=True, skip_group_check=True)
                        last.then_inc(sg_["st_ps"], 1)
                    if a >= 1:
                        n = a - 1
                        s.wait(pe, "st_exp", p, 4 + n + 1)
                        if n >= 2:
                            s.wait(pe, "cn_sb", p, n - 1)
                        for h in range(4):
                            last = pe.matmul((PC, PD)[n % 2][u][:, (C + 1) * h:(C + 1) * (h + 1)], PT[u][:, n % 2, h, :],
                                             kvr[u][:, 0:C + 1], start=True, stop=True)
                        last.then_inc(sg_["pv_ps"], 1)
                elif what == "xct":
                    n = a
                    s.wait(pe, "cn_sb", p, XJ)
                    for h in range(4):
                        last = pe.transpose((PC, PD)[n][u][:, 128 * h:128 * h + 128],
                                            cn[u][:, 8 * n + 2 * h:8 * n + 2 * h + 2, :].rearrange("p h c -> p (h c)"), ident[:])
                    last.then_inc(sg_["ct_ps"], 1)
                elif what == "xproj":
                    s.wait(pe, "ct_sb", p, 2)
                    for n in range(HX // 2):
                        last = pe.matmul(PA[u][:, 0:D], cT[u][:, n, :], weff[:, n, :], start=(n == 0), stop=(n == HX // 2 - 1))
                    last.then_inc(sg_["pr_ps"], 1)
                elif what == "logits":
                    s.wait(pe, "xnt_sb", p, 3)
                    rows_times(PB[u][:, 0:E1], xnT[u], w_rt1, 0, E1).then_inc(r1["lg_ps"], 1)

            two_streams(pe, B_HEAD, B_STEPS, LENGTH_B, LAG_B, step_b)

            pe.wait_ge(r1["done"], B)
            pe.wait_ge(f1["x_low"], KC)

            def ffn_inner(step, u, th, f):
                if not (isinstance(step, int) and step == 0):
                    pe.wait_ge(f1["a_sb"], step * 2 + f - 1)
                for k in range(2):
                    lo = I1 * k + FH * f
                    for c in range(KC):
                        for n, (w, rows) in enumerate(((wh, xh), (wh, xl), (wl, xh))):
                            last = pe.matmul(bank[2 * f + k][0:FH, :], w[:, u, c, lo:lo + FH],
                                             rows[c][:, 4 * th:4 * th + 4, :].rearrange("p b t -> p (b t)"),
                                             start=(c == 0 and n == 0), stop=(c == KC - 1 and n == 2))
                last.then_inc(f1["g_ps"], 1)

            def ffn_outer(step, u, th, quarters):
                pe.wait_ge(f1["a_sb"], step * 2 + 2)
                for q in quarters:
                    if not (isinstance(step, int) and step == 0):
                        pe.wait_ge(f1["y_sb"], step * 4 + q - 3)
                    for f in range(2):
                        last = pe.matmul(bank[4 + q][:, 0:D], af[th][:, f, 128 * q:128 * q + 128], wfd[:, u, f, :],
                                         start=(f == 0), stop=(f == 1))
                    last.then_inc(f1["y_ps"], 1)

            def ffn_turn(i):
                for u in range(2):
                    pe.wait_ge(f1["w_low"], i * 2 + u + 1)
                    for th in range(2):
                        step = i * 4 + u * 2 + th
                        for f in range(2):
                            ffn_inner(step, u, th, f)
                            if th == 1 and f == 0:
                                pe.wait_ge(f1[f"wd{u}"], i * 16 + 16)
                            if not (isinstance(i, int) and step == 0):
                                ffn_outer(step - 1, u if th else 1 - u, 1 - th, (2 * f, 2 * f + 1))

            ffn_turn(0)
            with pe.Fori(1, NF // 2) as i:
                ffn_turn(i)
            ffn_outer(NF * 2 - 1, 1, 1, range(4))

        @block.vector
        def _(dve):
            chain = Chain(dve, chains["dve"])

            def norm(s, u, p, k):
                chain(dve.bn_stats(stats[u][:], at(x, u, p)))
                dve.bn_aggr(mv[u][:], stats[u][:]).then_inc(stream[u]["stats"], 1)
                s[u].wait(dve, "rstd", p, k)
                return (at(x, u, p), mv[u][:, 0:1], rstd[u][:], ALU.subtract, ALU.mult)

            def split(dst, src, dim, heads, highs, low, last_sem=None):
                step = highs[1] - highs[0]
                for at_ in highs:
                    high = dve.tensor_copy(dst[:, :, at_:at_ + dim].bitcast(F32R), src)
                chain(high)
                return dve.tensor_tensor(dst[:, :, low:low + dim], src, dst[:, :, highs[0]:highs[0] + dim], ALU.subtract)

            def maxima(s, u, p, a, n):
                half, row = a.jobs[n]
                off, w = OFF[a], a.strips
                nm = nmx[u][:, 0:8 * w].rearrange("p (g r) -> p g r", r=w)
                s[u].wait(dve, "s_ps", p, off["s"] + n + 1)
                m = dve.tensor_reduce(nm[:, 4 * half:4 * half + 4, row],
                                      (PA, PB)[n % 2][u][:].rearrange("p (g t) -> p g t", g=4), AX.X, ALU.max,
                                      negate=True)
                m.then_inc(stream[u]["s_max"], 1)
                if row == w - 1:
                    s[u].wait(dve, "s_max", p, off["s"] + n + 1)
                    q = (qpad1 if a is L1 else qpad)[u][:, 4 * w * half:4 * w * (half + 1), :]
                    m = nmx[u][:, 4 * w * half:4 * w * (half + 1)]
                    chain(dve.tensor_copy(q[:, :, a.top].bitcast(F32R), m))
                    dve.tensor_tensor(q[:, :, a.top + 1], m, q[:, :, a.top], ALU.subtract) \
                        .then_inc(stream[u]["top"], 1)

            def weighted(s, u, p, a, dst):
                w = a.dim + 1
                pv = PC[u][:, 0:w * a.heads].rearrange("p (h w) -> p h w", w=w)
                s[u].wait(dve, "pv_ps", p, OFF[a]["s"] + len(a.jobs))
                chain(dve.reciprocal(rden[u][:, 0:a.heads], pv[:, :, a.dim]))
                return dve.tensor_tensor(dst.rearrange("p (h d) -> p h d", d=a.dim), pv[:, :, 0:a.dim],
                                         rden[u][:, 0:a.heads].unsqueeze(2).broadcast_to([128, a.heads, a.dim]),
                                         ALU.mult)

            dve.wait_ge(loaded["const"], 16 * 4)
            for dst, src in ((identb, ident), (maskq, never), (maskk, neverT)):
                dve.tensor_copy(dst[:], src[:]).then_inc(ready["masks"], 1)
            for tile in (*qarea, *karea, *kpadx, *kpad1, *vx, *vc, zrow, macc, *kvr):
                chain(dve.memset(tile[:], 0.0))
            for u in range(2):
                chain(dve.memset(qpad[u][:, :, L0.bias:L0.bias + 2], 1.0))
                chain(dve.memset(kpad[u][:, :, L0.top:L0.top + 2], 1.0))
                chain(dve.memset(kpadx[u][:, :, X0.top:X0.top + 2], 1.0))
                chain(dve.memset(kpad1[u][:, :, L1.top:L1.top + 2], 1.0))
                ah, al = kpad[u][:, :, L0.bias], kpad[u][:, :, L0.bias + 1]
                chain(dve.tensor_copy(ah.bitcast(F32R), alibi[:].broadcast_to([128, 32])))
                chain(dve.tensor_tensor(al, alibi[:].broadcast_to([128, 32]), ah, ALU.subtract))
                chain(dve.memset(vx[u][:, :, 8:9], 1.0))
                chain(dve.memset(vc[u][:, :, 8:9], 1.0))
                chain(dve.memset(vx1[u][:, :, 16:17], 1.0))
                chain(dve.memset(kvr[u][:, C:C + 1], 1.0))
            chain(dve.memset(dw[:, :, E1:NF], 1.0))
            chain(dve.memset(lgp[:, E1:E1 + 8], -3e38))
            dve.memset(fillt[:], NTOK).then_inc(ready["pads"], 1)
            dve.wait_ge(ready["pads"], 1)
            dve.wait_ge(loaded["w1"], 16 * N_W1)
            dve.wait_ge(loaded["x"], 16)
            dve.wait_ge(loaded["ctx"], 16)
            dve.wait_ge(loaded["w0"], 16 * N_W0)

            def heads(ap, dim):
                return ap.rearrange("p (h c) -> p h c", c=dim)

            def step_a(u, p, what, a=None, n=None):
                s = SA
                if what == "prenorm":
                    if next_batch(p) is None:
                        return
                    ln = norm(s, u, next_batch(p), 1)
                    if not (isinstance(p, int) and p == -1):
                        dve.wait_ge(r0["xn_st"], (p * 2 + u + 1) * 16)
                    dve.tensor_scalar(xn[u][:], *ln).then_inc(stream[u]["xn"], 1)
                elif what == "qkv":
                    s[u].wait(dve, "qkv_ps", p, 1)
                    chain(dve.tensor_tensor(qk0[u], PA[u][:], b_qkv0[:, 0:2 * D], ALU.add))
                    dve.tensor_tensor(vx[u][:, :, 0:8], heads(PB[u][:, 0:D], 8), heads(b_qkv0[:, 2 * D:3 * D], 8), ALU.add)
                    chain(split(kpad[u], heads(qk0[u][:, D:2 * D], 8), 8, 32, (0, 16), 8))
                    split(qpad[u], heads(qk0[u][:, 0:D], 8), 8, 32, (0, 8), 16).then_inc(stream[u]["qkv_sb"], 1)
                elif what == "s":
                    maxima(s, u, p, a, n)
                elif what == "out":
                    weighted(s, u, p, a=L0, dst=on[u][:]).then_inc(stream[u]["on_sb"], 1)
                elif what == "proj":
                    s[u].wait(dve, "pr_ps", p, 1)
                    chain(dve.tensor_tensor(tmp[u][:], PA[u][:, 0:D], b_pr0[:], ALU.add))
                    chain(dve.tensor_tensor(at(x, u, p), at(x, u, p), tmp[u][:], ALU.add))
                elif what == "norm":
                    cb = heads(at(ctxt, u, p), 8)
                    chain(split(kpadx[u], cb, 8, 8, (0, 16), 8))
                    chain(dve.tensor_copy(vc[u][:, :, 0:8], cb))
                    chain(dve.tensor_scalar(xn[u][:], *norm(s, u, p, 2)))
                    xv = xn[u][:].rearrange("p (h r g c) -> p h r g c", h=2, r=4, g=4)
                    qv = qpad[u].rearrange("p (h g r) c -> p h g r c", h=2, g=4)
                    for half in range(2):
                        src, dst = xv[:, half].rearrange("p r g c -> p g r c"), qv[:, half]
                        dve.tensor_copy(dst[:, :, :, 0:8].bitcast(F32R), src)
                        chain(dve.tensor_copy(dst[:, :, :, 8:16].bitcast(F32R), src))
                        last = dve.tensor_tensor(dst[:, :, :, 16:24], src, dst[:, :, :, 0:8], ALU.subtract)
                    last.then_inc(stream[u]["qkv_sb"], 1)
                elif what == "xout":
                    chain(weighted(s, u, p, X0, tmp[u][:]))
                    chain(dve.tensor_tensor(at(x, u, p), at(x, u, p), tmp[u][:], ALU.add))
                elif what == "rnorm":
                    dve.tensor_scalar(xn[u][:], *norm(s, u, p, 3)).then_inc(stream[u]["xn"], 1)
                elif what == "choose":
                    dve.wait_ge(r0["lg_ps"], p * 2 + u + 1)
                    chain(dve.tensor_copy(lg[:], PA[u][:, 0:E0]))
                    chain(dve.max(top8[:], lg[:]))
                    dve.tensor_scalar(nmax[:], top8[:, 0:1], -1.0, None, ALU.mult).then_inc(r0["top"], 1)
                    chain(dve.match_replace(lg2[:], top8[:], lg[:], -3e38))
                    dve.tensor_tensor(msk[:], lg[:], lg2[:], ALU.not_equal).then_inc(r0["msk"], 1)
                elif what == "weigh":
                    dve.wait_ge(r0["msk"], p * 2 + u + 1)
                    dve.wait_ge(r0["ex"], p * 2 + u + 1)
                    chain(dve.tensor_tensor(wk[:], ex[:], msk[:], ALU.mult))
                    chain(dve.tensor_reduce(den[:], wk[:], AX.X, ALU.add))
                    chain(dve.reciprocal(den[:], den[:]))
                    dve.wait_ge(r0["pos_ps"], p * 2 + u + 1)
                    chain(dve.scalar_tensor_tensor(keep[:], PB[u][:, 0:E0], float(CAP), msk[:], ALU.is_lt, ALU.mult))
                    chain(dve.scalar_tensor_tensor(slm[:], PB[u][:, 0:E0], float(E0), eplus1[:], ALU.mult, ALU.add))
                    dve.sem_inc(r0[f"free{u}"], 1)
                    chain(dve.tensor_tensor(slm[:], slm[:], keep[:], ALU.mult))
                    chain(dve.max(s8[:], slm[:]))
                    chain(dve.tensor_scalar(zz[:], s8[:], 0.0, float(NSLOT + 1), ALU.is_equal, ALU.mult))
                    dve.scalar_tensor_tensor(at(idx8, u, p), s8[:], -1.0, zz[:], ALU.add, ALU.add).then_inc(r0["idx"], 1)
                    chain(dve.scalar_tensor_tensor(wk[:], wk[:], den[:], keep[:], ALU.mult, ALU.mult))
                    chain(dve.tensor_tensor(eq[:], slm[:].unsqueeze(1).broadcast_to([128, 8, E0]),
                                            s8[:].unsqueeze(2).broadcast_to([128, 8, E0]), ALU.is_equal))
                    chain(dve.tensor_tensor(eq[:], eq[:], wk[:].unsqueeze(1).broadcast_to([128, 8, E0]), ALU.mult))
                    chain(dve.tensor_reduce(at(w8, u, p), eq[:], AX.X, ALU.add))
                    chain(dve.tensor_tensor(macc[:], macc[:], msk[:], ALU.add))

            for u in range(2):
                dve.sem_inc(r0[f"free{u}"], 1)
            two_streams(dve, A_HEAD, A_STEPS, LENGTH_A, LAG_A, step_a, chain.turn)

            for u in range(RING):
                dve.sem_inc(m0[f"yst{u}"], 16)

            def turned_expert(e, u):
                dve.wait_ge(m0["xt_ps"], e + 1)
                dve.tensor_copy(xeT[:, u % 2], bank[6 + u % 2][:, 0:D].rearrange("p (c t) -> p c t", c=KC)).then_inc(m0["xt_sb"], 1)

            def gated(e, u):
                dve.wait_ge(m0["sg"], e + 1)
                dve.tensor_tensor(aT[:, u % 2, :], sg[:, u % 2, :], bank[u % 2][0:I0, 128:256], ALU.mult) \
                    .then_inc(m0["a_sb"], 1)

            def result(e, u, i):
                dve.wait_ge(m0["y_ps"], e + 1)
                dve.wait_ge(m0[f"yst{u}"], i * 16 + 16)
                dve.tensor_copy(ye[:, u, :], bank[2 + u % 2][:, 0:D]).then_inc(m0["y_sb"], 1)

            turned_expert(0, 0)
            for u in range(RING):
                turned_expert(u + 1, u + 1)
                gated(u, u)
                if u >= 1:
                    result(u - 1, u - 1, 0)
            with dve.Fori(1, E0 // RING - 1) as i:
                for u in range(RING):
                    e = i * RING + u
                    turned_expert(e + 1, u + 1)
                    gated(e, u)
                    result(e - 1, (u - 1) % RING, i if u >= 1 else i - 1)
            for u in range(RING):
                e = E0 - RING + u
                if u < RING - 1:
                    turned_expert(e + 1, u + 1)
                gated(e, u)
                result(e - 1, (u - 1) % RING, E0 // RING - 1 if u >= 1 else E0 // RING - 2)
            result(E0 - 1, RING - 1, E0 // RING - 1)

            def rotate(u, p, n, half):
                SB[u].wait(dve, "qb_ps", p, 2 * n + half + 1)
                src = (PA, PB)[half][u][0:HQ, :].rearrange("p (h t) -> p h t", h=4)
                for k, tab in (((0, cosq[:, 0]), (3, sinq[:, 1])), ((2, cosq[:, 1]), (1, sinq[:, 0])))[half]:
                    last = dve.tensor_tensor(rp[u][:, k], src, tab.unsqueeze(1).broadcast_to([HQ, 4, 128]), ALU.mult)
                last.then_inc(stream[u]["rope"], 1)

            def step_b(u, p, what, a=None, n=None):
                s, sg_ = SB, stream[u]
                if what == "sum":
                    q = next_batch(p)
                    if q is None:
                        return
                    if a == 0:
                        chain(dve.tensor_copy(w8c[u][:], at(w8, u, q)))
                        dve.wait_ge(c0[f"yg{u}"], q * (16 * TOP0) + 16 * TOP0)
                    chain(dve.scalar_tensor_tensor(at(x, u, q), yg[u][:, a, :], w8c[u][:, a:a + 1], at(x, u, q), ALU.mult,
                                                   ALU.add))
                    if a == TOP0 - 1:
                        dve.sem_inc(c0[f"credit{u}"], 1)
                elif what == "prenorm":
                    if next_batch(p) is None:
                        return
                    ln = norm(s, u, next_batch(p), 1)
                    if not (isinstance(p, int) and p == -1):
                        s[u].wait(dve, "xnt_ps", p, 3)
                    dve.tensor_scalar(xn[u][:], *ln).then_inc(sg_["xn"], 1)
                elif what == "qkv":
                    s[u].wait(dve, "qkv_ps", p, 1)
                    chain(dve.tensor_tensor(qk1, PA[u][:, 0:320], b_qkv1[:, 0:320], ALU.add))
                    dve.tensor_tensor(vx1[u][:, :, 0:16], heads(PA[u][:, 320:384], 16), heads(b_qkv1[:, 320:384], 16), ALU.add)
                    dve.tensor_tensor(heads(ra1, 16), heads(qk1, 16),
                                      cos1[:].unsqueeze(1).broadcast_to([128, 20, 16]), ALU.mult)
                    pairs = qk1.rearrange("p (h c t) -> p h c t", c=8, t=2)
                    rpairs = rb1.rearrange("p (h c t) -> p h c t", c=8, t=2)
                    spairs = sin1[:].rearrange("p (c t) -> p c t", t=2)
                    dve.tensor_tensor(rpairs[:, :, :, 0], pairs[:, :, :, 1],
                                      spairs[:, :, 0].unsqueeze(1).broadcast_to([128, 20, 8]), ALU.mult)
                    chain(dve.tensor_tensor(rpairs[:, :, :, 1], pairs[:, :, :, 0],
                                            spairs[:, :, 1].unsqueeze(1).broadcast_to([128, 20, 8]), ALU.mult))
                    chain(dve.tensor_tensor(qk1, ra1, rb1, ALU.add))
                    chain(split(kpad1[u], heads(qk1[:, 256:320], 16), 16, 4, (0, 32), 16))
                    split(qpad1[u], heads(qk1[:, 0:256], 16), 16, 16, (0, 16), 32).then_inc(sg_["qkv_sb"], 1)
                elif what == "s":
                    maxima(s, u, p, a, n)
                elif what == "out":
                    weighted(s, u, p, a=L1, dst=on[u][:]).then_inc(sg_["on_sb"], 1)
                elif what == "proj":
                    s[u].wait(dve, "pr_ps", p, 1)
                    chain(dve.tensor_tensor(tmp[u][:], PA[u][:, 0:D], b_pr1[:], ALU.add))
                    chain(dve.tensor_tensor(at(x, u, p), at(x, u, p), tmp[u][:], ALU.add))
                elif what == "xnorm":
                    dve.tensor_scalar(xn[u][:], *norm(s, u, p, 2)).then_inc(sg_["xn"], 1)
                    cb = at(ctxt, u, p)
                    dve.tensor_tensor(kvr[u][:, 0:C], cb, cosk[:], ALU.mult)
                    dve.tensor_tensor(ka[:, 0:C // 2], cb[:, C // 2:C], sink[:, 0:C // 2], ALU.mult)
                    chain(dve.tensor_tensor(ka[:, C // 2:C], cb[:, 0:C // 2], sink[:, C // 2:C], ALU.mult))
                    dve.tensor_tensor(kvr[u][:, 0:C], kvr[u][:, 0:C], ka, ALU.add).then_inc(sg_["kv_sb"], 1)
                elif what == "big" and (n == 1 or a == 0):
                    rotate(u, p, a, n)
                elif what == "keys" and a + 1 < XJ:
                    s[u].wait(dve, "qk_ps", p, a + 1)
                    rotate(u, p, a + 1, 0)
                elif what == "xs":
                    n = a
                    s[u].wait(dve, "s_ps", p, 4 + n + 1)
                    dve.tensor_reduce(nmx[u][:, 4 * n:4 * n + 4], (PA, PB)[n % 2][u][:].rearrange("p (g t) -> p g t", g=4),
                                      AX.X, ALU.max, negate=True).then_inc(sg_["s_max"], 1)
                elif what == "xst" and a >= 1:
                    n = a - 1
                    s[u].wait(dve, "pv_ps", p, 4 + n + 1)
                    pv = (PC, PD)[n % 2][u][:, 0:4 * (C + 1)].rearrange("p (h w) -> p h w", w=C + 1)
                    chain(dve.reciprocal(rden[u][:, 4 * n:4 * n + 4], pv[:, :, C]))
                    dve.tensor_tensor(cn[u][:, 4 * n:4 * n + 4, :], pv[:, :, 0:C],
                                      rden[u][:, 4 * n:4 * n + 4].unsqueeze(2).broadcast_to([128, 4, C]), ALU.mult) \
                        .then_inc(sg_["cn_sb"], 1)
                elif what == "xproj":
                    s[u].wait(dve, "pr_ps", p, 2)
                    chain(dve.tensor_tensor(at(x, u, p), PA[u][:, 0:D], at(x, u, p), ALU.add))
                elif what == "rnorm":
                    dve.tensor_scalar(xn[u][:], *norm(s, u, p, 3)).then_inc(sg_["xn"], 1)
                elif what == "choose":
                    dve.wait_ge(r1["lg_ps"], p * 2 + u + 1)
                    chain(dve.tensor_copy(lgp[:, 0:E1], PB[u][:, 0:E1]))
                    chain(dve.max(top8[:], lgp[:, 0:E1]))
                    chain(dve.memset(top8[:, TOP1:8], -3e38))
                    dve.tensor_scalar(nmax[:], top8[:, 0:1], -1.0, None, ALU.mult).then_inc(r1["top"], 1)
                    chain(dve.match_replace(lgp2[:], top8[:], lgp[:], -2e38))
                    chain(dve.tensor_tensor(msk[:, 0:E1], lgp[:, 0:E1], lgp2[:, 0:E1], ALU.not_equal))
                    dve.wait_ge(r1["ex"], p * 2 + u + 1)
                    chain(dve.tensor_reduce(den[:], ex[:, 0:E1], AX.X, ALU.add))
                    chain(dve.reciprocal(den[:], den[:]))
                    dve.scalar_tensor_tensor(at(dw[:, :, 0:E1], u, p), ex[:, 0:E1], den[:],
                                             msk[:, 0:E1], ALU.mult, ALU.mult).then_inc(r1["done"], 1)

            two_streams(dve, B_HEAD, B_STEPS, LENGTH_B, LAG_B, step_b, chain.turn)

            dve.wait_ge(r1["done"], B)
            dve.sem_inc(f1["free"], 2)
            for c in range(KC):
                dve.wait_ge(f1["x_high"], c + 1)
                dve.tensor_tensor(xl[c][:], xT6[:, c], xh[c][:].bitcast(F32), ALU.subtract).then_inc(f1["x_low"], 1)

            def weights_low(u, e):
                dve.wait_ge(f1["w_high"], e + 1)
                dve.tensor_tensor(wl[:, u], wf[:, u], wh[:, u].bitcast(F32), ALU.subtract).then_inc(f1["w_low"], 1)

            def ffn_gated(step, th, f):
                dve.wait_ge(f1["sg"], step * 2 + f + 1)
                m = dve.tensor_tensor(af[th][:, f, :], sgf[:, f, :], bank[2 * f + 1][0:FH, :], ALU.mult)
                m.then_inc(f1["a_sb"], 1)

            def ffn_add(step, u, th, quarters):
                for q in quarters:
                    dve.wait_ge(f1["y_ps"], step * 4 + q + 1)
                    dve.scalar_tensor_tensor(x[:, 4 * th + q, :], bank[4 + q][:, 0:D], dwc[:, u, 4 * th + q:4 * th + q + 1],
                                             x[:, 4 * th + q, :], ALU.mult, ALU.add).then_inc(f1["y_sb"], 1)

            def ffn_turn(i, last=False):
                for u in range(2):
                    for th in range(2):
                        step = i * 4 + u * 2 + th
                        for f in range(2):
                            ffn_gated(step, th, f)
                            if th == 0 and f == 0 and not (last and u == 1):
                                weights_low(1 - u, i * 2 + u + 1)
                            dve.wait_ge(f1["a_sb"], step * 2 + f + 1)
                            dve.sem_inc(f1["free"], 1)
                            if not (isinstance(i, int) and step == 0):
                                ffn_add(step - 1, u if th else 1 - u, 1 - th, (2 * f, 2 * f + 1))
                        if th == 0:
                            chain(dve.tensor_copy(dwc[:, u, :], dw[:, :, bass.ds(i * 2 + u, 1)].rearrange("p b a -> p (b a)")))

            weights_low(0, 0)
            chain.turn()
            ffn_turn(0)
            with dve.Fori(1, NF // 2 - 1) as i:
                chain.turn()
                ffn_turn(i)
            chain.turn()
            ffn_turn(NF // 2 - 1, last=True)
            ffn_add(NF * 2 - 1, 1, 1, range(4))
            dve.wait_ge(f1["y_sb"], NF * 8)
            dve.sem_inc(f1["x_new"], 1)


def constants():
    import numpy as np
    q, k = np.arange(128)[:, None], np.arange(128)[None, :]
    never = np.where(k > q, -1e30, 0.0)
    slope = 2.0 ** (-8.0 / 32.0)
    e = np.arange(E0)[None, :]

    def angles(n, dim):
        inv = (1.0 / 10000.0 ** (np.arange(0, dim, 2, dtype=np.float32) / np.float32(dim))).astype(np.float32)
        return np.repeat((np.arange(n, dtype=np.float32)[:, None] * inv[None, :]).astype(np.float32), 2, axis=1)

    f1, fq, fk = angles(S, 16), angles(S, QX), angles(S, C)
    sign = np.where(np.arange(16) % 2 == 0, -1.0, 1.0)
    halves = lambda a: np.ascontiguousarray(a.T.reshape(2, HQ, S).transpose(1, 0, 2)).astype(np.float32)
    first = lambda w: np.where(np.arange(w) < w // 2, -1.0, 1.0)
    f = lambda a: np.ascontiguousarray(a).astype(np.float32)
    return {
        "tri": f(q < k), "ones": np.ones((128, 128), np.float32), "eplus1": f(np.broadcast_to(e + 1, (128, E0))),
        "tokall": (np.arange(B)[None, :] * S + np.arange(128)[:, None]).astype(np.int32),
        "cos1": f(np.cos(f1)), "sin1": f(np.sin(f1) * sign),
        "cosq": halves(np.cos(fq)), "sinq": halves(np.sin(fq) * first(QX)),
        "cosk": f(np.cos(fk)), "sink": f(np.sin(fk) * first(C)),
        "ident": np.eye(128, dtype=np.float32),
        "never": never.astype(np.float32),
        "neverT": np.ascontiguousarray(never.T).astype(np.float32),
        "alibi": (slope * np.arange(128) * np.sqrt(8.0)).astype(np.float32)[:, None],
    }


def laid_out(w):
    import numpy as np

    def by_group(a):
        return a.reshape(*a.shape[:-1], 2, 2, 4, 16).swapaxes(-3, -2).reshape(*a.shape)

    def pairs(a):
        return a.reshape(HX // 2, 2, *a.shape[1:]).transpose(0, 2, 1, 3)

    shared = lambda a: a.reshape(D, 2, I1).transpose(1, 0, 2)
    return {
        "w_gu0": np.concatenate([w["L0_ffn_gate_proj"], w["L0_ffn_up_proj"]], axis=2),
        "w_qkv1": np.concatenate([by_group(w["L1_attn_Wq"].T), w["L1_attn_Wk"].T, w["L1_attn_Wv"].T], axis=1),
        "b_qkv1": np.concatenate([by_group(w["L1_attn_bq"]), w["L1_attn_bk"], w["L1_attn_bv"]]),
        "w_o1": w["L1_attn_Wo"].T,
        "w_rt1": w["L1_ffn_gate_weight"].T,
        "wq_x": pairs(w["L1_xattn_Wq"].reshape(HX, KX, D)),
        "w_kc_q": pairs(w["L1_xattn_w_kc_q"]),
        "w_qr": pairs(w["L1_xattn_W_qr"].transpose(0, 2, 1)),
        "w_kr": pairs(w["L1_xattn_W_kr"].transpose(0, 2, 1)),
        "w_kc_kv": pairs(w["L1_xattn_w_kc_kv"]),
        "wo_x": pairs(w["L1_xattn_Wo"].T.reshape(HX, KX, D)),
        "w_gu1": np.concatenate([
            np.concatenate([w["L1_ffn_w_gate"], shared(w["L1_ffn_ws_gate"])], axis=0),
            np.concatenate([w["L1_ffn_w_up"], shared(w["L1_ffn_ws_up"])], axis=0)], axis=2),
        "w_d1": np.concatenate([w["L1_ffn_w_down"], w["L1_ffn_ws_down"].reshape(2, I1, D)], axis=0),
    }


def kernel(**inputs):
    import numpy as _np
    import concourse.bacc as _bacc
    from concourse import mybir as _mybir
    from concourse.bass_utils import run_bass_kernel_spmd as _run

    nc = _bacc.Bacc("TRN2", target_bir_lowering=False, num_devices=1)
    host = {n: inputs[n] for n in ("x", "ctx_512", "L0_attn_W_attn", "L0_attn_b_attn", "L0_attn_W_proj",
                                   "L0_attn_b_proj", "L0_ffn_router_weight", "L0_ffn_down_proj", "L1_attn_bo")}
    host.update(laid_out({k: _np.asarray(v) for k, v in inputs.items()}))
    host = {k: _np.ascontiguousarray(v) for k, v in host.items()}
    host.update(constants())
    arrays, t = {}, {}
    for name, a in host.items():
        arrays[f"in_{name}"] = a
        t[name] = nc.dram_tensor(f"in_{name}", a.shape, _mybir.dt.from_np(a.dtype), kind="ExternalInput").ap()
    out = nc.dram_tensor("out_x", (B, S, D), F32, kind="ExternalOutput").ap()
    program(nc, t, out, None)
    r = _run(nc, [arrays], core_ids=[0])
    return r.results[0]["out_x"]
```
